# Optimizing a Trainium2 kernel written in Bass

```python
import numpy as np
import jax
import jax.numpy as jnp

def _softmax(x, axis=-1):
    return jax.nn.softmax(x, axis=axis)

def _gelu(x):
    return jax.nn.gelu(x, approximate=True)

def _silu(x):
    return jax.nn.silu(x)

def _sigmoid(x):
    return jax.nn.sigmoid(x)

def _layernorm(x, axis=-1, eps=1e-05):
    m = jnp.mean(x, axis=axis, keepdims=True)
    v = jnp.var(x, axis=axis, keepdims=True)
    return (x - m) / jnp.sqrt(v + eps)

def _scatter_add(tgt, idx, src, axis=0):
    return tgt.at[idx].add(src)

def _segment_sum(src, seg, n):
    return jax.ops.segment_sum(src, seg, n)
kernel_name = 'mk_gnn_resnorm_d4_gnn_r32_b5463b'

def setup_inputs(seed: int=0):
    np.random.seed(seed)
    _w = jnp.asarray

    def _rec_inputs():
        import jax
        import jax.numpy as jnp
        _gk = jax.random.key(seed)
        x = -0.0003713 + 1 * jax.random.normal(jax.random.fold_in(_gk, 1), (3125, 128), jnp.float32)
        src = jax.random.randint(jax.random.fold_in(_gk, 2), (50000,), 0, 3125, jnp.int32)
        dst = jnp.minimum((3125 * jax.random.uniform(jax.random.fold_in(_gk, 3), (50000,)) ** 2.0).astype(jnp.int32), 99999)
        _o = jnp.argsort(dst, stable=True)
        src = src[_o]
        dst = dst[_o]
        edge_attr_128 = -8.16379e-05 + 0.999858 * jax.random.normal(jax.random.fold_in(_gk, 12), (50000, 128), jnp.float32)
        return (x, src, dst, edge_attr_128)
    x, src, dst, edge_attr_128 = _rec_inputs()

    def _L0_gnn_setup():
        import jax, jax.numpy as jnp
        import numpy as np
        N_NODES = 3125
        N_EDGES = 50000
        D_IN = 128
        D_HID = 128
        D_OUT = 128
        BN_EPS = 1e-05

        def _sage_conv(x, src, dst, W_l, W_r, b):
            msgs = x[src]
            s = jax.ops.segment_sum(msgs, dst, num_segments=N_NODES)
            deg = jax.ops.segment_sum(jnp.ones((src.shape[0], 1), x.dtype), dst, num_segments=N_NODES)
            aggr = s / jnp.maximum(deg, 1.0)
            return aggr @ W_l + x @ W_r + b
        key = jax.random.key(seed)
        ks = jax.random.split(key, 10)
        glorot = lambda k, i, o: jax.random.normal(k, (i, o), jnp.float32) * (1.0 / np.sqrt(i))
        x = jax.random.normal(ks[0], (N_NODES, D_IN), jnp.float32)
        edge_index = jax.random.randint(ks[1], (2, N_EDGES), 0, N_NODES)
        return {'x': x, 'edge_index': edge_index, 'W1_l': glorot(ks[2], D_IN, D_HID), 'W1_r': glorot(ks[3], D_IN, D_HID), 'b1': jnp.zeros((D_HID,), jnp.float32), 'bn_gamma': jnp.ones((D_HID,), jnp.float32), 'bn_beta': jnp.zeros((D_HID,), jnp.float32), 'bn_mean': jax.random.normal(ks[4], (D_HID,), jnp.float32) * 0.1, 'bn_var': jax.random.uniform(ks[5], (D_HID,), jnp.float32, 0.5, 1.5), 'W2_l': glorot(ks[6], D_HID, D_OUT), 'W2_r': glorot(ks[7], D_HID, D_OUT), 'b2': jnp.zeros((D_OUT,), jnp.float32)}
    _L0_gnn_all = _L0_gnn_setup()
    _L0_gnn_in = {k: v for k, v in _L0_gnn_all.items() if k in ('W1_l', 'W1_r', 'b1', 'bn_gamma', 'bn_beta', 'bn_mean', 'bn_var', 'W2_l', 'W2_r', 'b2')}
    del _L0_gnn_all

    def _L1_gnn_setup():
        import jax, jax.numpy as jnp
        from jax import lax
        import numpy as np
        N_NODES = 50000
        N_EDGES = 25000
        IN_CH = 128
        HEADS = 4
        OUT_CH = 32
        TOP_K = 8

        def _topk_mask_1h(e_h, row, k):
            E = e_h.shape[0]
            order = jnp.lexsort((-e_h, row))
            srow = row[order]
            seg_start = jnp.searchsorted(srow, srow, side='left')
            pos_in_seg = jnp.arange(E, dtype=seg_start.dtype) - seg_start
            keep_sorted = pos_in_seg < k
            return jnp.zeros((E,), jnp.bool_).at[order].set(keep_sorted)
        key = jax.random.key(seed)
        k1, k2, k3, k4 = jax.random.split(key, 4)
        x = jax.random.normal(k1, (N_NODES, IN_CH), jnp.float32)
        edge_index = jax.random.randint(k2, (2, N_EDGES), 0, N_NODES, dtype=jnp.int32)
        scale = float(np.sqrt(2.0 / (IN_CH + HEADS * OUT_CH)))
        W = jax.random.normal(k3, (IN_CH, HEADS * OUT_CH), jnp.float32) * scale
        att = jax.random.normal(k4, (HEADS, 2 * OUT_CH), jnp.float32) * 0.1
        return {'x': x, 'W': W, 'att': att, 'edge_index': edge_index}
    _L1_gnn_all = _L1_gnn_setup()
    _L1_gnn_in = {k: v for k, v in _L1_gnn_all.items() if k in ('W', 'att')}
    del _L1_gnn_all

    def _L2_gnn_setup():
        import jax, jax.numpy as jnp
        import numpy as np
        N, E, H, T = (50000, 25000, 128, 2)

        def _gru_cell(x, h, Wih, Whh, bih, bhh):
            gi = x @ Wih.T + bih
            gh = h @ Whh.T + bhh
            ir, iz, inn = jnp.split(gi, 3, axis=1)
            hr, hz, hn = jnp.split(gh, 3, axis=1)
            r = jax.nn.sigmoid(ir + hr)
            z = jax.nn.sigmoid(iz + hz)
            n = jnp.tanh(inn + r * hn)
            return (1.0 - z) * n + z * h
        key = jax.random.key(seed)
        ks = jax.random.split(key, 16)
        inp = {'h': jax.random.normal(ks[0], (N, H), dtype=jnp.float32), 'e': jax.random.normal(ks[1], (E, H), dtype=jnp.float32), 'src': jax.random.randint(ks[2], (E,), 0, N), 'dst': jax.random.randint(ks[3], (E,), 0, N)}
        i = 4
        for t in range(T):
            inp[f'W_msg_{t}'] = jax.random.normal(ks[i], (2 * H, 3 * H), dtype=jnp.float32) * 0.05
            i += 1
            inp[f'b_msg_{t}'] = jnp.zeros((2 * H,), jnp.float32)
            inp[f'Wih_{t}'] = jax.random.normal(ks[i], (3 * H, 2 * H), dtype=jnp.float32) * 0.05
            i += 1
            inp[f'Whh_{t}'] = jax.random.normal(ks[i], (3 * H, H), dtype=jnp.float32) * 0.05
            i += 1
            inp[f'bih_{t}'] = jnp.zeros((3 * H,), jnp.float32)
            inp[f'bhh_{t}'] = jnp.zeros((3 * H,), jnp.float32)
        return inp
    _L2_gnn_all = _L2_gnn_setup()
    _L2_gnn_in = {k: v for k, v in _L2_gnn_all.items() if k in ('W_msg_0', 'b_msg_0', 'Wih_0', 'Whh_0', 'bih_0', 'bhh_0', 'W_msg_1', 'b_msg_1', 'Wih_1', 'Whh_1', 'bih_1', 'bhh_1')}
    del _L2_gnn_all

    def _L3_gnn_setup():
        import jax, jax.numpy as jnp
        import numpy as np
        N_NODES = 50000
        N_EDGES = 18750
        D_IN = 128
        D_OUT = 128

        def _aggregate(h, src, dst, n_nodes):
            return jax.ops.segment_sum(h[src], dst, num_segments=n_nodes)
        key = jax.random.key(seed)
        k1, k2, k3, k4, k5 = jax.random.split(key, 5)
        feature = jax.random.normal(k1, (N_NODES, D_IN), dtype=jnp.float32)
        W = jax.random.normal(k2, (D_IN, D_OUT), dtype=jnp.float32) * (1.0 / np.sqrt(D_IN))
        b = jax.random.normal(k3, (D_OUT,), dtype=jnp.float32) * 0.01
        src = jax.random.randint(k4, (N_EDGES,), 0, N_NODES, dtype=jnp.int32)
        dst = jax.random.randint(k5, (N_EDGES,), 0, N_NODES, dtype=jnp.int32)
        return {'feature': feature, 'W': W, 'b': b, 'src': src, 'dst': dst}
    _L3_gnn_all = _L3_gnn_setup()
    _L3_gnn_in = {k: v for k, v in _L3_gnn_all.items() if k in ('W', 'b')}
    del _L3_gnn_all
    return {'x': x, 'src': src, 'dst': dst, 'edge_attr_128': edge_attr_128, 'L0_gnn_W1_l': _L0_gnn_in['W1_l'], 'L0_gnn_W1_r': _L0_gnn_in['W1_r'], 'L0_gnn_b1': _L0_gnn_in['b1'], 'L0_gnn_bn_gamma': _L0_gnn_in['bn_gamma'], 'L0_gnn_bn_beta': _L0_gnn_in['bn_beta'], 'L0_gnn_bn_mean': _L0_gnn_in['bn_mean'], 'L0_gnn_bn_var': _L0_gnn_in['bn_var'], 'L0_gnn_W2_l': _L0_gnn_in['W2_l'], 'L0_gnn_W2_r': _L0_gnn_in['W2_r'], 'L0_gnn_b2': _L0_gnn_in['b2'], 'L1_gnn_W': _L1_gnn_in['W'], 'L1_gnn_att': _L1_gnn_in['att'], 'L2_gnn_W_msg_0': _L2_gnn_in['W_msg_0'], 'L2_gnn_b_msg_0': _L2_gnn_in['b_msg_0'], 'L2_gnn_Wih_0': _L2_gnn_in['Wih_0'], 'L2_gnn_Whh_0': _L2_gnn_in['Whh_0'], 'L2_gnn_bih_0': _L2_gnn_in['bih_0'], 'L2_gnn_bhh_0': _L2_gnn_in['bhh_0'], 'L2_gnn_W_msg_1': _L2_gnn_in['W_msg_1'], 'L2_gnn_b_msg_1': _L2_gnn_in['b_msg_1'], 'L2_gnn_Wih_1': _L2_gnn_in['Wih_1'], 'L2_gnn_Whh_1': _L2_gnn_in['Whh_1'], 'L2_gnn_bih_1': _L2_gnn_in['bih_1'], 'L2_gnn_bhh_1': _L2_gnn_in['bhh_1'], 'L3_gnn_W': _L3_gnn_in['W'], 'L3_gnn_b': _L3_gnn_in['b']}

def reference(x, src, dst, edge_attr_128, L0_gnn_W1_l, L0_gnn_W1_r, L0_gnn_b1, L0_gnn_bn_gamma, L0_gnn_bn_beta, L0_gnn_bn_mean, L0_gnn_bn_var, L0_gnn_W2_l, L0_gnn_W2_r, L0_gnn_b2, L1_gnn_W, L1_gnn_att, L2_gnn_W_msg_0, L2_gnn_b_msg_0, L2_gnn_Wih_0, L2_gnn_Whh_0, L2_gnn_bih_0, L2_gnn_bhh_0, L2_gnn_W_msg_1, L2_gnn_b_msg_1, L2_gnn_Wih_1, L2_gnn_Whh_1, L2_gnn_bih_1, L2_gnn_bhh_1, L3_gnn_W, L3_gnn_b):
    import jax
    import jax.numpy as jnp

    def _L0_gnn_ref(x, edge_index, W1_l, W1_r, b1, bn_gamma, bn_beta, bn_mean, bn_var, W2_l, W2_r, b2):
        import jax, jax.numpy as jnp
        import numpy as np
        N_NODES = 3125
        N_EDGES = 50000
        D_IN = 128
        D_HID = 128
        D_OUT = 128
        BN_EPS = 1e-05

        def _sage_conv(x, src, dst, W_l, W_r, b):
            msgs = x[src]
            s = jax.ops.segment_sum(msgs, dst, num_segments=N_NODES)
            deg = jax.ops.segment_sum(jnp.ones((src.shape[0], 1), x.dtype), dst, num_segments=N_NODES)
            aggr = s / jnp.maximum(deg, 1.0)
            return aggr @ W_l + x @ W_r + b
        src, dst = (edge_index[0], edge_index[1])
        h = _sage_conv(x, src, dst, W1_l, W1_r, b1)
        h = (h - bn_mean) * (bn_gamma / jnp.sqrt(bn_var + BN_EPS)) + bn_beta
        h = jax.nn.relu(h)
        out = _sage_conv(h, src, dst, W2_l, W2_r, b2)
        return out

    def _L1_gnn_ref(x, W, att, edge_index):
        import jax, jax.numpy as jnp
        from jax import lax
        import numpy as np
        N_NODES = 50000
        N_EDGES = 25000
        IN_CH = 128
        HEADS = 4
        OUT_CH = 32
        TOP_K = 8

        def _topk_mask_1h(e_h, row, k):
            E = e_h.shape[0]
            order = jnp.lexsort((-e_h, row))
            srow = row[order]
            seg_start = jnp.searchsorted(srow, srow, side='left')
            pos_in_seg = jnp.arange(E, dtype=seg_start.dtype) - seg_start
            keep_sorted = pos_in_seg < k
            return jnp.zeros((E,), jnp.bool_).at[order].set(keep_sorted)
        N = x.shape[0]
        H, C = (HEADS, OUT_CH)
        h = (x @ W).reshape(N, H, C)
        loops = jnp.arange(N, dtype=edge_index.dtype)
        ei = jnp.concatenate([edge_index, jnp.stack([loops, loops])], axis=1)
        row, col = (ei[0], ei[1])
        x_i = h[row]
        x_j = h[col]
        a_i, a_j = (att[:, :C], att[:, C:])
        e = jnp.einsum('ehc,hc->eh', x_i, a_i) + jnp.einsum('ehc,hc->eh', x_j, a_j)
        e = jax.nn.leaky_relu(e, negative_slope=0.2)
        mask = jax.vmap(lambda eh: _topk_mask_1h(eh, row, TOP_K), in_axes=1, out_axes=1)(e)
        e = jnp.where(mask, e, -jnp.inf)
        seg_max = jax.ops.segment_max(e, row, num_segments=N)
        ez = jnp.exp(e - lax.stop_gradient(seg_max)[row])
        denom = jax.ops.segment_sum(ez, row, num_segments=N)
        alpha = ez / denom[row]
        out = jax.ops.segment_sum(alpha[:, :, None] * x_j, row, num_segments=N)
        out = out.reshape(N, H * C)
        return jax.nn.elu(out)

    def _L2_gnn_ref(h, e, src, dst, W_msg_0, b_msg_0, Wih_0, Whh_0, bih_0, bhh_0, W_msg_1, b_msg_1, Wih_1, Whh_1, bih_1, bhh_1):
        import jax, jax.numpy as jnp
        import numpy as np
        N, E, H, T = (50000, 25000, 128, 2)

        def _gru_cell(x, h, Wih, Whh, bih, bhh):
            gi = x @ Wih.T + bih
            gh = h @ Whh.T + bhh
            ir, iz, inn = jnp.split(gi, 3, axis=1)
            hr, hz, hn = jnp.split(gh, 3, axis=1)
            r = jax.nn.sigmoid(ir + hr)
            z = jax.nn.sigmoid(iz + hz)
            n = jnp.tanh(inn + r * hn)
            return (1.0 - z) * n + z * h
        params = [(W_msg_0, b_msg_0, Wih_0, Whh_0, bih_0, bhh_0), (W_msg_1, b_msg_1, Wih_1, Whh_1, bih_1, bhh_1)]
        n_nodes = h.shape[0]
        deg = jax.ops.segment_sum(jnp.ones((dst.shape[0],), h.dtype), dst, num_segments=n_nodes)
        denom = jnp.maximum(deg, 1.0)[:, None]
        for Wm, bm, Wih, Whh, bih, bhh in params:
            msg_in = jnp.concatenate([h[dst], h[src], e], axis=1)
            act_e = msg_in @ Wm.T + bm
            a = jax.ops.segment_sum(act_e, dst, num_segments=n_nodes) / denom
            h = _gru_cell(a, h, Wih, Whh, bih, bhh)
        return h

    def _L3_gnn_ref(feature, W, b, src, dst):
        import jax, jax.numpy as jnp
        import numpy as np
        N_NODES = 50000
        N_EDGES = 18750
        D_IN = 128
        D_OUT = 128

        def _aggregate(h, src, dst, n_nodes):
            return jax.ops.segment_sum(h[src], dst, num_segments=n_nodes)
        n = feature.shape[0]
        h = _aggregate(feature, src, dst, n)
        h = _aggregate(h, src, dst, n)
        return h @ W + b
    edge_index = jnp.stack([src, dst])
    x = _layernorm(x + _L0_gnn_ref(x, edge_index, L0_gnn_W1_l, L0_gnn_W1_r, L0_gnn_b1, L0_gnn_bn_gamma, L0_gnn_bn_beta, L0_gnn_bn_mean, L0_gnn_bn_var, L0_gnn_W2_l, L0_gnn_W2_r, L0_gnn_b2), axis=-1)
    x = _layernorm(x + _L1_gnn_ref(x, L1_gnn_W, L1_gnn_att, edge_index), axis=-1)
    x = _layernorm(x + _L2_gnn_ref(x, edge_attr_128, src, dst, L2_gnn_W_msg_0, L2_gnn_b_msg_0, L2_gnn_Wih_0, L2_gnn_Whh_0, L2_gnn_bih_0, L2_gnn_bhh_0, L2_gnn_W_msg_1, L2_gnn_b_msg_1, L2_gnn_Wih_1, L2_gnn_Whh_1, L2_gnn_bih_1, L2_gnn_bhh_1), axis=-1)
    x = _layernorm(x + _L3_gnn_ref(x, L3_gnn_W, L3_gnn_b, src, dst), axis=-1)
    return x

_drawn_inputs = setup_inputs


def setup_inputs(seed=0):
    import zlib

    import numpy as np

    out = dict(_drawn_inputs(seed))
    spreads = {'L0_gnn_b1': (0.0, 0.1),
     'L0_gnn_bn_gamma': (1.0, 0.2),
     'L0_gnn_bn_beta': (0.0, 0.1),
     'L0_gnn_b2': (0.0, 0.1),
     'L2_gnn_b_msg_0': (0.0, 0.35),
     'L2_gnn_bih_0': (0.0, 0.338),
     'L2_gnn_bhh_0': (0.0, 0.421),
     'L2_gnn_b_msg_1': (0.0, 0.1),
     'L2_gnn_bih_1': (0.0, 0.1),
     'L2_gnn_bhh_1': (0.0, 0.272)}
    factors = {'edge_attr_128': 6.812, 'L3_gnn_b': 200.0}
    for name, (base, spread) in spreads.items():
        noise = np.random.default_rng([zlib.crc32(name.encode()), seed]).standard_normal(out[name].shape)
        drawn = base * np.exp(spread * noise) if base else spread * noise
        out[name] = jnp.asarray(drawn.astype(out[name].dtype))
    for name, factor in factors.items():
        out[name] = (out[name] * factor).astype(out[name].dtype)
    return out
```

```python
from contextlib import ExitStack

import concourse.bass as bass
from concourse import mybir

F32 = mybir.dt.float32
BF16 = mybir.dt.bfloat16
I32 = mybir.dt.int32
I16 = mybir.dt.int16
U32 = mybir.dt.uint32
ALU = mybir.AluOpType
ACT = mybir.ActivationFunctionType
AX = mybir.AxisListType

P = 128
N = 3125
E = 50000
D = 128
WIN = 32
NWIN = -(-N // WIN)
NPAD = NWIN * WIN
KB = -(-N // P)
ROWS = KB * P
GT = 2
GE = GT * P
NG = -(-E // GE)
NQ = NG // 2
NT = NG * GT
TAIL = E - (NG - 1) * GE
SHIFT = GE - TAIL
PADW = 4095
NC = 7
CH = NPAD // NC
SUB = 4
SN = CH // SUB
HEADS = 4
HC = D // HEADS
TOPK = 8
AHEAD = NG
SRING = 8


class Mem:

    def __init__(self, nc, ctx, phase):
        self.nc, self.ctx, self.phase, self.sems = nc, ctx, phase, []
        ctx.callback(self.clear)

    def clear(self):
        if self.sems:
            self.nc.clear_and_free_semaphores(self.sems)
            self.nc.all_engine_barrier()

    def sb(self, name, shape, dt=F32):
        return self.ctx.enter_context(self.nc.sbuf_tensor(f"{self.phase}_{name}", shape, dt))

    def ps(self, name, shape, dt=F32):
        return self.ctx.enter_context(self.nc.psum_tensor(f"{self.phase}_{name}", shape, dt))

    def sem(self, name):
        self.sems.append(self.nc.alloc_semaphore(f"{self.phase}_{name}"))
        return self.sems[-1]


def phase_index(nc, d, src, dst):
    with ExitStack() as ctx:
        m = Mem(nc, ctx, "ix")
        ids = m.sb("ids", [NQ, 2, 512], I32)
        part = m.sb("part", [NQ, 4, 512], I32)
        partf = m.sb("partf", [NQ, 4, 512])
        local = m.sb("local", [NQ, 512], I32)
        gm = m.sb("gm", [NQ, 4])
        spread = m.sb("spread", [NQ, 4, NQ])
        first = m.sb("first", [NQ, NQ, 2])
        last = m.sb("last", [NQ, NQ, 2])
        wcol = m.sb("wcol", [NQ, 1])
        ones = m.sb("ones", [NQ, NQ])
        a = m.sb("a", [NQ, NQ, 2])
        b = m.sb("b", [NQ, NQ, 2])
        c = m.sb("c", [NQ, NQ, 2])
        tab = m.sb("tab", [NQ, 8])
        tabi = m.sb("tabi", [NQ, 1], I32)
        cols_ps = m.ps("cols_ps", [P, 4, 512])
        row_ps = m.ps("row_ps", [NQ, 4, NQ])
        padded, loaded, consts, v, floats, bounds, tp, row, done, stored = (m.sem(n) for n in (
            "padded", "loaded", "consts", "v", "floats", "bounds", "tp", "row", "done", "stored"))
        block = ctx.enter_context(nc.Block())
        full = NQ - 1

        @block.sync
        def _(sp):
            sp.wait_ge(padded, 2)
            for n, ap in ((0, src), (1, dst)):
                sp.dma_start(ids[0:full, n, :], ap[0:full * 512].rearrange("(q e) -> q e", e=512)).then_inc(loaded, 16)
                sp.dma_start(ids[full:NQ, n, 0:GE], ap[full * 512:full * 512 + GE].rearrange("(q e) -> q e", q=1)).then_inc(loaded, 16)
                sp.dma_start(ids[full:NQ, n, GE + SHIFT:512], ap[E - TAIL:E].rearrange("(q e) -> q e", q=1)).then_inc(loaded, 16)
            sp.wait_ge(done, 1)
            sp.dma_start(d["wins"].rearrange("a w -> w a"), tabi[:]).then_inc(stored, 16)
            sp.wait_ge(stored, 16)

        @block.gpsimd
        def _(pool):
            nc.gpsimd.memset(ids[:, 0, :], 0).then_inc(padded, 1)
            nc.gpsimd.memset(ids[:, 1, :], PADW).then_inc(padded, 1)
            nc.gpsimd.iota(first[:], [[-2, NQ], [-1, 2]], base=NG, channel_multiplier=0,
                           allow_small_or_imprecise_dtypes=True).then_inc(consts, 1)
            nc.gpsimd.iota(last[:], [[2, NQ], [1, 2]], base=1, channel_multiplier=0,
                           allow_small_or_imprecise_dtypes=True).then_inc(consts, 1)
            nc.gpsimd.iota(wcol[:], [[0, 1]], base=0, channel_multiplier=1,
                           allow_small_or_imprecise_dtypes=True).then_inc(consts, 1)
            nc.gpsimd.memset(ones[:], 1.0).then_inc(consts, 1)

        @block.vector
        def _(dve):
            steps = [0]

            def step(ins):
                steps[0] += 1
                ins.then_inc(v, 1)
                dve.wait_ge(v, steps[0])

            dve.wait_ge(loaded, 96)
            nc.vector.tensor_scalar(part[:, 1, :], ids[:, 1, :], 5, None, ALU.logical_shift_right)
            nc.vector.tensor_scalar(local[:], ids[:, 1, :], WIN - 1, None, ALU.bitwise_and)
            nc.vector.tensor_scalar(part[:, 2, :], ids[:, 0, :], P - 1, None, ALU.bitwise_and)
            nc.vector.tensor_copy(part[:, 0, :], ids[:, 1, :])
            step(nc.vector.tensor_scalar(part[:, 3, :], ids[:, 0, :], 7, 5, ALU.logical_shift_right,
                                         ALU.logical_shift_left))
            step(nc.vector.tensor_tensor(part[:, 3, :], part[:, 3, :], local[:], ALU.bitwise_or))
            step(nc.vector.tensor_copy(partf[:], part[:]))
            nc.vector.nop().then_inc(floats, 1)
            w = partf[:, 1, :].rearrange("q (g e) -> q g e", g=2)
            nc.vector.tensor_reduce(gm[:, 0:2], w, AX.X, ALU.min)
            step(nc.vector.tensor_reduce(gm[:, 2:4], w, AX.X, ALU.max))
            for n in range(4):
                ins = nc.vector.tensor_scalar(spread[:, n, :], d["ident"][0:NQ, 0:NQ], gm[:, n:n + 1], None, ALU.mult)
            step(ins)
            nc.vector.nop().then_inc(bounds, 1)
            dve.wait_ge(tp, 1)
            for n, to in enumerate((None, d["windows"], d["lows"], d["codes"])):
                for j in range(4):
                    if n == 0:
                        out = d["dsts"][:].rearrange("p (q h) i -> p q h i", h=2)[:, :, j // 2, j % 2]
                    else:
                        out = to[j % 2][:].rearrange("p (q h) -> p q h", h=2)[:, :, j // 2]
                    nc.vector.tensor_copy(out, cols_ps[:, n, j * NQ:(j + 1) * NQ])
            dve.wait_ge(row, 1)
            dve.wait_ge(consts, 4)
            least = row_ps[:, 0:2, :].rearrange("w j q -> w q j")
            most = row_ps[:, 2:4, :].rearrange("w j q -> w q j")
            nc.vector.tensor_scalar(a[:], least, wcol[:, 0:1], None, ALU.is_le)
            step(nc.vector.tensor_scalar(b[:], most, wcol[:, 0:1], None, ALU.is_ge))
            step(nc.vector.tensor_tensor(c[:], a[:], b[:], ALU.mult))
            nc.vector.tensor_tensor(a[:], c[:], first[:], ALU.mult)
            step(nc.vector.tensor_tensor(b[:], c[:], last[:], ALU.mult))
            nc.vector.tensor_reduce(tab[:, 4:5], a[:], AX.XY, ALU.max)
            step(nc.vector.tensor_reduce(tab[:, 5:6], b[:], AX.XY, ALU.max))
            step(nc.vector.tensor_scalar(tab[:, 6:7], tab[:, 4:5], -1.0, float(NG), ALU.mult, ALU.add))
            step(nc.vector.tensor_scalar(tab[:, 0:1], tab[:, 6:7], float(NG - 1), None, ALU.min))
            step(nc.vector.tensor_scalar(tab[:, 6:7], tab[:, 0:1], 1.0, None, ALU.add))
            step(nc.vector.tensor_tensor(tab[:, 1:2], tab[:, 6:7], tab[:, 5:6], ALU.max))
            step(nc.vector.scalar_tensor_tensor(out=tab[:, 3:4], in0=tab[:, 1:2], scalar=256.0, in1=tab[:, 0:1],
                                                op0=ALU.mult, op1=ALU.add))
            step(nc.vector.tensor_copy(tabi[:], tab[:, 3:4]))
            nc.vector.nop().then_inc(done, 1)

        @block.tensor
        def _(pe):
            pe.wait_ge(floats, 1)
            for n in range(4):
                for j in range(4):
                    ins = nc.tensor.transpose(cols_ps[:, n, j * NQ:(j + 1) * NQ],
                                              partf[:, n, j * P:(j + 1) * P], d["ident"][0:NQ, 0:NQ])
            ins.then_inc(tp, 1)
            pe.wait_ge(bounds, 1)
            pe.wait_ge(consts, 4)
            nc.tensor.matmul(row_ps[:], ones[:], spread[:], start=True, stop=True).then_inc(row, 1)


def bounded(nc, value, most):
    return nc.s_assert_within(value, min_val=0, max_val=most,
                              skip_runtime_bounds_check_because="it follows from the clamped table of windows")


BATCH = 7
HALVES = 2


class Held:

    def __init__(self, nc, eng, name, most, value=0):
        self.nc, self.eng, self.most = nc, eng, most
        self.reg = eng.alloc_register(f"{name}_{eng.engine.name}")
        self.set(value)

    def set(self, value):
        self.eng.reg_mov(self.reg, value)

    def add(self, value):
        self.eng.reg_add(self.reg, self.reg, value)

    def least(self, value, other):
        self.eng.reg_alu(self.reg, value, other, ALU.min)

    @property
    def value(self):
        return bounded(self.nc, self.eng.snap(self.reg), self.most)


def windows(nc, eng, wins, body):
    lo, end = Held(nc, eng, "lo", NG - 1), Held(nc, eng, "end", NG)
    with eng.Fori(0, NWIN, BATCH * HALVES) as w0:
        for half in range(HALVES):
            first = bounded(nc, eng.snap(w0 + half * BATCH), NWIN - BATCH)
            _, entries = nc.values_load_multi_w_load_instructions(
                wins[:, bass.ds(first, BATCH)], engines=[eng.engine], min_val=0, max_val=256 * NG + NG,
                skip_runtime_bounds_check_because="phase_index clamps the table to the groups there are")
            for i, entry in enumerate(entries):
                lo.set(entry & 255)
                end.set(entry >> 8)
                body(bounded(nc, eng.snap(first + i), NWIN - 1), (half * BATCH + i) % 2, lo.value, end.value)


def phase_build(nc, d, edge_attr):
    with ExitStack() as ctx:
        m = Mem(nc, ctx, "bd")
        codes = m.sb("codes", [P, KB * WIN], I16)
        nodes = m.sb("nodes", [P, NPAD])
        low = m.sb("low", [P, P], I16)
        wins = m.sb("wins", [P, NWIN])
        zero = m.sb("zero", [P, P], BF16)
        zeroc = m.sb("zeroc", [P, 512], BF16)
        inside = [m.sb(f"inside{j}", [P, NG]) for j in range(GT)]
        hot_lo = m.sb("hot_lo", [P, GT, P], BF16)
        hot_hd = m.sb("hot_hd", [P, GT, KB * WIN], BF16)
        hot_d = m.sb("hot_d", [P, GT, WIN])
        ring = m.sb("ring", [P, SRING, GT, D])
        seg = m.sb("seg", [WIN, 2, D])
        cnt_ps = [m.ps(f"cnt_ps{i}", [P, 2, 512]) for i in range(2)]
        seg_ps = [m.ps(f"seg_ps{i}", [WIN, 512]) for i in range(2)]
        consts, dots, attrs, past, past_dve, summed, closed, emptied, ins_ = (
            m.sem(n) for n in ("consts", "dots", "attrs", "past", "past_dve", "summed", "closed", "emptied", "inside"))
        hots, counted, stored = ([m.sem(f"{n}{j}") for j in range(2)] for n in ("hots", "counted", "stored"))
        arrived = [m.sem(f"arrived{i}") for i in range(2)]
        lows, highs, dsts, its = (d[n] for n in ("lows", "codes", "dsts", "windows"))
        MOST = NWIN * NG + 1
        block = ctx.enter_context(nc.Block())

        @block.gpsimd
        def _(pool):
            nc.gpsimd.iota(codes[:], [[1, KB * WIN]], base=0, channel_multiplier=0).then_inc(consts, 1)
            nc.gpsimd.iota(low[:], [[1, P]], base=0, channel_multiplier=0).then_inc(consts, 1)
            nc.gpsimd.iota(wins[:], [[1, NWIN]], base=0, channel_multiplier=0,
                           allow_small_or_imprecise_dtypes=True).then_inc(consts, 1)
            nc.gpsimd.iota(nodes[:], [[1, NPAD]], base=0, channel_multiplier=0,
                           allow_small_or_imprecise_dtypes=True).then_inc(consts, 1)
            nc.gpsimd.memset(zero[:], 0.0).then_inc(consts, 1)
            nc.gpsimd.memset(zeroc[:], 0.0).then_inc(consts, 1)

        @block.sync
        def _(sp):
            n, start, due = Held(nc, sp, "n", MOST, 1), Held(nc, sp, "start", E - GE), Held(nc, sp, "due", 8 * MOST, 8)
            sp.sem_inc(arrived[1], 8)
            sp.sem_inc(arrived[0], 16)

            def body(w, u, lo, end):
                with sp.Fori(lo, end) as g:
                    start.least(g * GE, E - GE)
                    now = n.value
                    slot = bounded(nc, sp.snap(now % SRING), SRING - 1)
                    odd = bounded(nc, sp.snap(now % 2), 1)
                    to = ring[:, bass.ds(slot, 1), :, :].rearrange("p a j f -> p (a j) f")
                    edges = edge_attr[bass.ds(start.value, GE), :].rearrange("(j p) f -> p j f", p=P)
                    arrival = due.value
                    sp.wait_ge(summed, now)
                    waited(sp, past)
                    with sp.If(odd == 1):
                        sp.wait_ge(arrived[1], arrival)
                        waited(sp, attrs)
                        sp.dma_start(to, edges).then_inc(arrived[1], 16)
                    with sp.Else():
                        sp.wait_ge(arrived[0], arrival)
                        waited(sp, attrs)
                        sp.dma_start(to, edges).then_inc(arrived[0], 16)
                    n.add(1)
                    due.add(8)

            windows(nc, sp, d["wins"], body)
            sp.wait_ge(arrived[1], (n.value >> 1) * 16 + 8)
            sp.wait_ge(arrived[0], ((n.value + 1) >> 1) * 16)
            sp.sem_inc(attrs, 2)

        @block.vector
        def _(dve):
            dve.wait_ge(consts, 4)
            n = Held(nc, dve, "n", MOST, 1)

            def body(w, u, lo, end):
                dve.wait_ge(hots[1], n.value)
                for j in range(GT):
                    nc.vector.tensor_scalar(inside[j][:], its[j][:], wins[:, bass.ds(w, 1)], None, ALU.is_equal).then_inc(ins_, 1)
                dve.wait_ge(ins_, GT * (w + 1))
                waited(dve, past_dve)
                with dve.Fori(lo, end) as g:
                    at, now = bass.ds(g, 1), n.value
                    for j in range(GT):
                        dve.wait_ge(counted[j], now)
                        nc.vector.tensor_scalar(hot_lo[:, j, :], low[:], lows[j][:, at], None, ALU.is_equal)
                        nc.vector.tensor_scalar(hot_hd[:, j, :], codes[:], highs[j][:, at],
                                                inside[j][:, at], ALU.is_equal, ALU.mult).then_inc(hots[j], 1)
                    dve.wait_ge(summed, now + SRING - 1)
                    nc.vector.tensor_tensor(hot_d[:], nodes[:, bass.ds(w * WIN, WIN)].unsqueeze(1).to_broadcast([P, GT, WIN]),
                                            dsts[:, at, :].rearrange("p a j -> p (a j)").unsqueeze(2).to_broadcast([P, GT, WIN]),
                                            ALU.is_equal).then_inc(dots, 1)
                    n.add(1)

            windows(nc, dve, d["wins"], body)

        @block.tensor
        def _(pe):
            for j in range(GT):
                pe.sem_inc(counted[j], 1)
            pe.sem_inc(hots[1], 1)
            pe.sem_inc(summed, SRING)
            pe.sem_inc(emptied, 2)
            pe.wait_ge(consts, 6)
            n = Held(nc, pe, "n", MOST, 1)

            def body(w, u, lo, end):
                pe.wait_ge(emptied, w + 1)
                nc.tensor.matmul(cnt_ps[u][:, 0, :], zero[:], zeroc[:], start=True, stop=False, skip_group_check=True)
                nc.tensor.matmul(cnt_ps[u][:, 1, 0:KB * WIN - 512], zero[:], zeroc[:, 0:KB * WIN - 512], start=True, stop=False, skip_group_check=True)
                nc.tensor.matmul(seg_ps[u][:, 0:D], zero[:, 0:WIN], zeroc[:, 0:D], start=True, stop=False, skip_group_check=True)
                with pe.Fori(lo, end):
                    now = n.value
                    slot = bounded(nc, pe.snap(now % SRING), SRING - 1)
                    for j in range(GT):
                        pe.wait_ge(hots[j], now + j)
                        nc.tensor.matmul(cnt_ps[u][:, 0, :], hot_lo[:, j, :], hot_hd[:, j, 0:512], start=False, stop=False, skip_group_check=True)
                        nc.tensor.matmul(cnt_ps[u][:, 1, 0:KB * WIN - 512], hot_lo[:, j, :], hot_hd[:, j, 512:], start=False, stop=False, skip_group_check=True).then_inc(counted[j], 1)
                    pe.wait_ge(dots, now)
                    pe.wait_ge(attrs, now + 2)
                    for j in range(GT):
                        attr = ring[:, bass.ds(slot, 1), j, :].rearrange("p a f -> p (a f)")
                        ins = nc.tensor.matmul(seg_ps[u][:, 0:D], hot_d[:, j, :], attr, start=False, stop=True, skip_group_check=True)
                    ins.then_inc(summed, 1)
                    n.add(1)
                nc.tensor.matmul(seg_ps[u][:, 0:D], zero[:, 0:WIN], zeroc[:, 0:D], start=False, stop=True, skip_group_check=True).then_inc(closed, 1)

            windows(nc, pe, d["wins"], body)

        @block.scalar
        def _(act):
            def body(w, u):
                act.wait_ge(closed, w + 1)
                act.wait_ge(stored[u], 16 * (w >> 1))
                nc.scalar.copy(d["AT"][:, :, bass.ds(w * WIN, WIN)],
                               cnt_ps[u][:, :, :].rearrange("p a c -> p (a c)")[:, 0:KB * WIN].rearrange("p (h e) -> p h e", e=WIN))
                nc.scalar.copy(seg[:, u, :], seg_ps[u][:, 0:D]).then_inc(emptied, 1)
                act.wait_ge(emptied, w + 3)
                act.dma_start(d["se"][bass.ds(w * WIN, WIN), :], seg[:, u, :]).then_inc(stored[u], 16)

            with act.Fori(0, NWIN, 2) as w0:
                for u in range(2):
                    body(bounded(nc, act.snap(w0 + u), NWIN - 1), u)
            for u in range(2):
                act.wait_ge(stored[u], 16 * NWIN // 2)


class Repeats:

    PARTS = 4
    WIDE = NPAD // PARTS
    STEPS = 10

    def __init__(self, nc, d, mem):
        self.nc, self.d = nc, d
        self.dest = mem.sb("dest", [P, NPAD], I16)
        self.key = mem.sb("key", [P, 2, self.WIDE])
        self.best = mem.sb("best", [P, self.PARTS, TOPK])
        self.eight = mem.sb("eight", [P, TOPK])

    def block(self, dve, sem, past, i, number):
        V, W = self.nc.vector, self.WIDE

        def after(k):
            dve.wait_ge(sem, self.STEPS * number + k)

        def keys(part):
            V.scalar_tensor_tensor(out=self.key[:, part % 2, :],
                                   in0=self.d["AT"][:, bass.ds(i, 1), part * W:(part + 1) * W].rearrange("p a n -> p (a n)"),
                                   scalar=4096.0, in1=self.dest[:, part * W:(part + 1) * W],
                                   op0=ALU.mult, op1=ALU.subtract).then_inc(sem, 1)

        def greatest(part):
            waited(dve, past)
            V.max(self.best[:, part, :], self.key[:, part % 2, :]).then_inc(sem, 1)

        after(0)
        keys(0)
        keys(1)
        after(1)
        greatest(0)
        after(3)
        keys(2)
        after(4)
        greatest(1)
        after(5)
        keys(3)
        after(6)
        greatest(2)
        greatest(3)
        after(8)
        waited(dve, past)
        V.max(self.eight[:], self.best[:].rearrange("p a e -> p (a e)")).then_inc(sem, 1)
        after(9)
        V.tensor_copy(self.d["again"][:, bass.ds(i, 1), :].rearrange("p a e -> p (a e)"), self.eight[:]).then_inc(sem, 1)

    def finish(self, dve, sem, number):
        V = self.nc.vector
        done = self.STEPS * number
        a, b = (self.key[:, k, 0:KB * TOPK].bitcast(I32) for k in range(2))
        again, more = (self.d[n][:].rearrange("p k e -> p (k e)") for n in ("again", "more"))
        dve.wait_ge(sem, done)
        V.tensor_scalar(a, again, -1.0, 0.0, ALU.add, ALU.max).then_inc(sem, 1)
        dve.wait_ge(sem, done + 1)
        V.tensor_scalar(b, a, 4095, None, ALU.bitwise_and).then_inc(sem, 1)
        V.tensor_scalar(a, a, 12, None, ALU.logical_shift_right).then_inc(sem, 1)
        dve.wait_ge(sem, done + 3)
        V.tensor_copy(more, a)
        V.tensor_scalar(again, b, -1.0, 4095.0, ALU.mult, ALU.add)


def phase_start(nc, d, x, repeats):
    PB = 5
    NP = KB // PB
    with ExitStack() as ctx:
        m = Mem(nc, ctx, "st")
        xb = m.sb("xb", [P, 2, PB * D])
        rest = m.sb("rest", [P, PB * D])
        xtb = m.sb("xtb", [P, PB * P])
        ones = m.sb("ones", [P, P], BF16)
        zrows = m.sb("zrows", [ROWS - NPAD, 3 * D], BF16)
        zrowf = m.sb("zrowf", [ROWS - NPAD, D])
        least1 = m.sb("least1", [P, CH])
        inv = m.sb("inv", [P, CH])
        ind = m.sb("ind", [P, CH])
        mean_e = m.sb("mean_e", [P, CH])
        sum_e = m.sb("sum_e", [SN, SUB, D])
        tp_ps = m.ps("tp_ps", [P, PB, P])
        deg_ps = m.ps("deg_ps", [P, 512])
        se_ps = m.ps("se_ps", [P, 512])
        consts, zeroed, x_in, hi, r, mid, lo, tp, xt, xt_out, deg, inv_r, ind_r, me_r, i_out, n_out, e_out, z_out, m1, s_in, se_t, past, dest_r = (
            m.sem(n) for n in ("consts", "zeroed", "x_in", "hi", "r", "mid", "lo", "tp", "xt", "xt_out", "deg",
                               "inv_r", "ind_r", "me_r", "i_out", "n_out", "e_out", "z_out", "m1", "s_in", "se_t", "past", "dest_r"))
        parts = d["parts"]
        x_in = [x_in, m.sem("x_in1")]

        def piece_in(i):
            return x_in[i % 2], 16 * (i // 2 + 1) + 16 * (i == NP - 1)

        block = ctx.enter_context(nc.Block())

        @block.gpsimd
        def _(pool):
            nc.gpsimd.iota(repeats.dest[:], [[1, NPAD]], base=0, channel_multiplier=0).then_inc(dest_r, 1)
            nc.gpsimd.memset(ones[:], 1.0).then_inc(consts, 1)
            nc.gpsimd.memset(zrows[:], 0.0).then_inc(consts, 1)
            nc.gpsimd.memset(zrowf[:], 0.0).then_inc(consts, 1)
            nc.gpsimd.memset(xb[:, 0, :], 0.0).then_inc(zeroed, 1)

        @block.sync
        def _(sp):
            for i in range(NP):
                if i == 0:
                    sp.wait_ge(zeroed, 1)
                if i >= 2:
                    sp.wait_ge(lo, i - 1)
                    sp.wait_ge(tp, i - 1)
                rows = min(N, (i + 1) * PB * P) - i * PB * P
                full = rows // P
                sp.dma_start(xb[:, i % 2, 0:full * D].rearrange("p (k f) -> p k f", f=D),
                             x[i * PB * P:i * PB * P + full * P, :].rearrange("(k p) f -> p k f", p=P)).then_inc(x_in[i % 2], 16)
                if full < PB:
                    sp.dma_start(xb[0:rows - full * P, i % 2, full * D:], x[i * PB * P + full * P:N, :]).then_inc(x_in[i % 2], 16)
                if i >= 1:
                    sp.wait_ge(xt, i)
                    sp.dma_start(d["xT"][:, (i - 1) * PB * P:i * PB * P], xtb[:]).then_inc(xt_out, 16)
            sp.wait_ge(xt, NP)
            sp.dma_start(d["xT"][:, (NP - 1) * PB * P:], xtb[:]).then_inc(xt_out, 16)
            sp.wait_ge(consts, 3)
            sp.dma_start(d["ptab"][NPAD:ROWS, :], zrows[:]).then_inc(z_out, 16)
            sp.dma_start(d["xn"][NPAD:ROWS, :], zrowf[:]).then_inc(z_out, 16)
            sp.dma_start(d["heads"][NPAD:ROWS, :], zrowf[:]).then_inc(z_out, 16)
            sp.dma_start(d["score"][NPAD:ROWS, :], zrowf[:, 0:2 * HEADS]).then_inc(z_out, 16)
            with sp.Fori(0, NC) as c:
                sp.wait_ge(se_t, c)
                sp.dma_start(sum_e[:], rows_of(d["se"], c)).then_inc(s_in, 16)
                sp.wait_ge(inv_r, c + 1)
                waited(sp, past)
                sp.dma_start(d["inv"][:, bass.ds(c * CH, CH)], inv[:]).then_inc(i_out, 16)
                sp.wait_ge(ind_r, c + 1)
                sp.dma_start(d["ind"][:, bass.ds(c * CH, CH)], ind[:]).then_inc(n_out, 16)
                sp.wait_ge(me_r, c + 1)
                sp.dma_start(d["meT"][:, bass.ds(c * CH, CH)], mean_e[:]).then_inc(e_out, 16)
            for q, n in ((xt_out, NP), (z_out, 4), (i_out, NC), (n_out, NC), (e_out, NC)):
                sp.wait_ge(q, 16 * n)

        @block.scalar
        def _(act):
            for i in range(NP):
                piece = parts[:, i * PB:(i + 1) * PB, :, :]
                src = xb[:, i % 2, :].rearrange("p (k f) -> p k f", f=D)
                act.wait_ge(*piece_in(i))
                nc.scalar.copy(piece[:, :, 0, :], src).then_inc(hi, 1)
                act.wait_ge(tp, i + 1)
                if i:
                    act.wait_ge(xt_out, 16 * i)
                nc.scalar.copy(xtb[:], tp_ps[:].rearrange("p k n -> p (k n)")).then_inc(xt, 1)
                act.wait_ge(r, i + 1)
                nc.scalar.copy(piece[:, :, 1, :], rest[:].rearrange("p (k f) -> p k f", f=D)).then_inc(mid, 1)

        @block.vector
        def _(dve):
            for i in range(NP):
                piece = parts[:, i * PB:(i + 1) * PB, :, :]
                r3 = rest[:].rearrange("p (k f) -> p k f", f=D)
                dve.wait_ge(hi, i + 1)
                if i:
                    dve.wait_ge(lo, i)
                nc.vector.tensor_tensor(r3, xb[:, i % 2, :].rearrange("p (k f) -> p k f", f=D), piece[:, :, 0, :],
                                        ALU.subtract).then_inc(r, 1)
                dve.wait_ge(mid, i + 1)
                nc.vector.tensor_tensor(piece[:, :, 2, :], r3, piece[:, :, 1, :], ALU.subtract).then_inc(lo, 1)
            dve.wait_ge(dest_r, 1)
            with dve.Fori(0, NC) as c:
                dve.wait_ge(deg, c + 1)
                nc.vector.tensor_scalar(least1[:], deg_ps[:, 0:CH], 1.0, None, ALU.max).then_inc(m1, 1)
                dve.wait_ge(n_out, 16 * c)
                nc.vector.tensor_scalar(ind[:], deg_ps[:, 0:CH], 1.0, None, ALU.min).then_inc(ind_r, 1)
                dve.wait_ge(m1, c + 1)
                dve.wait_ge(i_out, 16 * c)
                nc.vector.reciprocal(inv[:], least1[:]).then_inc(inv_r, 1)
                dve.wait_ge(inv_r, c + 1)
                dve.wait_ge(e_out, 16 * c)
                dve.wait_ge(se_t, c + 1)
                nc.vector.tensor_tensor(mean_e[:], se_ps[:, 0:CH], inv[:], ALU.mult).then_inc(me_r, 1)

        @block.tensor
        def _(pe):
            for i in range(NP):
                pe.wait_ge(*piece_in(i))
                if i:
                    pe.wait_ge(xt, i)
                for k in range(PB):
                    ins = nc.tensor.transpose(tp_ps[:, k, :], xb[:, i % 2, k * D:(k + 1) * D], d["ident"][:])
                ins.then_inc(tp, 1)
            pe.wait_ge(consts, 1)
            with pe.Fori(0, NC) as c:
                pe.wait_ge(ind_r, c)
                for k in range(KB):
                    ins = nc.tensor.matmul(deg_ps[:, 0:CH], ones[:], d["AT"][:, k, bass.ds(c * CH, CH)],
                                           start=(k == 0), stop=(k == KB - 1))
                ins.then_inc(deg, 1)
                pe.wait_ge(s_in, 16 * (c + 1))
                pe.wait_ge(me_r, c)
                for s in range(SUB):
                    ins = nc.tensor.transpose(se_ps[:, s * SN:(s + 1) * SN], sum_e[:, s, :], d["ident"][0:SN, 0:SN])
                ins.then_inc(se_t, 1)


def sum_chunk(nc, d, out, c, between):
    for k in range(KB):
        for part in range(3):
            ins = nc.tensor.matmul(out, d["parts"][:, k, part, :], d["AT"][:, k, bass.ds(c * CH, CH)],
                                   start=(k == 0 and part == 0), stop=(k == KB - 1 and part == 2))
        if k in between:
            between[k]()
    return ins


def sum_all(nc, pe, d, agg, summed, taken, wait_parts, steps, at):
    def chunk(c, between):
        pe.wait_ge(taken, c)
        sum_chunk(nc, d, agg[:, bass.ds(c & 1, 1), 0:CH].rearrange("p a n -> p (a n)"), c, between).then_inc(summed, 1)

    pe.sem_inc(taken, 1)
    chunk(0, {5 * j - 1: (lambda j=j: wait_parts(j)) for j in range(1, 5)} | {})
    with pe.Fori(1, NC) as c:
        before = pe.snap(c - 1)
        chunk(c, {k: (lambda s=s: s(before)) for k, s in zip(at, steps)})
    for s in steps:
        s(NC - 1)


def load_parts(nc, d, eng, sems):
    for j in range(5):
        eng.dma_start(d["parts"][:, 5 * j:5 * j + 5, :, :].rearrange("p k a f -> p k (a f)"),
                      d["ptab"][5 * j * P:(5 * j + 5) * P, :].rearrange("(k p) f -> p k f", p=P)).then_inc(sems[j], 16)


def rows_of(ap, c):
    return ap[bass.ds(c * CH, CH), :].rearrange("(s p) f -> p s f", p=SN)


def phase_conv1(nc, d, w, repeats):
    with ExitStack() as ctx:
        m = Mem(nc, ctx, "c1")
        sT, inv, xT, hT = (m.sb(n, [P, CH]) for n in ("sT", "inv", "xT", "hT"))
        wl, wr = m.sb("wl", [D, D]), m.sb("wr", [D, D])
        vec = m.sb("vec", [D, 8])
        scale, shift, eps = m.sb("scale", [D, 1]), m.sb("shift", [D, 1]), m.sb("eps", [D, 1])
        rest = m.sb("rest", [SN, SUB, D])
        stage = m.sb("stage", [SN, SUB, 3, D], BF16)
        agg = m.ps("agg", [P, 2, 512])
        h_ps = m.ps("h_ps", [P, 512])
        t_ps = m.ps("t_ps", [SN, SUB, D])
        (w_in, cst, sd, v, summed, taken, i_in, x_in, h_done, h_ready, turned, hi, r, mid, lo, h_out, p_out, rep, rep_past) = (
            m.sem(n) for n in ("w_in", "cst", "sd", "v", "summed", "taken", "i_in", "x_in", "h_done", "h_ready",
                               "turned", "hi", "r", "mid", "lo", "h_out", "p_out", "rep", "rep_past"))
        names = ("b1", "bn_gamma", "bn_beta", "bn_mean", "bn_var")
        block = ctx.enter_context(nc.Block())

        @block.sync
        def _(sp):
            sp.dma_start(wl[:], w["L0_gnn_W1_l"]).then_inc(w_in, 16)
            sp.dma_start(wr[:], w["L0_gnn_W1_r"]).then_inc(w_in, 16)
            for n, name in enumerate(names):
                sp.dma_start(vec[:, n:n + 1], w["L0_gnn_" + name].rearrange("(p a) -> p a", a=1)).then_inc(w_in, 16)
            with sp.Fori(0, NC) as c:
                sp.wait_ge(taken, c + 1)
                sp.dma_start(inv[:], d["inv"][:, bass.ds(c * CH, CH)]).then_inc(i_in, 16)
                sp.wait_ge(h_done, c)
                sp.dma_start(xT[:], d["xT"][:, bass.ds(c * CH, CH)]).then_inc(x_in, 16)
                sp.wait_ge(h_ready, c + 1)
                sp.dma_start(d["hT"][:, bass.ds(c * CH, CH)], hT[:]).then_inc(h_out, 16)
                sp.wait_ge(lo, c + 1)
                sp.dma_start(rows_of(d["ptab"], c), stage[:].rearrange("p s a f -> p s (a f)")).then_inc(p_out, 16)
            sp.wait_ge(h_out, 16 * NC)
            sp.wait_ge(p_out, 16 * NC)

        @block.gpsimd
        def _(pool):
            nc.gpsimd.memset(eps[:], 1e-5).then_inc(cst, 1)

        @block.scalar
        def _(act):
            act.wait_ge(w_in, 16 * 7)
            act.wait_ge(cst, 1)
            nc.scalar.activation(vec[:, 5:6], vec[:, 4:5], ACT.Sqrt, bias=eps[:, 0:1]).then_inc(sd, 1)
            act.wait_ge(v, 4)
            with act.Fori(0, NC) as c:
                act.wait_ge(h_done, c + 1)
                act.wait_ge(h_out, 16 * c)
                act.wait_ge(turned, c)
                nc.scalar.activation(hT[:], h_ps[:, 0:CH], ACT.Relu, bias=shift[:, 0:1], scale=scale[:, 0:1]).then_inc(h_ready, 1)
                split_act(nc, act, t_ps[:], rest, stage, c, turned, r, p_out, hi, mid)

        @block.vector
        def _(dve):
            dve.wait_ge(sd, 1)
            nc.vector.reciprocal(vec[:, 6:7], vec[:, 5:6]).then_inc(v, 1)
            dve.wait_ge(v, 1)
            nc.vector.tensor_tensor(scale[:], vec[:, 1:2], vec[:, 6:7], ALU.mult).then_inc(v, 1)
            nc.vector.tensor_tensor(vec[:, 7:8], vec[:, 0:1], vec[:, 3:4], ALU.subtract)
            dve.wait_ge(v, 2)
            dve.drain()
            nc.vector.scalar_tensor_tensor(out=shift[:], in0=vec[:, 7:8], scalar=scale[:, 0:1], in1=vec[:, 2:3],
                                           op0=ALU.mult, op1=ALU.add).then_inc(v, 2)
            for k in range(2):
                repeats.block(dve, rep, rep_past, k, k)
            with dve.Fori(0, NC) as c:
                dve.wait_ge(summed, c + 1)
                dve.wait_ge(i_in, 16 * (c + 1))
                dve.wait_ge(h_done, c)
                nc.vector.tensor_tensor(sT[:], agg[:, bass.ds(c & 1, 1), 0:CH].rearrange("p a n -> p (a n)"), inv[:],
                                        ALU.mult).then_inc(taken, 1)
                repeats.block(dve, rep, rep_past, c * 2 + 2, c * 2 + 2)
                split_dve(nc, dve, t_ps[:], rest, stage, c, hi, mid, r, lo)
                repeats.block(dve, rep, rep_past, c * 2 + 3, c * 2 + 3)

        @block.tensor
        def _(pe):
            def hidden(c):
                pe.wait_ge(taken, c + 2)
                pe.wait_ge(x_in, 16 * (c + 1))
                pe.wait_ge(h_ready, c)
                nc.tensor.matmul(h_ps[:, 0:CH], wl[:], sT[:], start=True, stop=False)
                nc.tensor.matmul(h_ps[:, 0:CH], wr[:], xT[:], start=False, stop=True).then_inc(h_done, 1)

            def turn(c):
                pe.wait_ge(h_ready, c + 1)
                pe.wait_ge(r, c)
                for s in range(SUB):
                    ins = nc.tensor.transpose(t_ps[:, s, :], hT[:, s * SN:(s + 1) * SN], d["ident"][:])
                ins.then_inc(turned, 1)

            pe.wait_ge(w_in, 16 * 7)
            sum_all(nc, pe, d, agg, summed, taken, lambda j: None, (hidden, turn), (4, 10))


def split_act(nc, act, src, rest, stage, c, ready, r, stored, hi, mid):
    act.wait_ge(ready, c + 1)
    act.wait_ge(stored, 16 * c)
    nc.scalar.copy(stage[:, :, 0, :], src).then_inc(hi, 1)
    act.wait_ge(r, c + 1)
    nc.scalar.copy(stage[:, :, 1, :], rest[:]).then_inc(mid, 1)


def split_dve(nc, dve, src, rest, stage, c, hi, mid, r, lo):
    dve.wait_ge(hi, c + 1)
    dve.wait_ge(lo, c)
    nc.vector.tensor_tensor(rest[:], src, stage[:, :, 0, :], ALU.subtract).then_inc(r, 1)
    dve.wait_ge(mid, c + 1)
    nc.vector.tensor_tensor(stage[:, :, 2, :], rest[:], stage[:, :, 1, :], ALU.subtract).then_inc(lo, 1)


def waited(eng, sem):
    eng.sem_inc(sem, 1)


def norm_dve(nc, dve, y, stats, mv, sdev, rstd, out, c, y_ready, mv_ready, sd_ready, rs_ready, bn, out_ready):
    dve.wait_ge(y_ready, c + 1)
    for s in range(SUB):
        ins = nc.vector.bn_stats(stats[:, s, :], y[:, s, :])
    ins.then_inc(bn, 1)
    dve.wait_ge(bn, 2 * c + 1)
    waited(dve, bn)
    for s in range(SUB):
        ins = nc.vector.bn_aggr(mv[:, s, :], stats[:, s, :])
    ins.then_inc(mv_ready, 1)
    dve.wait_ge(sd_ready, c + 1)
    nc.vector.reciprocal(rstd[:], sdev[:]).then_inc(rs_ready, 1)
    dve.wait_ge(rs_ready, c + 1)
    for s in range(SUB):
        ins = nc.vector.tensor_scalar(out[:, s, :], y[:, s, :], mv[:, s, 0:1], rstd[:, s:s + 1], ALU.subtract, ALU.mult)
    ins.then_inc(out_ready, 1)


def phase_conv2(nc, d, w, repeats):
    with ExitStack() as ctx:
        m = Mem(nc, ctx, "c2")
        sT, inv, hT, xT, xtn = (m.sb(n, [P, CH]) for n in ("sT", "inv", "hT", "xT", "xtn"))
        wl, wr, wg, wgT = (m.sb(n, [D, D]) for n in ("wl", "wr", "wg", "wgT"))
        att = m.sb("att", [D, 2 * HEADS])
        wa = m.sb("wa", [D, 2 * HEADS])
        b2 = m.sb("b2", [1, D])
        ones = m.sb("ones", [1, SN])
        eps = m.sb("eps", [P, 1])
        stats, mv = m.sb("stats", [SN, SUB, 6]), m.sb("mv", [SN, SUB, 2])
        sdev, rstd = m.sb("sdev", [SN, SUB]), m.sb("rstd", [SN, SUB])
        xn = m.sb("xn", [SN, SUB, D])
        gb = m.sb("gb", [SN, SUB, D])
        sc = m.sb("sc", [SN, SUB, 2 * HEADS])
        ajb = m.sb("ajb", [HEADS, 3, CH], BF16)
        ajr = m.sb("ajr", [HEADS, CH])
        agg = m.ps("agg", [P, 2, 512])
        y_ps = m.ps("y_ps", [SN, SUB, D])
        x_ps = m.ps("x_ps", [P, 512])
        g_ps = m.ps("g_ps", [P, SUB, D])
        sc_ps = m.ps("sc_ps", [P, SUB, 128])
        aj_ps = m.ps("aj_ps", [HEADS, 512])
        names = ("w_in", "cst", "wt", "wtc", "wa_r", "wa_c", "summed", "taken", "i_in", "h_in", "x_in", "y_done", "bn", "mvr",
                 "sdr", "rsr", "xnr", "turned", "xtr", "proj", "gr", "scr", "aj_hi", "aj_r", "aj_mid", "aj_lo",
                 "xt_out", "xn_out", "g_out", "sc_out", "aj_out", "past", "rep", "rep_past")
        q = {n: m.sem(n) for n in names}
        parts_in = [m.sem(f"parts_in{j}") for j in range(5)]
        block = ctx.enter_context(nc.Block())

        @block.sync
        def _(sp):
            load_parts(nc, d, sp, parts_in)
            for t, name in ((wl, "L0_gnn_W2_l"), (wr, "L0_gnn_W2_r"), (wg, "L1_gnn_W")):
                sp.dma_start(t[:], w[name]).then_inc(q["w_in"], 16)
            sp.dma_start(b2[:], w["L0_gnn_b2"].rearrange("(a f) -> a f", a=1)).then_inc(q["w_in"], 16)
            sp.wait_ge(q["cst"], 1)
            for h in range(HEADS):
                rows = slice(h * HC, (h + 1) * HC)
                for half in range(2):
                    sp.dma_start(att[rows, half * HEADS + h:half * HEADS + h + 1],
                                 w["L1_gnn_att"][h:h + 1, (1 - half) * HC:(2 - half) * HC].rearrange("a c -> c a")).then_inc(q["w_in"], 16)
            with sp.Fori(0, NC) as c:
                cols = bass.ds(c * CH, CH)
                sp.wait_ge(q["taken"], c + 1)
                sp.dma_start(inv[:], d["inv"][:, cols]).then_inc(q["i_in"], 16)
                sp.wait_ge(q["y_done"], c)
                sp.dma_start(hT[:], d["hT"][:, cols]).then_inc(q["h_in"], 16)
                sp.dma_start(xT[:], d["xT"][:, cols]).then_inc(q["x_in"], 16)
                sp.wait_ge(q["xnr"], c + 1)
                sp.dma_start(rows_of(d["xn"], c), xn[:]).then_inc(q["xn_out"], 16)
                sp.wait_ge(q["xtr"], c + 1)
                sp.dma_start(d["xT"][:, cols], xtn[:]).then_inc(q["xt_out"], 16)
                sp.wait_ge(q["gr"], c + 1)
                sp.dma_start(rows_of(d["heads"], c), gb[:]).then_inc(q["g_out"], 16)
                sp.wait_ge(q["scr"], c + 1)
                sp.dma_start(rows_of(d["score"], c), sc[:]).then_inc(q["sc_out"], 16)
                sp.wait_ge(q["aj_lo"], c + 1)
                waited(sp, q["past"])
                sp.dma_start(d["aj"][:, :, cols].rearrange("a h n -> h a n"), ajb[:]).then_inc(q["aj_out"], 16)
            for n in ("xt_out", "xn_out", "g_out", "sc_out", "aj_out"):
                sp.wait_ge(q[n], 16 * NC)

        @block.gpsimd
        def _(pool):
            nc.gpsimd.memset(att[:], 0.0).then_inc(q["cst"], 1)
            nc.gpsimd.memset(ones[:], 1.0).then_inc(q["cst"], 1)
            nc.gpsimd.memset(eps[:], 1e-5).then_inc(q["cst"], 1)

        @block.scalar
        def _(act):
            act.wait_ge(q["wt"], 1)
            nc.scalar.copy(wgT[:], g_ps[:, 0, :]).then_inc(q["wtc"], 1)
            act.wait_ge(q["wa_r"], 1)
            nc.scalar.copy(wa[:], sc_ps[:, 0, 0:2 * HEADS]).then_inc(q["wa_c"], 1)
            act.wait_ge(q["cst"], 3)
            with act.Fori(0, NC) as c:
                act.wait_ge(q["mvr"], c + 1)
                nc.scalar.activation(sdev[:], mv[:, :, 1], ACT.Sqrt, bias=eps[0:SN, 0:1]).then_inc(q["sdr"], 1)
                act.wait_ge(q["turned"], c + 1)
                act.wait_ge(q["xt_out"], 16 * c)
                act.wait_ge(q["proj"], c)
                nc.scalar.copy(xtn[:], x_ps[:, 0:CH]).then_inc(q["xtr"], 1)
                act.wait_ge(q["proj"], c + 1)
                act.wait_ge(q["g_out"], 16 * c)
                nc.scalar.copy(gb[:], g_ps[0:SN, :, :]).then_inc(q["gr"], 1)
                act.wait_ge(q["sc_out"], 16 * c)
                nc.scalar.copy(sc[:], sc_ps[0:SN, :, 0:2 * HEADS]).then_inc(q["scr"], 1)
                act.wait_ge(q["aj_out"], 16 * c)
                nc.scalar.copy(ajb[:, 0, :], aj_ps[:, 0:CH]).then_inc(q["aj_hi"], 1)
                act.wait_ge(q["aj_r"], c + 1)
                nc.scalar.copy(ajb[:, 1, :], ajr[:]).then_inc(q["aj_mid"], 1)

        @block.vector
        def _(dve):
            first = 2 + 2 * NC
            for k in range(2):
                repeats.block(dve, q["rep"], q["rep_past"], first + k, k)
            with dve.Fori(0, NC) as c:
                dve.wait_ge(q["summed"], c + 1)
                dve.wait_ge(q["i_in"], 16 * (c + 1))
                dve.wait_ge(q["y_done"], c)
                nc.vector.tensor_tensor(sT[:], agg[:, bass.ds(c & 1, 1), 0:CH].rearrange("p a n -> p (a n)"), inv[:],
                                        ALU.mult).then_inc(q["taken"], 1)
                dve.wait_ge(q["xn_out"], 16 * c)
                dve.wait_ge(q["turned"], c)
                norm_dve(nc, dve, y_ps, stats, mv, sdev, rstd, xn, c, q["y_done"], q["mvr"], q["sdr"], q["rsr"], q["bn"], q["xnr"])
                repeats.block(dve, q["rep"], q["rep_past"], c + (first + 2), c + 2)
                dve.wait_ge(q["aj_hi"], c + 1)
                nc.vector.tensor_tensor(ajr[:], aj_ps[:, 0:CH], ajb[:, 0, :], ALU.subtract).then_inc(q["aj_r"], 1)
                dve.wait_ge(q["aj_mid"], c + 1)
                nc.vector.tensor_tensor(ajb[:, 2, :], ajr[:], ajb[:, 1, :], ALU.subtract).then_inc(q["aj_lo"], 1)
            repeats.finish(dve, q["rep"], KB - first)

        @block.tensor
        def _(pe):
            pe.wait_ge(q["w_in"], 16 * 12)
            nc.tensor.transpose(g_ps[:, 0, :], wg[:], d["ident"][:]).then_inc(q["wt"], 1)
            pe.wait_ge(q["wtc"], 1)
            nc.tensor.matmul(sc_ps[:, 0, 0:2 * HEADS], wgT[:], att[:], start=True, stop=True).then_inc(q["wa_r"], 1)
            pe.wait_ge(q["wa_c"], 1)
            pe.wait_ge(q["cst"], 3)

            def products(c):
                pe.wait_ge(q["taken"], c + 2)
                pe.wait_ge(q["h_in"], 16 * (c + 1))
                pe.wait_ge(q["x_in"], 16 * (c + 1))
                pe.wait_ge(q["xnr"], c)
                for s in range(SUB):
                    n = slice(s * SN, (s + 1) * SN)
                    nc.tensor.matmul(y_ps[:, s, :], xT[:, n], d["ident"][:], start=True, stop=False)
                    nc.tensor.matmul(y_ps[:, s, :], sT[:, n], wl[:], start=False, stop=False)
                    nc.tensor.matmul(y_ps[:, s, :], hT[:, n], wr[:], start=False, stop=False)
                    ins = nc.tensor.matmul(y_ps[:, s, :], ones[:], b2[:], start=False, stop=True)
                ins.then_inc(q["y_done"], 1)

            def turn(c):
                pe.wait_ge(q["xnr"], c + 1)
                pe.wait_ge(q["xtr"], c)
                for s in range(SUB):
                    ins = nc.tensor.transpose(x_ps[:, s * SN:(s + 1) * SN], xn[:, s, :], d["ident"][0:SN, 0:SN])
                ins.then_inc(q["turned"], 1)

            def project(c):
                pe.wait_ge(q["xtr"], c + 1)
                pe.wait_ge(q["aj_r"], c)
                for s in range(SUB):
                    nc.tensor.matmul(g_ps[0:SN, s, :], xtn[:, s * SN:(s + 1) * SN], wg[:], start=True, stop=True)
                for s in range(SUB):
                    nc.tensor.matmul(sc_ps[0:SN, s, 0:2 * HEADS], xtn[:, s * SN:(s + 1) * SN], wa[:], start=True, stop=True)
                nc.tensor.matmul(aj_ps[:, 0:CH], wa[:, 0:HEADS], xtn[:], start=True, stop=True).then_inc(q["proj"], 1)

            pe.wait_ge(parts_in[0], 16)
            sum_all(nc, pe, d, agg, q["summed"], q["taken"], lambda j: pe.wait_ge(parts_in[j], 16),
                    (products, turn, project), (3, 11, 19))


NOEDGE = -1e30
OWN = NPAD
SC = NPAD + 1
LAST = KB - 1


def phase_attention(nc, d):
    K = HEADS * TOPK
    with ExitStack() as ctx:
        m = Mem(nc, ctx, "at")
        spare = d["parts"][:].rearrange("p k a f -> p (k a f)").bitcast(F32)
        none = m.sb("none", [P, NPAD], BF16)
        S = [m.sb("S0", [P, SC]), spare[:, 0:SC]]
        G = spare[:, 3200:3200 + K * HC].rearrange("p (k c) -> p k c", c=HC)
        ajp = m.sb("ajp", [3 * HEADS, NPAD], BF16)
        pick = m.sb("pick", [3 * HEADS, HEADS, P], BF16)
        identb = m.sb("identb", [P, P], BF16)
        score = m.sb("score", [P, KB, 2 * HEADS])
        own = m.sb("own", [P, KB])
        headno = m.sb("headno", [P, K])
        within = m.sb("within", [P, K])
        eps, one = m.sb("eps", [P, 1]), m.sb("one", [P, 1])
        left = m.sb("left", [P, K])
        top = m.sb("top", [P, K])
        idx = m.sb("idx", [P, K], U32)
        idxf, isown, topc, count, upto, room, take, e, lr, rel, ex, wt, alpha = (
            m.sb(n, [P, K]) for n in ("idxf", "isown", "topc", "count", "upto", "room", "take", "e", "lr", "rel", "ex", "wt", "alpha"))
        node = m.sb("node", [P, K])
        rowno = m.sb("rowno", [P, K], U32)
        same = m.sb("same", [P, K, TOPK])
        den, rden = m.sb("den", [P, HEADS]), m.sb("rden", [P, HEADS])
        o, neg, ex2, y = (spare[:, 4224 + j * D:4224 + (j + 1) * D] for j in range(4))
        xb, xn, rest, xt = (m.sb(n, [P, D]) for n in ("xb", "xn", "rest", "xt"))
        stats, mv, sdev, rstd = m.sb("stats", [P, 6]), m.sb("mv", [P, 2]), m.sb("sdev", [P, 1]), m.sb("rstd", [P, 1])
        stage = m.sb("stage", [P, 3, D], BF16)
        s_ps = [m.ps(f"s_ps{i}", [P, 512]) for i in range(4)]
        t_ps = m.ps("t_ps", [P, 512])
        names = ("cst", "past", "past_sp", "past_pool", "in_", "nmr", "smm", "sev", "mx", "mi", "v", "own_in", "t", "relr", "exr", "rowr0", "rowr1", "gath0", "gath1", "aw0", "aw1", "or_", "negr", "ex2r",
                 "x_in", "yr", "bn", "mvr", "sdr", "rsr", "xnr", "tr", "xtr", "hi", "r", "mid", "lo", "xt_out", "p_out")
        q = {n: m.sem(n) for n in names}
        block = ctx.enter_context(nc.Block())

        def grid(t):
            return t[:].rearrange("p (h k) -> p h k", k=TOPK)

        @block.gpsimd
        def _(pool):
            kw = dict(allow_small_or_imprecise_dtypes=True)
            c = q["cst"]
            nc.gpsimd.iota(own[:], [[P, KB]], base=0, channel_multiplier=1, **kw).then_inc(c, 1)
            nc.gpsimd.iota(headno[:], [[1, HEADS], [0, TOPK]], base=0, channel_multiplier=0, **kw).then_inc(c, 1)
            nc.gpsimd.memset(within[:], 1.0).then_inc(c, 1)
            nc.gpsimd.memset(identb[:], 0.0).then_inc(c, 1)
            nc.gpsimd.memset(pick[:], 1.0).then_inc(c, 1)
            nc.gpsimd.memset(eps[:], 1e-5).then_inc(c, 1)
            nc.gpsimd.memset(one[:], 1.0).then_inc(c, 1)
            nc.gpsimd.iota(left[:], [[0, HEADS], [-1, TOPK]], base=TOPK, channel_multiplier=0, **kw).then_inc(c, 1)
            pool.wait_ge(c, 8)
            nc.gpsimd.memset(grid(within)[:, :, 0:1], 0.0).then_inc(c, 1)
            nc.gpsimd.affine_select(out=identb[:], in_=identb[:], compare_op=ALU.not_equal, fill=NOEDGE, base=0,
                                    pattern=[[-1, P]], channel_multiplier=1).then_inc(c, 1)
            nc.gpsimd.affine_select(out=pick[:], in_=pick[:], compare_op=ALU.is_ge, fill=0.0, base=0,
                                    pattern=[[-3, HEADS], [0, P]], channel_multiplier=1).then_inc(c, 1)
            pool.wait_ge(c, 11)
            nc.gpsimd.affine_select(out=pick[:], in_=pick[:], compare_op=ALU.is_ge, fill=0.0, base=2,
                                    pattern=[[3, HEADS], [0, P]], channel_multiplier=-1).then_inc(c, 1)
            heads = d["heads"].rearrange("n (h c) -> (n h) c", c=HC)
            pool.wait_ge(c, 12)
            with pool.Fori(0, KB) as i:
                for half in range(2):
                    pool.wait_ge(q[f"rowr{half}"], i + 1)
                    pool.wait_ge(q[f"aw{half}"], i)
                    waited(pool, q["past_pool"])
                    for k in range(half * K // 2, (half + 1) * K // 2):
                        nc.gpsimd.indirect_dma_start(G[:, k, :], None, heads, bass.IndirectOffsetOnAxis(
                            ap=rowno[:, k:k + 1], axis=0)).then_inc(q[f"gath{half}"], 16)

        @block.sync
        def _(sp):
            for h in range(HEADS):
                sp.dma_start(ajp[3 * h:3 * h + 3, :], d["aj"][:, h, :]).then_inc(q["in_"], 16)
            sp.dma_start(score[:], d["score"].rearrange("(i p) f -> p i f", p=P)).then_inc(q["in_"], 16)
            sp.dma_start(xb[:], d["xn"][0:P, :]).then_inc(q["x_in"], 16)

            def store(i):
                rows = bass.ds(i * P, P)
                sp.wait_ge(q["lo"], i + 1)
                sp.dma_start(d["ptab"][rows, :], stage[:].rearrange("p a f -> p (a f)")).then_inc(q["p_out"], 16)
                sp.wait_ge(q["xtr"], i + 1)
                waited(sp, q["past_sp"])
                sp.dma_start(d["xT"][:, rows], xt[:]).then_inc(q["xt_out"], 16)

            with sp.Fori(0, KB - 1) as i:
                sp.wait_ge(q["yr"], i + 1)
                sp.dma_start(xb[:], d["xn"][bass.ds((i + 1) * P, P), :]).then_inc(q["x_in"], 16)
                store(i)
            store(KB - 1)
            sp.wait_ge(q["xt_out"], 16 * KB)
            sp.wait_ge(q["p_out"], 16 * KB)

        @block.tensor
        def _(pe):
            pe.sem_inc(q["sev"], 4)
            pe.wait_ge(q["cst"], 12)
            pe.wait_ge(q["in_"], 16 * (HEADS + 1))

            def turn(i):
                pe.wait_ge(q["xnr"], i + 1)
                pe.wait_ge(q["xtr"], i)
                nc.tensor.transpose(t_ps[:, 0:P], xn[:], d["ident"][:]).then_inc(q["tr"], 1)

            def scores(i, then=None):
                pe.wait_ge(q["nmr"], i + 1)
                for h in range(HEADS):
                    for c in range(NC):
                        n = h * NC + c
                        cols = slice(c * CH, (c + 1) * CH)
                        pe.wait_ge(q["sev"], HEADS * NC * i + n + 1)
                        nc.tensor.matmul(s_ps[n % 4][:, 0:CH], identb[:], none[:, cols], start=True, stop=False)
                        nc.tensor.matmul(s_ps[n % 4][:, 0:CH], pick[:, h, :], ajp[:, cols], start=False, stop=True).then_inc(q["smm"], 1)
                    if h == 2 and then is not None:
                        turn(then)

            scores(0)
            scores(1)
            scores(2)
            with pe.Fori(3, KB) as i:
                scores(i, pe.snap(i - 3))
            for i in range(KB - 3, KB):
                turn(i)

        @block.scalar
        def _(act):
            act.wait_ge(q["in_"], 16 * (HEADS + 1))
            act.wait_ge(q["cst"], 12)

            def evacuate(i, h):
                for c in range(NC):
                    n = h * NC + c
                    act.wait_ge(q["smm"], HEADS * NC * i + n + 1)
                    if c == 0:
                        act.wait_ge(q["mi"], HEADS * i + h + 1)
                    nc.scalar.copy(S[h % 2][:, c * CH:(c + 1) * CH], s_ps[n % 4][:, 0:CH]).then_inc(q["sev"], 1)
                nc.scalar.copy(S[h % 2][:, OWN:SC], score[:, bass.ds(i, 1), h:h + 1].rearrange("p a b -> p (a b)")).then_inc(q["own_in"], 1)

            def no_edges(i):
                if not isinstance(i, int) or i:
                    act.wait_ge(q["smm"], HEADS * NC * i)
                nc.scalar.activation(none[:], d["AT"][:, bass.ds(i, 1), :].rearrange("p a n -> p (a n)"), ACT.Relu,
                                     bias=one[:, 0:1], scale=-1.0).then_inc(q["nmr"], 1)

            def softmax(i):
                act.wait_ge(q["relr"], i + 1)
                nc.scalar.activation(ex[:], rel[:], ACT.Exp).then_inc(q["exr"], 1)

            def elu(i):
                act.wait_ge(q["negr"], i + 1)
                nc.scalar.activation(ex2, neg, ACT.Exp).then_inc(q["ex2r"], 1)

            def deviation(i):
                act.wait_ge(q["mvr"], i + 1)
                nc.scalar.activation(sdev[:], mv[:, 1:2], ACT.Sqrt, bias=eps[:, 0:1]).then_inc(q["sdr"], 1)

            def split_hi(i):
                act.wait_ge(q["xnr"], i + 1)
                act.wait_ge(q["p_out"], 16 * i)
                nc.scalar.copy(stage[:, 0, :], xn[:]).then_inc(q["hi"], 1)

            def split_mid(i):
                act.wait_ge(q["r"], i + 1)
                nc.scalar.copy(stage[:, 1, :], rest[:]).then_inc(q["mid"], 1)

            def turned(i):
                act.wait_ge(q["tr"], i + 1)
                act.wait_ge(q["xt_out"], 16 * i)
                nc.scalar.copy(xt[:], t_ps[:, 0:P]).then_inc(q["xtr"], 1)

            def tile(i, before, old, older, following):
                evacuate(i, 1)
                evacuate(i, 2)
                if old is not None:
                    deviation(old)
                evacuate(i, 3)
                if following is not None:
                    no_edges(following)
                if old is not None:
                    split_hi(old)
                if older is not None:
                    turned(older)
                if old is not None:
                    split_mid(old)
                if following is not None:
                    evacuate(following, 0)
                if before is not None:
                    elu(before)
                softmax(i)

            no_edges(0)
            evacuate(0, 0)
            tile(0, None, None, None, 1)
            tile(1, 0, None, None, 2)
            tile(2, 1, 0, None, 3)
            with act.Fori(3, LAST) as i:
                tile(i, act.snap(i - 1), act.snap(i - 2), act.snap(i - 3), act.snap(i + 1))
            tile(LAST, LAST - 1, LAST - 2, LAST - 3, None)
            for i in (LAST - 1, LAST):
                if i == LAST:
                    elu(i)
                deviation(i)
                split_hi(i)
                turned(i - 1)
                split_mid(i)
            turned(LAST)

        @block.vector
        def _(dve):
            dve.sem_inc(q["mi"], 2)
            dve.wait_ge(q["cst"], 12)
            nc.vector.tensor_scalar(own[:], own[:], float(N - 1), float(-OWN), ALU.min, ALU.add).then_inc(q["v"], 1)
            dve.wait_ge(q["in_"], 16 * (HEADS + 1))
            STEPS = 17

            def greatest(i, h):
                dve.wait_ge(q["sev"], HEADS * NC * i + NC * (h + 1) + 4)
                dve.wait_ge(q["own_in"], HEADS * i + h + 1)
                waited(dve, q["past"])
                nc.vector.max(top[:, h * TOPK:(h + 1) * TOPK], S[h % 2][:] if h % 2 == 0 else S[1]).then_inc(q["mx"], 1)

            def places(i, h):
                dve.wait_ge(q["mx"], HEADS * i + h + 1)
                waited(dve, q["past"])
                nc.vector.max_index(idx[:, h * TOPK:(h + 1) * TOPK], top[:, h * TOPK:(h + 1) * TOPK],
                                    S[h % 2][:] if h % 2 == 0 else S[1]).then_inc(q["mi"], 1)

            def done(i, k, ins):
                ins.then_inc(q["t"], 1)

            def after(i, k):
                dve.wait_ge(q["t"], STEPS * i + k)

            def row_numbers(i, half):
                V = nc.vector
                part = slice(half * K // 2, (half + 1) * K // 2)
                if half == 0:
                    dve.wait_ge(q["mi"], HEADS * i + HEADS + 2)
                    done(i, 1, V.tensor_copy(idxf[:], idx[:]))
                    done(i, 2, V.tensor_scalar(isown[:], idx[:], float(OWN), None, ALU.is_equal))
                    done(i, 3, V.tensor_copy(topc[:], top[:]))
                    after(i, 2)
                    done(i, 4, V.scalar_tensor_tensor(out=node[:], in0=isown[:], scalar=own[:, bass.ds(i, 1)], in1=idxf[:],
                                                      op0=ALU.mult, op1=ALU.add))
                    after(i, 4)
                dve.wait_ge(q[f"gath{half}"], 8 * K * i)
                V.scalar_tensor_tensor(out=rowno[:, part], in0=node[:, part], scalar=float(HEADS), in1=headno[:, part],
                                       op0=ALU.mult, op1=ALU.add).then_inc(q[f"rowr{half}"], 1)

            def weights(i):
                V = nc.vector
                again = d["again"][:, bass.ds(i, 1), :].to_broadcast([P, K, TOPK])
                more = d["more"][:, bass.ds(i, 1), :].to_broadcast([P, K, TOPK])
                ai = score[:, bass.ds(i, 1), HEADS:2 * HEADS].rearrange("p a h -> p h a").to_broadcast([P, HEADS, TOPK])
                done(i, 5, V.tensor_tensor(same[:], idxf[:].unsqueeze(2).to_broadcast([P, K, TOPK]), again, ALU.is_equal))
                done(i, 6, V.tensor_tensor(grid(e), grid(topc), ai, ALU.add))
                after(i, 5)
                done(i, 7, V.tensor_tensor(same[:], same[:], more, ALU.mult))
                after(i, 6)
                done(i, 8, V.scalar_tensor_tensor(out=lr[:], in0=e[:], scalar=0.2, in1=e[:], op0=ALU.mult, op1=ALU.max))
                after(i, 7)
                done(i, 9, V.tensor_reduce(count[:], same[:], AX.X, ALU.add))
                after(i, 8)
                V.tensor_tensor(grid(rel), grid(lr), grid(lr)[:, :, 0:1].to_broadcast([P, HEADS, TOPK]),
                                ALU.subtract).then_inc(q["relr"], 1)
                after(i, 9)
                done(i, 10, V.tensor_tensor_scan(upto[:], within[:], count[:], 0.0, ALU.mult, ALU.add))
                done(i, 11, V.tensor_tensor(room[:], left[:], count[:], ALU.add))
                after(i, 10)
                after(i, 11)
                done(i, 12, V.scalar_tensor_tensor(out=room[:], in0=upto[:], scalar=-1.0, in1=room[:], op0=ALU.mult, op1=ALU.add))
                after(i, 12)
                done(i, 13, V.scalar_tensor_tensor(out=take[:], in0=count[:], scalar=1.0, in1=room[:], op0=ALU.add, op1=ALU.min))

            def shares(i, k):
                V = nc.vector
                if k == 0:
                    after(i, 13)
                    dve.wait_ge(q["exr"], i + 1)
                    done(i, 14, V.scalar_tensor_tensor(out=wt[:], in0=take[:], scalar=0.0, in1=ex[:], op0=ALU.max, op1=ALU.mult))

                elif k == 1:
                    after(i, 14)
                    done(i, 15, V.tensor_reduce(den[:], grid(wt), AX.X, ALU.add))
                elif k == 2:
                    after(i, 15)
                    done(i, 16, V.reciprocal(rden[:], den[:]))
                else:
                    after(i, 16)
                    done(i, 17, V.tensor_tensor(grid(alpha), grid(wt), rden[:].unsqueeze(2).to_broadcast([P, HEADS, TOPK]), ALU.mult))

            def combine(i, half):
                part = slice(half * K // 2, (half + 1) * K // 2)
                if half == 0:
                    after(i, 17)
                dve.wait_ge(q[f"gath{half}"], 8 * K * (i + 1))
                nc.vector.tensor_tensor(G[:, part, :], G[:, part, :], alpha[:, part].unsqueeze(2).to_broadcast([P, K // 2, HC]),
                                        ALU.mult).then_inc(q["or_"], 1)
                dve.wait_ge(q["or_"], 2 * i + half + 1)
                nc.vector.tensor_reduce(o[:, half * D // 2:(half + 1) * D // 2].rearrange("p (h c) -> p h c", c=HC),
                                        G[:, part, :].rearrange("p (h k) c -> p h c k", k=TOPK), AX.X, ALU.add).then_inc(q[f"aw{half}"], 1)
                if half == 1:
                    dve.wait_ge(q["aw1"], i + 1)
                    nc.vector.tensor_scalar(neg, o, 0.0, None, ALU.min).then_inc(q["negr"], 1)

            def residual(i, k):
                if k == 0:
                    dve.wait_ge(q["ex2r"], i + 1)
                    dve.wait_ge(q["x_in"], 16 * (i + 1))
                    nc.vector.scalar_tensor_tensor(out=y, in0=o, scalar=0.0, in1=ex2, op0=ALU.max, op1=ALU.add).then_inc(q["bn"], 1)
                elif k == 1:
                    dve.wait_ge(q["bn"], 3 * i + 1)
                    nc.vector.scalar_tensor_tensor(out=y, in0=y, scalar=-1.0, in1=xb[:], op0=ALU.add, op1=ALU.add).then_inc(q["yr"], 1)
                elif k == 2:
                    dve.wait_ge(q["yr"], i + 1)
                    nc.vector.bn_stats(stats[:], y).then_inc(q["bn"], 2)
                else:
                    dve.wait_ge(q["bn"], 3 * i + 3)
                    waited(dve, q["past"])
                    nc.vector.bn_aggr(mv[:], stats[:]).then_inc(q["mvr"], 1)

            def normalize(i, k):
                if k == 0:
                    dve.wait_ge(q["sdr"], i + 1)
                    nc.vector.reciprocal(rstd[:], sdev[:]).then_inc(q["rsr"], 1)
                else:
                    dve.wait_ge(q["rsr"], i + 1)
                    dve.wait_ge(q["tr"], i)
                    dve.wait_ge(q["hi"], i)
                    nc.vector.tensor_scalar(xn[:], y, mv[:, 0:1], rstd[:, 0:1], ALU.subtract, ALU.mult).then_inc(q["xnr"], 1)

            def split_r(i):
                dve.wait_ge(q["hi"], i + 1)
                nc.vector.tensor_tensor(rest[:], xn[:], stage[:, 0, :], ALU.subtract).then_inc(q["r"], 1)

            def split_lo(i):
                dve.wait_ge(q["mid"], i + 1)
                nc.vector.tensor_tensor(stage[:, 2, :], rest[:], stage[:, 1, :], ALU.subtract).then_inc(q["lo"], 1)

            def tile(i, before, old):
                greatest(i, 0)
                if before is not None:
                    shares(before, 0)
                if old is not None:
                    residual(old, 0)
                places(i, 0)
                if before is not None:
                    shares(before, 1)
                if old is not None:
                    residual(old, 1)
                greatest(i, 1)
                if before is not None:
                    shares(before, 2)
                if old is not None:
                    residual(old, 2)
                places(i, 1)
                if before is not None:
                    shares(before, 3)
                if old is not None:
                    residual(old, 3)
                greatest(i, 2)
                if before is not None:
                    combine(before, 0)
                if old is not None:
                    normalize(old, 0)
                places(i, 2)
                if old is not None:
                    normalize(old, 1)
                greatest(i, 3)
                if old is not None:
                    split_r(old)
                places(i, 3)
                if old is not None:
                    split_lo(old)
                row_numbers(i, 0)
                if before is not None:
                    combine(before, 1)
                row_numbers(i, 1)
                weights(i)

            tile(0, None, None)
            tile(1, 0, None)
            with dve.Fori(2, KB) as i:
                tile(i, dve.snap(i - 1), dve.snap(i - 2))
            for i in (LAST - 1, LAST):
                if i == LAST:
                    for k in range(4):
                        shares(i, k)
                    combine(i, 0)
                    combine(i, 1)
                for k in range(4):
                    residual(i, k)
                for k in range(2):
                    normalize(i, k)
                split_r(i)
                split_lo(i)


def phase_gru(nc, d, w, t, last):
    with ExitStack() as ctx:
        m = Mem(nc, ctx, f"g{t}")
        sT, inv, ind, hT, hm, meT, r, z = (m.sb(n, [P, CH]) for n in ("sT", "inv", "ind", "hT", "hm", "meT", "r", "z"))
        a = [m.sb(f"a{j}", [P, 512]) for j in range(2)]
        hnew = a[0]
        rest = a[1][0:SN, :].rearrange("p (s f) -> p s f", f=D)
        xn = a[0][0:SN, :].rearrange("p (s f) -> p s f", f=D)
        stage = m.sb("stage", [SN, SUB, 3, D], BF16)
        wm, wi, wh = m.sb("wm", [D, 3, 2 * D]), m.sb("wi", [D, 2, 3 * D]), m.sb("wh", [D, 3 * D])
        bm = m.sb("bm", [1, 2 * D])
        bi, bh, brz = m.sb("bi", [D, 3]), m.sb("bh", [D, 3]), m.sb("brz", [D, 2])
        if last:
            xT = m.sb("xT", [P, CH])
            stats, mv = m.sb("stats", [SN, SUB, 6]), m.sb("mv", [SN, SUB, 2])
            sdev, rstd = m.sb("sdev", [SN, SUB]), m.sb("rstd", [SN, SUB])
            eps = m.sb("eps", [P, 1])
        agg = m.ps("agg", [P, 2, 512])
        a_ps = [m.ps(f"a_ps{j}", [P, 512]) for j in range(2)]
        gate_ps = [m.ps(f"gate_ps{j}", [P, 512]) for j in range(4)]
        t_ps = a_ps[0][0:SN, :].rearrange("p (s f) -> p s f", f=D)
        names = ("w_in", "cst", "b", "summed", "taken", "i_in", "n_in", "h_in", "e_in", "x_in", "hmr", "a_done", "a_out", "gates",
                 "rr", "zr", "u", "nin", "nr", "v1", "v2", "hr", "td", "hi", "r_", "mid", "lo", "h_out", "p_out",
                 "bn", "mvr", "sdr", "rsr", "xnr", "xn_out", "y_done")
        q = {n: m.sem(n) for n in names}
        parts_in = [m.sem(f"parts_in{j}") for j in range(5)]
        h_from = d["hT"] if t else d["xT"]
        final = q["xnr"] if last else q["hr"]
        block = ctx.enter_context(nc.Block())

        @block.sync
        def _(sp):
            load_parts(nc, d, sp, parts_in)
            sp.dma_start(wm[:], w[f"L2_gnn_W_msg_{t}"].rearrange("(k p) n -> p k n", p=D)).then_inc(q["w_in"], 16)
            sp.dma_start(wi[:], w[f"L2_gnn_Wih_{t}"].rearrange("(k p) n -> p k n", p=D)).then_inc(q["w_in"], 16)
            sp.dma_start(wh[:], w[f"L2_gnn_Whh_{t}"]).then_inc(q["w_in"], 16)
            sp.dma_start(bm[:], w[f"L2_gnn_b_msg_{t}"].rearrange("(a f) -> a f", a=1)).then_inc(q["w_in"], 16)
            sp.dma_start(bi[:], w[f"L2_gnn_bih_{t}"].rearrange("(k p) -> p k", p=D), allow_slow_non_contiguous=True).then_inc(q["w_in"], 16)
            sp.dma_start(bh[:], w[f"L2_gnn_bhh_{t}"].rearrange("(k p) -> p k", p=D), allow_slow_non_contiguous=True).then_inc(q["w_in"], 16)
            with sp.Fori(0, NC) as c:
                cols = bass.ds(c * CH, CH)
                sp.wait_ge(q["taken"], c + 1)
                sp.dma_start(inv[:], d["inv"][:, cols]).then_inc(q["i_in"], 16)
                sp.wait_ge(q["a_done"], c)
                sp.dma_start(ind[:], d["ind"][:, cols]).then_inc(q["n_in"], 16)
                sp.dma_start(meT[:], d["meT"][:, cols]).then_inc(q["e_in"], 16)
                sp.wait_ge(q["hr"], c)
                sp.dma_start(hT[:], h_from[:, cols]).then_inc(q["h_in"], 16)
                if last:
                    sp.wait_ge(q["y_done"], c)
                    sp.dma_start(xT[:], d["xT"][:, cols]).then_inc(q["x_in"], 16)
                    sp.wait_ge(q["xnr"], c + 1)
                    sp.dma_start(rows_of(d["xn"], c), xn).then_inc(q["xn_out"], 16)
                else:
                    sp.wait_ge(q["hr"], c + 1)
                    sp.dma_start(d["hT"][:, cols], hnew[:, 0:CH]).then_inc(q["h_out"], 16)
                sp.wait_ge(q["lo"], c + 1)
                sp.dma_start(rows_of(d["ptab"], c), stage[:].rearrange("p s a f -> p s (a f)")).then_inc(q["p_out"], 16)
            sp.wait_ge(q["xn_out"] if last else q["h_out"], 16 * NC)
            sp.wait_ge(q["p_out"], 16 * NC)

        if last:
            @block.gpsimd
            def _(pool):
                nc.gpsimd.memset(eps[:], 1e-5).then_inc(q["cst"], 1)

        @block.scalar
        def _(act):
            act.wait_ge(q["w_in"], 16 * 6)
            act.wait_ge(q["b"], 1)
            if last:
                act.wait_ge(q["cst"], 1)
            with act.Fori(0, NC) as c:
                act.wait_ge(q["a_done"], c + 1)
                act.wait_ge(q["xn_out"] if last else q["h_out"], 16 * c)
                if not last:
                    act.wait_ge(q["td"], c)
                nc.scalar.copy(a[0][:, 0:CH], a_ps[0][:, 0:CH])
                act.wait_ge(q["lo"], c)
                nc.scalar.copy(a[1][:, 0:CH], a_ps[1][:, 0:CH]).then_inc(q["a_out"], 1)
                act.wait_ge(q["gates"], c + 1)
                nc.scalar.activation(r[:], gate_ps[0][:, 0:CH], ACT.Sigmoid, bias=brz[:, 0:1]).then_inc(q["rr"], 1)
                nc.scalar.activation(z[:], gate_ps[1][:, 0:CH], ACT.Sigmoid, bias=brz[:, 1:2]).then_inc(q["zr"], 1)
                act.wait_ge(q["nin"], c + 1)
                nc.scalar.activation(r[:], r[:], ACT.Tanh, bias=bi[:, 2:3]).then_inc(q["nr"], 1)
                if last:
                    act.wait_ge(q["mvr"], c + 1)
                    nc.scalar.activation(sdev[:], mv[:, :, 1], ACT.Sqrt, bias=eps[0:SN, 0:1]).then_inc(q["sdr"], 1)
                split_act(nc, act, xn if last else t_ps, rest, stage, c, q["xnr"] if last else q["td"], q["r_"], q["p_out"],
                          q["hi"], q["mid"])

        @block.vector
        def _(dve):
            dve.wait_ge(q["w_in"], 16 * 6)
            nc.vector.tensor_tensor(brz[:], bi[:, 0:2], bh[:, 0:2], ALU.add).then_inc(q["b"], 1)
            with dve.Fori(0, NC) as c:
                dve.wait_ge(q["h_in"], 16 * (c + 1))
                dve.wait_ge(q["n_in"], 16 * (c + 1))
                dve.wait_ge(q["a_done"], c)
                nc.vector.tensor_tensor(hm[:], hT[:], ind[:], ALU.mult).then_inc(q["hmr"], 1)
                dve.wait_ge(q["summed"], c + 1)
                dve.wait_ge(q["i_in"], 16 * (c + 1))
                nc.vector.tensor_tensor(sT[:], agg[:, bass.ds(c & 1, 1), 0:CH].rearrange("p a n -> p (a n)"), inv[:],
                                        ALU.mult).then_inc(q["taken"], 1)
                dve.wait_ge(q["rr"], c + 1)
                nc.vector.scalar_tensor_tensor(out=r[:], in0=gate_ps[3][:, 0:CH], scalar=bh[:, 2:3], in1=r[:],
                                               op0=ALU.add, op1=ALU.mult).then_inc(q["u"], 1)
                dve.wait_ge(q["u"], c + 1)
                nc.vector.tensor_tensor(r[:], r[:], gate_ps[2][:, 0:CH], ALU.add).then_inc(q["nin"], 1)
                dve.wait_ge(q["nr"], c + 1)
                dve.wait_ge(q["zr"], c + 1)
                nc.vector.tensor_tensor(hm[:], hT[:], r[:], ALU.subtract).then_inc(q["v1"], 1)
                dve.wait_ge(q["v1"], c + 1)
                nc.vector.tensor_tensor(z[:], hm[:], z[:], ALU.mult).then_inc(q["v2"], 1)
                dve.wait_ge(q["v2"], c + 1)
                nc.vector.tensor_tensor(hnew[:, 0:CH], z[:], r[:], ALU.add).then_inc(q["hr"], 1)
                if last:
                    norm_dve(nc, dve, t_ps, stats, mv, sdev, rstd, xn, c, q["y_done"], q["mvr"], q["sdr"], q["rsr"], q["bn"], q["xnr"])
                split_dve(nc, dve, xn if last else t_ps, rest, stage, c, q["hi"], q["mid"], q["r_"], q["lo"])

        @block.tensor
        def _(pe):
            def message(c):
                pe.wait_ge(q["taken"], c + 2)
                pe.wait_ge(q["hmr"], c + 1)
                pe.wait_ge(q["e_in"], 16 * (c + 1))
                pe.wait_ge(q["r_"], c)
                for j in range(2):
                    out = a_ps[j][:, 0:CH]
                    n = slice(j * D, (j + 1) * D)
                    nc.tensor.matmul(out, wm[:, 2, n], meT[:], start=True, stop=False)
                    nc.tensor.matmul(out, wm[:, 0, n], hm[:], start=False, stop=False)
                    nc.tensor.matmul(out, wm[:, 1, n], sT[:], start=False, stop=False)
                    ins = nc.tensor.matmul(out, bm[:, n], ind[0:1, :], start=False, stop=True)
                ins.then_inc(q["a_done"], 1)

            def gates(c):
                pe.wait_ge(q["hr"], c)
                for g in range(3):
                    n = slice(g * D, (g + 1) * D)
                    hid = gate_ps[g if g < 2 else 3][:, 0:CH]
                    nc.tensor.matmul(hid, wh[:, n], hT[:], start=True, stop=g == 2)
                    if g == 0:
                        pe.wait_ge(q["a_out"], c + 1)
                    out = gate_ps[g][:, 0:CH]
                    nc.tensor.matmul(out, wi[:, 0, n], a[0][:, 0:CH], start=g == 2, stop=False)
                    ins = nc.tensor.matmul(out, wi[:, 1, n], a[1][:, 0:CH], start=False, stop=True)
                ins.then_inc(q["gates"], 1)

            def turn(c):
                pe.wait_ge(q["hr"], c + 1)
                if last:
                    pe.wait_ge(q["x_in"], 16 * (c + 1))
                for s in range(SUB):
                    n = slice(s * SN, (s + 1) * SN)
                    if last:
                        nc.tensor.matmul(t_ps[:, s, :], xT[:, n], d["ident"][:], start=True, stop=False)
                        ins = nc.tensor.matmul(t_ps[:, s, :], hnew[:, n], d["ident"][:], start=False, stop=True)
                    else:
                        ins = nc.tensor.transpose(t_ps[:, s, :], hnew[:, n], d["ident"][:])
                ins.then_inc(q["y_done"] if last else q["td"], 1)

            pe.wait_ge(q["w_in"], 16 * 6)
            pe.wait_ge(parts_in[0], 16)
            sum_all(nc, pe, d, agg, q["summed"], q["taken"], lambda j: pe.wait_ge(parts_in[j], 16),
                    (message, gates, turn), (3, 8, 18))


def phase_hop1(nc, d):
    with ExitStack() as ctx:
        m = Mem(nc, ctx, "h1")
        sT = m.sb("sT", [P, CH])
        rest = m.sb("rest", [SN, SUB, D])
        stage = m.sb("stage", [SN, SUB, 3, D], BF16)
        agg = m.ps("agg", [P, 2, 512])
        t_ps = m.ps("t_ps", [SN, SUB, D])
        summed, taken, td, hi, r, mid, lo, p_out = (
            m.sem(n) for n in ("summed", "taken", "td", "hi", "r", "mid", "lo", "p_out"))
        parts_in = [m.sem(f"parts_in{j}") for j in range(5)]
        block = ctx.enter_context(nc.Block())

        @block.sync
        def _(sp):
            load_parts(nc, d, sp, parts_in)
            with sp.Fori(0, NC) as c:
                sp.wait_ge(lo, c + 1)
                sp.dma_start(rows_of(d["ptab"], c), stage[:].rearrange("p s a f -> p s (a f)")).then_inc(p_out, 16)
            sp.wait_ge(p_out, 16 * NC)

        @block.scalar
        def _(act):
            with act.Fori(0, NC) as c:
                split_act(nc, act, t_ps[:], rest, stage, c, td, r, p_out, hi, mid)

        @block.vector
        def _(dve):
            with dve.Fori(0, NC) as c:
                dve.wait_ge(summed, c + 1)
                dve.wait_ge(td, c)
                nc.vector.tensor_copy(sT[:], agg[:, bass.ds(c & 1, 1), 0:CH].rearrange("p a n -> p (a n)")).then_inc(taken, 1)
                split_dve(nc, dve, t_ps[:], rest, stage, c, hi, mid, r, lo)

        @block.tensor
        def _(pe):
            def turn(c):
                pe.wait_ge(taken, c + 2)
                pe.wait_ge(r, c)
                for s in range(SUB):
                    ins = nc.tensor.transpose(t_ps[:, s, :], sT[:, s * SN:(s + 1) * SN], d["ident"][:])
                ins.then_inc(td, 1)

            pe.wait_ge(parts_in[0], 16)
            sum_all(nc, pe, d, agg, summed, taken, lambda j: pe.wait_ge(parts_in[j], 16), (turn,), (4,))


def phase_hop2(nc, d, w, out):
    with ExitStack() as ctx:
        m = Mem(nc, ctx, "h2")
        sT = m.sb("sT", [P, CH])
        wf, bf, ones = m.sb("wf", [D, D]), m.sb("bf", [1, D]), m.sb("ones", [1, SN])
        xb, y, xo = (m.sb(n, [SN, SUB, D]) for n in ("xb", "y", "xo"))
        stats, mv = m.sb("stats", [SN, SUB, 6]), m.sb("mv", [SN, SUB, 2])
        sdev, rstd = m.sb("sdev", [SN, SUB]), m.sb("rstd", [SN, SUB])
        eps = m.sb("eps", [P, 1])
        agg = m.ps("agg", [P, 2, 512])
        y_ps = m.ps("y_ps", [SN, SUB, D])
        names = ("w_in", "cst", "summed", "taken", "x_in", "y_done", "yr", "bn", "mvr", "sdr", "rsr", "xor_", "o_out")
        q = {n: m.sem(n) for n in names}
        parts_in = [m.sem(f"parts_in{j}") for j in range(5)]
        block = ctx.enter_context(nc.Block())

        @block.sync
        def _(sp):
            load_parts(nc, d, sp, parts_in)
            sp.dma_start(wf[:], w["L3_gnn_W"]).then_inc(q["w_in"], 16)
            sp.dma_start(bf[:], w["L3_gnn_b"].rearrange("(a f) -> a f", a=1)).then_inc(q["w_in"], 16)

            def load(c):
                sp.wait_ge(q["yr"], c)
                sp.dma_start(xb[:], rows_of(d["xn"], c)).then_inc(q["x_in"], 16)
                sp.wait_ge(q["xor_"], c + 1)

            with sp.Fori(0, NC - 1) as c:
                load(c)
                sp.dma_start(rows_of(out, c), xo[:]).then_inc(q["o_out"], 16)
            load(NC - 1)
            first = (NC - 1) * CH
            whole = (N - first) // SN
            sp.dma_start(out[first:first + whole * SN, :].rearrange("(s p) f -> p s f", p=SN),
                         xo[:, 0:whole, :]).then_inc(q["o_out"], 16)
            sp.dma_start(out[first + whole * SN:N, :], xo[0:N - first - whole * SN, whole, :]).then_inc(q["o_out"], 16)
            sp.wait_ge(q["o_out"], 16 * (NC + 1))

        @block.gpsimd
        def _(pool):
            nc.gpsimd.memset(eps[:], 1e-5).then_inc(q["cst"], 1)
            nc.gpsimd.memset(ones[:], 1.0).then_inc(q["cst"], 1)

        @block.scalar
        def _(act):
            act.wait_ge(q["cst"], 2)
            with act.Fori(0, NC) as c:
                act.wait_ge(q["mvr"], c + 1)
                nc.scalar.activation(sdev[:], mv[:, :, 1], ACT.Sqrt, bias=eps[0:SN, 0:1]).then_inc(q["sdr"], 1)

        @block.vector
        def _(dve):
            with dve.Fori(0, NC) as c:
                dve.wait_ge(q["summed"], c + 1)
                dve.wait_ge(q["y_done"], c)
                nc.vector.tensor_copy(sT[:], agg[:, bass.ds(c & 1, 1), 0:CH].rearrange("p a n -> p (a n)")).then_inc(q["taken"], 1)
                dve.wait_ge(q["y_done"], c + 1)
                dve.wait_ge(q["x_in"], 16 * (c + 1))
                nc.vector.tensor_tensor(y[:], y_ps[:], xb[:], ALU.add).then_inc(q["yr"], 1)
                dve.wait_ge(q["o_out"], 16 * c)
                norm_dve(nc, dve, y, stats, mv, sdev, rstd, xo, c, q["yr"], q["mvr"], q["sdr"], q["rsr"], q["bn"], q["xor_"])

        @block.tensor
        def _(pe):
            def products(c):
                pe.wait_ge(q["taken"], c + 2)
                pe.wait_ge(q["yr"], c)
                for s in range(SUB):
                    nc.tensor.matmul(y_ps[:, s, :], sT[:, s * SN:(s + 1) * SN], wf[:], start=True, stop=False)
                    ins = nc.tensor.matmul(y_ps[:, s, :], ones[:], bf[:], start=False, stop=True)
                ins.then_inc(q["y_done"], 1)

            pe.wait_ge(q["w_in"], 32)
            pe.wait_ge(q["cst"], 2)
            pe.wait_ge(parts_in[0], 16)
            sum_all(nc, pe, d, agg, q["summed"], q["taken"], lambda j: pe.wait_ge(parts_in[j], 16), (products,), (4,))


def phase_ident(nc, d):
    with ExitStack() as ctx:
        zeroed = Mem(nc, ctx, "id").sem("zeroed")
        block = ctx.enter_context(nc.Block())

        @block.gpsimd
        def _(pool):
            nc.gpsimd.memset(d["ident"][:], 0.0).then_inc(zeroed, 1)
            pool.wait_ge(zeroed, 1)
            nc.gpsimd.affine_select(out=d["ident"][:], in_=d["ident"][:], compare_op=ALU.not_equal, fill=1.0,
                                    base=0, pattern=[[-1, P]], channel_multiplier=1)


def make(nc, x, src, dst, edge_attr, w, out):
    with ExitStack() as ctx:
        m = Mem(nc, ctx, "g")
        d = {}

        def dram(name, shape, dt=F32):
            d[name] = nc.dram_tensor(name, shape, dt).ap()

        dram("wins", [1, NWIN], I32)
        dram("ptab", [ROWS, 3 * D], BF16)
        dram("xT", [D, ROWS])
        dram("hT", [D, ROWS])
        dram("xn", [ROWS, D])
        dram("inv", [P, ROWS])
        dram("ind", [P, ROWS])
        dram("se", [NPAD, D])
        dram("meT", [D, ROWS])
        dram("heads", [ROWS, D])
        dram("score", [ROWS, 2 * HEADS])
        dram("aj", [3, HEADS, NPAD], BF16)
        d["AT"] = m.sb("AT", [P, KB, NPAD], BF16)
        d["ident"] = m.sb("ident", [P, P])
        phase_ident(nc, d)
        with ExitStack() as edges:
            mem = Mem(nc, edges, "gi")
            d["dsts"] = mem.sb("dsts", [P, NG, GT])
            for name in ("windows", "lows", "codes"):
                d[name] = [mem.sb(f"{name}{j}", [P, NG]) for j in range(GT)]
            phase_index(nc, d, src, dst)
            phase_build(nc, d, edge_attr)
        d["parts"] = m.sb("parts", [P, KB, 3, D], BF16)
        with ExitStack() as rows:
            mem = Mem(nc, rows, "gr")
            d["again"] = mem.sb("again", [P, KB, TOPK])
            d["more"] = mem.sb("more", [P, KB, TOPK])
            with ExitStack() as search:
                repeats = Repeats(nc, d, Mem(nc, search, "rp"))
                phase_start(nc, d, x, repeats)
                phase_conv1(nc, d, w, repeats)
                phase_conv2(nc, d, w, repeats)
            phase_attention(nc, d)
        phase_gru(nc, d, w, 0, False)
        phase_gru(nc, d, w, 1, True)
        phase_hop1(nc, d)
        phase_hop2(nc, d, w, out)


def kernel(**inputs):
    import numpy as _np
    import concourse.bacc as _bacc
    from concourse import mybir as _mybir
    from concourse.bass_utils import run_bass_kernel_spmd as _run

    nc = _bacc.Bacc("TRN2", target_bir_lowering=False, num_devices=1)
    arrays, aps = {}, {}
    for name, a in inputs.items():
        a = _np.asarray(a)
        if "W_msg" in name or "Wih" in name or "Whh" in name:
            a = a.T
        a = _np.ascontiguousarray(a)
        arrays[f"in_{name}"] = a
        aps[name] = nc.dram_tensor(f"in_{name}", a.shape, _mybir.dt.from_np(a.dtype), kind="ExternalInput").ap()
    out = nc.dram_tensor("out_0", (N, D), _mybir.dt.float32, kind="ExternalOutput").ap()
    x, src, dst, ea = (aps.pop(k) for k in ("x", "src", "dst", "edge_attr_128"))
    make(nc, x, src, dst, ea, aps, out)
    r = _run(nc, [arrays], core_ids=[0])
    return r.results[0]["out_0"]
```

```python
from contextlib import ExitStack

import concourse.bass as bass
from concourse import mybir

F32 = mybir.dt.float32
BF16 = mybir.dt.bfloat16
I32 = mybir.dt.int32
I16 = mybir.dt.int16
U32 = mybir.dt.uint32
ALU = mybir.AluOpType
ACT = mybir.ActivationFunctionType
AX = mybir.AxisListType

P = 128
N = 3125
E = 50000
D = 128
WIN = 32
NWIN = -(-N // WIN)
NPAD = NWIN * WIN
KB = -(-N // P)
ROWS = KB * P
GT = 2
GE = GT * P
NG = -(-E // GE)
NQ = NG // 2
NT = NG * GT
TAIL = E - (NG - 1) * GE
SHIFT = GE - TAIL
PADW = 4095
NC = 7
CH = NPAD // NC
HEAD = (NC - 1) * CH // P
SUB = 4
SN = CH // SUB
HEADS = 4
HC = D // HEADS
TOPK = 8
MOST_EXACT = 256
SRING = 8


class Mem:

    def __init__(self, nc, ctx, phase):
        self.nc, self.ctx, self.phase, self.sems = nc, ctx, phase, []
        ctx.callback(self.clear)

    def clear(self):
        if self.sems:
            self.nc.clear_and_free_semaphores(self.sems)
            self.nc.all_engine_barrier()

    def sb(self, name, shape, dt=F32):
        return self.ctx.enter_context(self.nc.sbuf_tensor(f"{self.phase}_{name}", shape, dt))

    def ps(self, name, shape, dt=F32):
        return self.ctx.enter_context(self.nc.psum_tensor(f"{self.phase}_{name}", shape, dt))

    def sem(self, name):
        self.sems.append(self.nc.alloc_semaphore(f"{self.phase}_{name}"))
        return self.sems[-1]


def phase_index(nc, d, src, dst):
    with ExitStack() as ctx:
        m = Mem(nc, ctx, "ix")
        ids = m.sb("ids", [NQ, 2, 512], I32)
        part = m.sb("part", [NQ, 4, 512], I32)
        partf = m.sb("partf", [NQ, 4, 512])
        local = m.sb("local", [NQ, 512], I32)
        gm = m.sb("gm", [NQ, 4])
        spread = m.sb("spread", [NQ, 4, NQ])
        first = m.sb("first", [NQ, NQ, 2])
        last = m.sb("last", [NQ, NQ, 2])
        wcol = m.sb("wcol", [NQ, 1])
        ones = m.sb("ones", [NQ, NQ])
        a = m.sb("a", [NQ, NQ, 2])
        b = m.sb("b", [NQ, NQ, 2])
        c = m.sb("c", [NQ, NQ, 2])
        tab = m.sb("tab", [NQ, 8])
        tabi = m.sb("tabi", [NQ, 1], I32)
        cols_ps = m.ps("cols_ps", [P, 4, 512])
        row_ps = m.ps("row_ps", [NQ, 4, NQ])
        padded, loaded, consts, v, floats, bounds, tp, row, done, stored = (m.sem(n) for n in (
            "padded", "loaded", "consts", "v", "floats", "bounds", "tp", "row", "done", "stored"))
        block = ctx.enter_context(nc.Block())
        full = NQ - 1

        @block.sync
        def _(sp):
            sp.wait_ge(padded, 2)
            for n, ap in ((0, src), (1, dst)):
                sp.dma_start(ids[0:full, n, :], ap[0:full * 512].rearrange("(q e) -> q e", e=512)).then_inc(loaded, 16)
                sp.dma_start(ids[full:NQ, n, 0:GE], ap[full * 512:full * 512 + GE].rearrange("(q e) -> q e", q=1)).then_inc(loaded, 16)
                sp.dma_start(ids[full:NQ, n, GE + SHIFT:512], ap[E - TAIL:E].rearrange("(q e) -> q e", q=1)).then_inc(loaded, 16)
            sp.wait_ge(done, 1)
            sp.dma_start(d["wins"].rearrange("a w -> w a"), tabi[:]).then_inc(stored, 16)
            sp.wait_ge(stored, 16)

        @block.gpsimd
        def _(pool):
            nc.gpsimd.memset(ids[:, 0, :], 0).then_inc(padded, 1)
            nc.gpsimd.memset(ids[:, 1, :], PADW).then_inc(padded, 1)
            nc.gpsimd.iota(first[:], [[-2, NQ], [-1, 2]], base=NG, channel_multiplier=0,
                           allow_small_or_imprecise_dtypes=True).then_inc(consts, 1)
            nc.gpsimd.iota(last[:], [[2, NQ], [1, 2]], base=1, channel_multiplier=0,
                           allow_small_or_imprecise_dtypes=True).then_inc(consts, 1)
            nc.gpsimd.iota(wcol[:], [[0, 1]], base=0, channel_multiplier=1,
                           allow_small_or_imprecise_dtypes=True).then_inc(consts, 1)
            nc.gpsimd.memset(ones[:], 1.0).then_inc(consts, 1)

        @block.vector
        def _(dve):
            steps = [0]

            def step(ins):
                steps[0] += 1
                ins.then_inc(v, 1)
                dve.wait_ge(v, steps[0])

            dve.wait_ge(loaded, 96)
            nc.vector.tensor_scalar(part[:, 1, :], ids[:, 1, :], 5, None, ALU.logical_shift_right)
            nc.vector.tensor_scalar(local[:], ids[:, 1, :], WIN - 1, None, ALU.bitwise_and)
            nc.vector.tensor_scalar(part[:, 2, :], ids[:, 0, :], P - 1, None, ALU.bitwise_and)
            nc.vector.tensor_copy(part[:, 0, :], ids[:, 1, :])
            step(nc.vector.tensor_scalar(part[:, 3, :], ids[:, 0, :], 7, 5, ALU.logical_shift_right,
                                         ALU.logical_shift_left))
            step(nc.vector.tensor_tensor(part[:, 3, :], part[:, 3, :], local[:], ALU.bitwise_or))
            step(nc.vector.tensor_copy(partf[:], part[:]))
            nc.vector.nop().then_inc(floats, 1)
            w = partf[:, 1, :].rearrange("q (g e) -> q g e", g=2)
            nc.vector.tensor_reduce(gm[:, 0:2], w, AX.X, ALU.min)
            step(nc.vector.tensor_reduce(gm[:, 2:4], w, AX.X, ALU.max))
            for n in range(4):
                ins = nc.vector.tensor_scalar(spread[:, n, :], d["ident"][0:NQ, 0:NQ], gm[:, n:n + 1], None, ALU.mult)
            step(ins)
            nc.vector.nop().then_inc(bounds, 1)
            dve.wait_ge(tp, 1)
            for n, to in enumerate((None, d["windows"], d["lows"], d["codes"])):
                for j in range(4):
                    if n == 0:
                        out = d["dsts"][:].rearrange("p (q h) i -> p q h i", h=2)[:, :, j // 2, j % 2]
                    else:
                        out = to[j % 2][:].rearrange("p (q h) -> p q h", h=2)[:, :, j // 2]
                    nc.vector.tensor_copy(out, cols_ps[:, n, j * NQ:(j + 1) * NQ])
            dve.wait_ge(row, 1)
            dve.wait_ge(consts, 4)
            least = row_ps[:, 0:2, :].rearrange("w j q -> w q j")
            most = row_ps[:, 2:4, :].rearrange("w j q -> w q j")
            nc.vector.tensor_scalar(a[:], least, wcol[:, 0:1], None, ALU.is_le)
            step(nc.vector.tensor_scalar(b[:], most, wcol[:, 0:1], None, ALU.is_ge))
            step(nc.vector.tensor_tensor(c[:], a[:], b[:], ALU.mult))
            nc.vector.tensor_tensor(a[:], c[:], first[:], ALU.mult)
            step(nc.vector.tensor_tensor(b[:], c[:], last[:], ALU.mult))
            nc.vector.tensor_reduce(tab[:, 4:5], a[:], AX.XY, ALU.max)
            step(nc.vector.tensor_reduce(tab[:, 5:6], b[:], AX.XY, ALU.max))
            step(nc.vector.tensor_scalar(tab[:, 6:7], tab[:, 4:5], -1.0, float(NG), ALU.mult, ALU.add))
            step(nc.vector.tensor_scalar(tab[:, 0:1], tab[:, 6:7], float(NG - 1), None, ALU.min))
            step(nc.vector.tensor_scalar(tab[:, 6:7], tab[:, 0:1], 1.0, None, ALU.add))
            step(nc.vector.tensor_tensor(tab[:, 1:2], tab[:, 6:7], tab[:, 5:6], ALU.max))
            step(nc.vector.scalar_tensor_tensor(out=tab[:, 3:4], in0=tab[:, 1:2], scalar=256.0, in1=tab[:, 0:1],
                                                op0=ALU.mult, op1=ALU.add))
            step(nc.vector.tensor_copy(tabi[:], tab[:, 3:4]))
            nc.vector.nop().then_inc(done, 1)

        @block.tensor
        def _(pe):
            pe.wait_ge(floats, 1)
            for n in range(4):
                for j in range(4):
                    ins = nc.tensor.transpose(cols_ps[:, n, j * NQ:(j + 1) * NQ],
                                              partf[:, n, j * P:(j + 1) * P], d["ident"][0:NQ, 0:NQ])
            ins.then_inc(tp, 1)
            pe.wait_ge(bounds, 1)
            pe.wait_ge(consts, 4)
            nc.tensor.matmul(row_ps[:], ones[:], spread[:], start=True, stop=True).then_inc(row, 1)


def bounded(nc, value, most):
    return nc.s_assert_within(value, min_val=0, max_val=most,
                              skip_runtime_bounds_check_because="it follows from the clamped table of windows")


BATCH = 7
HALVES = 2


class Held:

    def __init__(self, m, eng, name, most, value=0):
        self.nc, self.eng, self.most = m.nc, eng, most
        self.reg = eng.alloc_register(f"{m.phase}_{name}")
        m.ctx.callback(lambda: eng.free_register(self.reg))
        self.set(value)

    def set(self, value):
        self.eng.reg_mov(self.reg, value)

    def add(self, value):
        self.eng.reg_add(self.reg, self.reg, value)

    def least(self, value, other):
        self.eng.reg_alu(self.reg, value, other, ALU.min)

    @property
    def value(self):
        return bounded(self.nc, self.eng.snap(self.reg), self.most)


def windows(m, eng, wins, body):
    nc = m.nc
    lo, end = Held(m, eng, "lo", NG - 1), Held(m, eng, "end", NG)
    with eng.Fori(0, NWIN, BATCH * HALVES) as w0:
        for half in range(HALVES):
            first = bounded(nc, eng.snap(w0 + half * BATCH), NWIN - BATCH)
            _, entries = nc.values_load_multi_w_load_instructions(
                wins[:, bass.ds(first, BATCH)], engines=[eng.engine], min_val=0, max_val=256 * NG + NG,
                skip_runtime_bounds_check_because="phase_index clamps the table to the groups there are")
            for i, entry in enumerate(entries):
                lo.set(entry & 255)
                end.set(entry >> 8)
                body(bounded(nc, eng.snap(first + i), NWIN - 1), (half * BATCH + i) % 2, lo.value, end.value)


def phase_build(nc, d, edge_attr):
    with ExitStack() as ctx:
        m = Mem(nc, ctx, "bd")
        codes = m.sb("codes", [P, KB * WIN], I16)
        nodes = m.sb("nodes", [P, NPAD])
        low = m.sb("low", [P, P], I16)
        wins = m.sb("wins", [P, NWIN])
        zero = m.sb("zero", [P, P], BF16)
        zeroc = m.sb("zeroc", [P, 512], BF16)
        inside = [m.sb(f"inside{j}", [P, NG]) for j in range(GT)]
        hot_lo = m.sb("hot_lo", [P, GT, P], BF16)
        hot_hd = m.sb("hot_hd", [P, GT, KB * WIN], BF16)
        hot_d = m.sb("hot_d", [P, GT, WIN])
        ring = m.sb("ring", [P, SRING, GT, D])
        seg = m.sb("seg", [WIN, 2, D])
        cnt_ps = [m.ps(f"cnt_ps{i}", [P, 2, 512]) for i in range(2)]
        seg_ps = [m.ps(f"seg_ps{i}", [WIN, 512]) for i in range(2)]
        consts, dots, attrs, past, past_dve, summed, closed, emptied, ins_ = (
            m.sem(n) for n in ("consts", "dots", "attrs", "past", "past_dve", "summed", "closed", "emptied", "inside"))
        hots, counted, stored = ([m.sem(f"{n}{j}") for j in range(2)] for n in ("hots", "counted", "stored"))
        arrived = [m.sem(f"arrived{i}") for i in range(2)]
        lows, highs, dsts, its = (d[n] for n in ("lows", "codes", "dsts", "windows"))
        MOST = NWIN * NG + 1
        block = ctx.enter_context(nc.Block())

        @block.gpsimd
        def _(pool):
            nc.gpsimd.iota(codes[:], [[1, KB * WIN]], base=0, channel_multiplier=0).then_inc(consts, 1)
            nc.gpsimd.iota(low[:], [[1, P]], base=0, channel_multiplier=0).then_inc(consts, 1)
            nc.gpsimd.iota(wins[:], [[1, NWIN]], base=0, channel_multiplier=0,
                           allow_small_or_imprecise_dtypes=True).then_inc(consts, 1)
            nc.gpsimd.iota(nodes[:], [[1, NPAD]], base=0, channel_multiplier=0,
                           allow_small_or_imprecise_dtypes=True).then_inc(consts, 1)
            nc.gpsimd.memset(zero[:], 0.0).then_inc(consts, 1)
            nc.gpsimd.memset(zeroc[:], 0.0).then_inc(consts, 1)

        @block.sync
        def _(sp):
            n, start, due = Held(m, sp, "n", MOST, 1), Held(m, sp, "start", E - GE), Held(m, sp, "due", 8 * MOST, 8)
            sp.sem_inc(arrived[1], 8)
            sp.sem_inc(arrived[0], 16)

            def body(w, u, lo, end):
                with sp.Fori(lo, end) as g:
                    start.least(g * GE, E - GE)
                    now = n.value
                    slot = bounded(nc, sp.snap(now % SRING), SRING - 1)
                    odd = bounded(nc, sp.snap(now % 2), 1)
                    to = ring[:, bass.ds(slot, 1), :, :].rearrange("p a j f -> p (a j) f")
                    edges = edge_attr[bass.ds(start.value, GE), :].rearrange("(j p) f -> p j f", p=P)
                    arrival = due.value
                    sp.wait_ge(summed, now)
                    waited(sp, past)
                    with sp.If(odd == 1):
                        sp.wait_ge(arrived[1], arrival)
                        waited(sp, attrs)
                        sp.dma_start(to, edges).then_inc(arrived[1], 16)
                    with sp.Else():
                        sp.wait_ge(arrived[0], arrival)
                        waited(sp, attrs)
                        sp.dma_start(to, edges).then_inc(arrived[0], 16)
                    n.add(1)
                    due.add(8)

            windows(m, sp, d["wins"], body)
            sp.wait_ge(arrived[1], (n.value >> 1) * 16 + 8)
            sp.wait_ge(arrived[0], ((n.value + 1) >> 1) * 16)
            sp.sem_inc(attrs, 2)

        @block.vector
        def _(dve):
            dve.wait_ge(consts, 4)
            n = Held(m, dve, "n", MOST, 1)

            def body(w, u, lo, end):
                dve.wait_ge(hots[1], n.value)
                for j in range(GT):
                    nc.vector.tensor_scalar(inside[j][:], its[j][:], wins[:, bass.ds(w, 1)], None, ALU.is_equal).then_inc(ins_, 1)
                dve.wait_ge(ins_, GT * (w + 1))
                waited(dve, past_dve)
                with dve.Fori(lo, end) as g:
                    at, now = bass.ds(g, 1), n.value
                    for j in range(GT):
                        dve.wait_ge(counted[j], now)
                        nc.vector.tensor_scalar(hot_lo[:, j, :], low[:], lows[j][:, at], None, ALU.is_equal)
                        nc.vector.tensor_scalar(hot_hd[:, j, :], codes[:], highs[j][:, at],
                                                inside[j][:, at], ALU.is_equal, ALU.mult).then_inc(hots[j], 1)
                    dve.wait_ge(summed, now + SRING - 1)
                    nc.vector.tensor_tensor(hot_d[:], nodes[:, bass.ds(w * WIN, WIN)].unsqueeze(1).to_broadcast([P, GT, WIN]),
                                            dsts[:, at, :].rearrange("p a j -> p (a j)").unsqueeze(2).to_broadcast([P, GT, WIN]),
                                            ALU.is_equal).then_inc(dots, 1)
                    n.add(1)

            windows(m, dve, d["wins"], body)

        @block.tensor
        def _(pe):
            for j in range(GT):
                pe.sem_inc(counted[j], 1)
            pe.sem_inc(hots[1], 1)
            pe.sem_inc(summed, SRING)
            pe.sem_inc(emptied, 2)
            pe.wait_ge(consts, 6)
            n = Held(m, pe, "n", MOST, 1)

            def body(w, u, lo, end):
                pe.wait_ge(emptied, w + 1)
                nc.tensor.matmul(cnt_ps[u][:, 0, :], zero[:], zeroc[:], start=True, stop=False, skip_group_check=True)
                nc.tensor.matmul(cnt_ps[u][:, 1, 0:KB * WIN - 512], zero[:], zeroc[:, 0:KB * WIN - 512], start=True, stop=False, skip_group_check=True)
                nc.tensor.matmul(seg_ps[u][:, 0:D], zero[:, 0:WIN], zeroc[:, 0:D], start=True, stop=False, skip_group_check=True)
                with pe.Fori(lo, end):
                    now = n.value
                    slot = bounded(nc, pe.snap(now % SRING), SRING - 1)
                    for j in range(GT):
                        pe.wait_ge(hots[j], now + j)
                        nc.tensor.matmul(cnt_ps[u][:, 0, :], hot_lo[:, j, :], hot_hd[:, j, 0:512], start=False, stop=False, skip_group_check=True)
                        nc.tensor.matmul(cnt_ps[u][:, 1, 0:KB * WIN - 512], hot_lo[:, j, :], hot_hd[:, j, 512:], start=False, stop=False, skip_group_check=True).then_inc(counted[j], 1)
                    pe.wait_ge(dots, now)
                    pe.wait_ge(attrs, now + 2)
                    for j in range(GT):
                        attr = ring[:, bass.ds(slot, 1), j, :].rearrange("p a f -> p (a f)")
                        ins = nc.tensor.matmul(seg_ps[u][:, 0:D], hot_d[:, j, :], attr, start=False, stop=True, skip_group_check=True)
                    ins.then_inc(summed, 1)
                    n.add(1)
                nc.tensor.matmul(seg_ps[u][:, 0:D], zero[:, 0:WIN], zeroc[:, 0:D], start=False, stop=True, skip_group_check=True).then_inc(closed, 1)

            windows(m, pe, d["wins"], body)

        @block.scalar
        def _(act):
            def body(w, u):
                act.wait_ge(closed, w + 1)
                act.wait_ge(stored[u], 16 * (w >> 1))
                nc.scalar.activation(d["AT"][:, :, bass.ds(w * WIN, WIN)],
                                     cnt_ps[u][:, :, :].rearrange("p a c -> p (a c)")[:, 0:KB * WIN].rearrange("p (h e) -> p h e", e=WIN),
                                     ACT.Copy, accum_out=d["bound"][:, bass.ds(w, 1)])
                nc.scalar.copy(seg[:, u, :], seg_ps[u][:, 0:D]).then_inc(emptied, 1)
                act.wait_ge(emptied, w + 3)
                act.dma_start(d["se"][bass.ds(w * WIN, WIN), :], seg[:, u, :]).then_inc(stored[u], 16)

            with act.Fori(0, NWIN, 2) as w0:
                for u in range(2):
                    body(bounded(nc, act.snap(w0 + u), NWIN - 1), u)
            for u in range(2):
                act.wait_ge(stored[u], 16 * NWIN // 2)


def to_flag(nc, m, d, name, column, least):
    col, row, flag = m.sb("col", [1, P]), m.sb("row", [1, 1]), m.sb("flag", [1, 1], I32)
    row_ps = m.ps("row_ps", [1, P])
    most, turned, copied, v, stored = (m.sem(n) for n in ("most", "turned", "copied", "v", "stored"))

    def vector(dve, ins):
        ins.then_inc(most, 1)
        dve.wait_ge(turned, 1)
        nc.vector.tensor_copy(col[:], row_ps[:]).then_inc(v, 1)
        dve.wait_ge(v, 1)
        nc.vector.tensor_reduce(row[:], col[:], AX.X, ALU.max).then_inc(v, 1)
        dve.wait_ge(v, 2)
        nc.vector.tensor_scalar(flag[:], row[:], float(least), None, ALU.is_ge).then_inc(copied, 1)

    def tensor(pe):
        pe.wait_ge(most, 1)
        nc.tensor.transpose(row_ps[:], column[:], d["ident"][:]).then_inc(turned, 1)

    def sync(sp):
        sp.wait_ge(copied, 1)
        sp.dma_start(d[name], flag[:]).then_inc(stored, 16)
        sp.wait_ge(stored, 16)

    return vector, tensor, sync


def phase_flag(nc, d):
    with ExitStack() as ctx:
        m = Mem(nc, ctx, "fl")
        most = m.sb("most", [P, 1])
        vector, tensor, sync = to_flag(nc, m, d, "flag", most, MOST_EXACT)
        block = ctx.enter_context(nc.Block())

        @block.vector
        def _(dve):
            vector(dve, nc.vector.tensor_reduce(most[:], d["bound"][:], AX.X, ALU.max))

        @block.tensor
        def _(pe):
            tensor(pe)

        @block.sync
        def _(sp):
            sync(sp)


def flagged(nc, eng, d, name):
    _, (value,) = nc.values_load_multi_w_load_instructions(
        d[name], engines=[eng.engine], min_val=0, max_val=1, skip_runtime_bounds_check_because="it is 0 or 1")
    return bounded(nc, value, 1)


def phase_rest(nc, d):
    with ExitStack() as ctx:
        m = Mem(nc, ctx, "re")
        codes = m.sb("codes", [P, KB * WIN], I16)
        low = m.sb("low", [P, P], I16)
        wins = m.sb("wins", [P, NWIN])
        inside = [m.sb(f"inside{j}", [P, NG]) for j in range(GT)]
        hot_lo = m.sb("hot_lo", [P, P], BF16)
        hot_hd = m.sb("hot_hd", [P, KB * WIN], BF16)
        zero = m.sb("zero", [P, 512], BF16)
        lost = m.sb("lost", [P, KB, WIN], BF16)
        cnt_ps = m.ps("cnt_ps", [P, 2, 512])
        consts, ins_, hots, counted, opened, closed, lost_r, stored, past = (
            m.sem(n) for n in ("consts", "inside", "hots", "counted", "opened", "closed", "lost_r", "stored", "past"))
        MOST = GT * NWIN * NG + 1
        block = ctx.enter_context(nc.Block())

        @block.gpsimd
        def _(pool):
            nc.gpsimd.iota(codes[:], [[1, KB * WIN]], base=0, channel_multiplier=0).then_inc(consts, 1)
            nc.gpsimd.iota(low[:], [[1, P]], base=0, channel_multiplier=0).then_inc(consts, 1)
            nc.gpsimd.iota(wins[:], [[1, NWIN]], base=0, channel_multiplier=0,
                           allow_small_or_imprecise_dtypes=True).then_inc(consts, 1)
            nc.gpsimd.memset(zero[:], 0.0).then_inc(consts, 1)

        @block.vector
        def _(dve):
            dve.wait_ge(consts, 4)
            n = Held(m, dve, "n", MOST, 1)

            def body(w, u, lo, end):
                for j in range(GT):
                    nc.vector.tensor_scalar(inside[j][:], d["windows"][j][:], wins[:, bass.ds(w, 1)], None, ALU.is_equal).then_inc(ins_, 1)
                dve.wait_ge(ins_, GT * (w + 1))
                waited(dve, past)
                with dve.Fori(lo, end) as g:
                    at = bass.ds(g, 1)
                    for j in range(GT):
                        dve.wait_ge(counted, n.value)
                        nc.vector.tensor_scalar(hot_lo[:], low[:], d["lows"][j][:, at], None, ALU.is_equal)
                        nc.vector.tensor_scalar(hot_hd[:], codes[:], d["codes"][j][:, at], inside[j][:, at],
                                                ALU.is_equal, ALU.mult).then_inc(hots, 1)
                        n.add(1)
                dve.wait_ge(closed, w + 1)
                dve.wait_ge(stored, 16 * w)
                nc.vector.tensor_tensor(lost[:], cnt_ps[:].rearrange("p a c -> p (a c)")[:, 0:KB * WIN].rearrange("p (h e) -> p h e", e=WIN),
                                        d["AT"][:, :, bass.ds(w * WIN, WIN)], ALU.subtract).then_inc(lost_r, 1)

            with dve.If(flagged(nc, dve, d, "flag") == 1):
                windows(m, dve, d["wins"], body)

        @block.tensor
        def _(pe):
            pe.wait_ge(consts, 4)
            pe.sem_inc(counted, 1)
            n = Held(m, pe, "n", MOST, 1)

            def body(w, u, lo, end):
                pe.wait_ge(lost_r, w)
                parts = ((0, 512), (512, KB * WIN))
                for a, (i, j) in enumerate(parts):
                    nc.tensor.matmul(cnt_ps[:, a, 0:j - i], zero[:, 0:P], zero[:, 0:j - i], start=True, stop=False, skip_group_check=True)
                with pe.Fori(lo, end):
                    for _ in range(GT):
                        pe.wait_ge(hots, n.value)
                        for a, (i, j) in enumerate(parts):
                            ins = nc.tensor.matmul(cnt_ps[:, a, 0:j - i], hot_lo[:], hot_hd[:, i:j], start=False, stop=False, skip_group_check=True)
                        ins.then_inc(counted, 1)
                        n.add(1)
                for a, (i, j) in enumerate(parts):
                    ins = nc.tensor.matmul(cnt_ps[:, a, 0:j - i], zero[:, 0:P], zero[:, 0:j - i], start=False, stop=True, skip_group_check=True)
                ins.then_inc(closed, 1)

            with pe.If(flagged(nc, pe, d, "flag") == 1):
                windows(m, pe, d["wins"], body)

        @block.sync
        def _(sp):
            with sp.If(flagged(nc, sp, d, "flag") == 1):
                with sp.Fori(0, NWIN) as w:
                    sp.wait_ge(lost_r, w + 1)
                    waited(sp, past)
                    sp.dma_start(d["AR"][:, :, bass.ds(w * WIN, WIN)], lost[:]).then_inc(stored, 16)
                sp.wait_ge(stored, 16 * NWIN)


class Rest:

    def __init__(self, nc, d, m):
        self.nc, self.d = nc, d
        self.rows = m.sb("rest_rows", [P, CH], BF16)
        self.loaded, self.used = m.sem("rest_loaded"), m.sem("rest_used")
        self.past = m.sem("rest_past")

    def load(self, pool):
        with pool.If(flagged(self.nc, pool, self.d, "flag") == 1):
            with pool.Fori(0, NC) as c:
                with pool.Fori(0, KB) as k:
                    pool.wait_ge(self.used, c * KB + k)
                    waited(pool, self.past)
                    pool.dma_start(self.rows[:], self.d["AR"][:, bass.ds(k, 1), bass.ds(c * CH, CH)].rearrange("p a n -> p (a n)")
                                   ).then_inc(self.loaded, 16)

    def start(self, pe):
        self.flag = flagged(self.nc, pe, self.d, "flag")

    def add(self, pe, out, c, left):
        with pe.If(self.flag == 1):
            with pe.Fori(0, KB) as k:
                pe.wait_ge(self.loaded, 16 * (c * KB + k) + 16)
                for part in range(len(left)):
                    ins = self.nc.tensor.matmul(out, left[part](k), self.rows[:], start=False, stop=False, skip_group_check=True)
                ins.then_inc(self.used, 1)


class Repeats:

    PARTS = 4
    WIDE = NPAD // PARTS
    STEPS = 10

    def __init__(self, nc, d, mem):
        self.nc, self.d = nc, d
        self.dest = mem.sb("dest", [P, NPAD], I16)
        self.key = mem.sb("key", [P, 2, self.WIDE])
        self.best = mem.sb("best", [P, self.PARTS, TOPK])
        self.eight = mem.sb("eight", [P, TOPK])

    def block(self, dve, sem, past, i, number):
        V, W = self.nc.vector, self.WIDE

        def after(k):
            dve.wait_ge(sem, self.STEPS * number + k)

        def keys(part):
            V.scalar_tensor_tensor(out=self.key[:, part % 2, :],
                                   in0=self.d["AT"][:, bass.ds(i, 1), part * W:(part + 1) * W].rearrange("p a n -> p (a n)"),
                                   scalar=4096.0, in1=self.dest[:, part * W:(part + 1) * W],
                                   op0=ALU.mult, op1=ALU.subtract).then_inc(sem, 1)

        def greatest(part):
            waited(dve, past)
            V.max(self.best[:, part, :], self.key[:, part % 2, :]).then_inc(sem, 1)

        after(0)
        keys(0)
        keys(1)
        after(1)
        greatest(0)
        after(2)
        greatest(1)
        after(3)
        keys(2)
        after(4)
        keys(3)
        after(5)
        greatest(2)
        after(6)
        greatest(3)
        after(8)
        waited(dve, past)
        V.max(self.eight[:], self.best[:].rearrange("p a e -> p (a e)")).then_inc(sem, 1)
        after(9)
        V.tensor_copy(self.d["again"][:, bass.ds(i, 1), :].rearrange("p a e -> p (a e)"), self.eight[:]).then_inc(sem, 1)

    def finish(self, dve, sem, number):
        V = self.nc.vector
        done = self.STEPS * number
        a, b = (self.key[:, k, 0:KB * TOPK].bitcast(I32) for k in range(2))
        again, more = (self.d[n][:].rearrange("p k e -> p (k e)") for n in ("again", "more"))
        dve.wait_ge(sem, done)
        V.tensor_scalar(a, again, -1.0, 0.0, ALU.add, ALU.max).then_inc(sem, 1)
        dve.wait_ge(sem, done + 1)
        V.tensor_scalar(b, a, 4095, None, ALU.bitwise_and).then_inc(sem, 1)
        V.tensor_scalar(a, a, 12, None, ALU.logical_shift_right).then_inc(sem, 1)
        dve.wait_ge(sem, done + 3)
        V.tensor_copy(more, a)
        V.tensor_scalar(again, b, -1.0, 4095.0, ALU.mult, ALU.add)


def phase_start(nc, d, x, repeats):
    PB = 5
    NP = KB // PB
    with ExitStack() as ctx:
        m = Mem(nc, ctx, "st")
        xb = m.sb("xb", [P, 2, PB * D])
        rest = m.sb("rest", [P, PB * D])
        xtb = m.sb("xtb", [P, PB * P])
        ones = m.sb("ones", [P, P], BF16)
        zrows = m.sb("zrows", [ROWS - NPAD, 3 * D], BF16)
        zrowf = m.sb("zrowf", [ROWS - NPAD, D])
        least1 = m.sb("least1", [P, CH])
        inv = m.sb("inv", [P, CH])
        ind = m.sb("ind", [P, CH])
        mean_e = m.sb("mean_e", [P, CH])
        sum_e = m.sb("sum_e", [SN, SUB, D])
        share = Rest(nc, d, m)
        tp_ps = m.ps("tp_ps", [P, PB, P])
        deg_ps = m.ps("deg_ps", [P, 2, 512])
        se_ps = m.ps("se_ps", [P, 512])
        consts, zeroed, x_in, hi, r, mid, lo, tp, xt, xt_out, deg, inv_r, ind_r, me_r, i_out, n_out, e_out, z_out, m1, s_in, se_t, past, dest_r, rep, rep_past = (
            m.sem(n) for n in ("consts", "zeroed", "x_in", "hi", "r", "mid", "lo", "tp", "xt", "xt_out", "deg",
                               "inv_r", "ind_r", "me_r", "i_out", "n_out", "e_out", "z_out", "m1", "s_in", "se_t", "past", "dest_r", "rep", "rep_past"))
        parts = d["parts"]
        x_in = [x_in, m.sem("x_in1")]

        def piece_in(i):
            return x_in[i % 2], 16 * (i // 2 + 1) + 16 * (i == NP - 1)

        def in_degrees(c):
            return deg_ps[:, bass.ds(c & 1, 1), 0:CH].rearrange("p a n -> p (a n)")

        block = ctx.enter_context(nc.Block())

        @block.gpsimd
        def _(pool):
            nc.gpsimd.iota(repeats.dest[:], [[1, NPAD]], base=0, channel_multiplier=0).then_inc(dest_r, 1)
            nc.gpsimd.memset(ones[:], 1.0).then_inc(consts, 1)
            nc.gpsimd.memset(zrows[:], 0.0).then_inc(consts, 1)
            nc.gpsimd.memset(zrowf[:], 0.0).then_inc(consts, 1)
            nc.gpsimd.memset(xb[:, 0, :], 0.0).then_inc(zeroed, 1)
            share.load(pool)

        @block.sync
        def _(sp):
            for i in range(NP):
                if i == 0:
                    sp.wait_ge(zeroed, 1)
                if i >= 2:
                    sp.wait_ge(lo, i - 1)
                    sp.wait_ge(tp, i - 1)
                rows = min(N, (i + 1) * PB * P) - i * PB * P
                full = rows // P
                sp.dma_start(xb[:, i % 2, 0:full * D].rearrange("p (k f) -> p k f", f=D),
                             x[i * PB * P:i * PB * P + full * P, :].rearrange("(k p) f -> p k f", p=P)).then_inc(x_in[i % 2], 16)
                if full < PB:
                    sp.dma_start(xb[0:rows - full * P, i % 2, full * D:], x[i * PB * P + full * P:N, :]).then_inc(x_in[i % 2], 16)
                if i >= 1:
                    sp.wait_ge(xt, i)
                    sp.dma_start(d["xT"][:, (i - 1) * PB * P:i * PB * P], xtb[:]).then_inc(xt_out, 16)
            sp.wait_ge(xt, NP)
            sp.dma_start(d["xT"][:, (NP - 1) * PB * P:], xtb[:]).then_inc(xt_out, 16)
            sp.wait_ge(consts, 3)
            sp.dma_start(d["ptab"][NPAD:ROWS, :], zrows[:]).then_inc(z_out, 16)
            sp.dma_start(d["xn"][NPAD:ROWS, :], zrowf[:]).then_inc(z_out, 16)
            sp.dma_start(d["heads"][NPAD:ROWS, :], zrowf[:]).then_inc(z_out, 16)
            sp.dma_start(d["score"][NPAD:ROWS, :], zrowf[:, 0:2 * HEADS]).then_inc(z_out, 16)
            sp.dma_start(sum_e[:], rows_of(d["se"], 0)).then_inc(s_in, 16)

            def store(c):
                sp.wait_ge(inv_r, c + 1)
                waited(sp, past)
                sp.dma_start(d["inv"][:, bass.ds(c * CH, CH)], inv[:]).then_inc(i_out, 16)
                sp.wait_ge(ind_r, c + 2)
                sp.dma_start(d["ind"][:, bass.ds(c * CH, CH)], ind[:]).then_inc(n_out, 16)
                sp.wait_ge(me_r, c + 1)
                sp.dma_start(d["meT"][:, bass.ds(c * CH, CH)], mean_e[:]).then_inc(e_out, 16)

            with sp.Fori(0, NC - 1) as c:
                sp.wait_ge(se_t, c + 1)
                sp.dma_start(sum_e[:], rows_of(d["se"], c + 1)).then_inc(s_in, 16)
                store(c)
            store(NC - 1)
            for q, n in ((xt_out, NP), (z_out, 4), (i_out, NC), (n_out, NC), (e_out, NC)):
                sp.wait_ge(q, 16 * n)

        @block.scalar
        def _(act):
            for i in range(NP):
                piece = parts[:, i * PB:(i + 1) * PB, :, :]
                src = xb[:, i % 2, :].rearrange("p (k f) -> p k f", f=D)
                act.wait_ge(*piece_in(i))
                nc.scalar.copy(piece[:, :, 0, :], src).then_inc(hi, 1)
                act.wait_ge(tp, i + 1)
                if i:
                    act.wait_ge(xt_out, 16 * i)
                nc.scalar.copy(xtb[:], tp_ps[:].rearrange("p k n -> p (k n)")).then_inc(xt, 1)
                act.wait_ge(r, i + 1)
                nc.scalar.copy(piece[:, :, 1, :], rest[:].rearrange("p (k f) -> p k f", f=D)).then_inc(mid, 1)

        @block.vector
        def _(dve):
            dve.wait_ge(dest_r, 1)
            repeats.block(dve, rep, rep_past, 0, 0)
            for i in range(NP):
                piece = parts[:, i * PB:(i + 1) * PB, :, :]
                r3 = rest[:].rearrange("p (k f) -> p k f", f=D)
                dve.wait_ge(hi, i + 1)
                if i:
                    dve.wait_ge(lo, i)
                nc.vector.tensor_tensor(r3, xb[:, i % 2, :].rearrange("p (k f) -> p k f", f=D), piece[:, :, 0, :],
                                        ALU.subtract).then_inc(r, 1)
                dve.wait_ge(mid, i + 1)
                nc.vector.tensor_tensor(piece[:, :, 2, :], r3, piece[:, :, 1, :], ALU.subtract).then_inc(lo, 1)
            with dve.Fori(0, NC) as c:
                dve.wait_ge(deg, c + 1)
                nc.vector.tensor_scalar(least1[:], in_degrees(c), 1.0, None, ALU.max).then_inc(m1, 1)
                dve.wait_ge(n_out, 16 * c)
                nc.vector.tensor_scalar(ind[:], in_degrees(c), 1.0, None, ALU.min).then_inc(ind_r, 1)
                dve.wait_ge(m1, c + 1)
                dve.wait_ge(i_out, 16 * c)
                nc.vector.reciprocal(inv[:], least1[:]).then_inc(inv_r, 1)
                dve.wait_ge(inv_r, c + 1)
                dve.wait_ge(e_out, 16 * c)
                dve.wait_ge(se_t, c + 1)
                nc.vector.tensor_tensor(mean_e[:], se_ps[:, 0:CH], inv[:], ALU.mult).then_inc(me_r, 1)

        @block.tensor
        def _(pe):
            for i in range(NP):
                pe.wait_ge(*piece_in(i))
                if i:
                    pe.wait_ge(xt, i)
                for k in range(PB):
                    ins = nc.tensor.transpose(tp_ps[:, k, :], xb[:, i % 2, k * D:(k + 1) * D], d["ident"][:])
                ins.then_inc(tp, 1)
            pe.wait_ge(consts, 1)
            pe.sem_inc(ind_r, 1)
            share.start(pe)
            with pe.Fori(0, NC) as c:
                pe.wait_ge(ind_r, c)
                for k in range(KB):
                    ins = nc.tensor.matmul(in_degrees(c), ones[:], d["AT"][:, k, bass.ds(c * CH, CH)],
                                           start=(k == 0), stop=(k == KB - 1), skip_group_check=True)
                    if k == 0:
                        share.add(pe, in_degrees(c), c, [lambda k: ones[:]])
                ins.then_inc(deg, 1)
                pe.wait_ge(s_in, 16 * (c + 1))
                pe.wait_ge(me_r, c)
                for s in range(SUB):
                    ins = nc.tensor.transpose(se_ps[:, s * SN:(s + 1) * SN], sum_e[:, s, :], d["ident"][0:SN, 0:SN])
                ins.then_inc(se_t, 1)


def sum_blocks(nc, pe, d, out, c, between, rest, blocks):
    for k in blocks:
        for part in range(3):
            ins = nc.tensor.matmul(out, d["parts"][:, k, part, :], d["AT"][:, k, bass.ds(c * CH, CH)],
                                   start=(k == 0 and part == 0), stop=(k == KB - 1 and part == 2),
                                   skip_group_check=True)
        if k in between:
            between[k]()
        if k == KB - 2:
            rest.add(pe, out, c, [lambda k, part=part: d["parts"][:, bass.ds(k, 1), part, :].rearrange("p a f -> p (a f)") for part in range(3)])
    return ins


def bank(d, c, flip):
    return d["agg"][:, bass.ds((c + flip) & 1, 1), 0:CH].rearrange("p a n -> p (a n)")


class Sums:

    def __init__(self, nc, d, m, begun=False, ahead=False, flip=0):
        self.nc, self.d, self.begun, self.ahead, self.flip = nc, d, begun, ahead, flip
        self.rest = Rest(nc, d, m)
        self.parts_in = [m.sem(f"parts_in{j}") for j in range(5)]
        self.last_in = m.sem("last_in")
        self.ahead_in = [m.sem(f"ahead_in{j}") for j in range(3)]

    def bank(self, c):
        return bank(self.d, c, self.flip)

    def load_blocks(self, sp, first, end, sem):
        sp.dma_start(self.d["parts"][:, first:end, :, :].rearrange("p k a f -> p k (a f)"),
                     self.d["ptab"][first * P:end * P, :].rearrange("(k p) f -> p k f", p=P)).then_inc(sem, 16)

    def load(self, sp):
        if not self.begun:
            for j in range(5):
                self.load_blocks(sp, 5 * j, 5 * j + 5, self.parts_in[j])

    def load_ahead(self, sp, summed, stored):
        sp.wait_ge(stored, 16 * (NC - 1))
        sp.wait_ge(summed, NC)
        for j in range(3):
            self.load_blocks(sp, j * HEAD // 3, (j + 1) * HEAD // 3, self.ahead_in[j])

    def load_last(self, sp, stored):
        sp.wait_ge(stored, 16 * NC)
        self.load_blocks(sp, HEAD, KB, self.last_in)
        sp.wait_ge(self.last_in, 16)

    def run(self, pe, summed, taken, wait_parts, steps, at, prepare=lambda: None):
        nc, d = self.nc, self.d

        def chunk(c, between, blocks=range(KB)):
            pe.wait_ge(taken, c)
            sum_blocks(nc, pe, d, self.bank(c), c, between, self.rest, blocks).then_inc(summed, 1)

        def at_blocks(before, places):
            return {k: (lambda s=s: s(before)) for k, s in zip(places, steps)}

        pe.sem_inc(taken, 1)
        self.rest.start(pe)
        first = 1
        if self.begun:
            chunk(0, {}, range(HEAD, KB))
            later = [max(k, 8 + 2 * n) for n, k in enumerate(at)]
            chunk(1, {6: prepare} | at_blocks(0, later))
            first = 2
        elif wait_parts:
            pe.wait_ge(self.parts_in[0], 16)
            chunk(0, {5 * j - 1: (lambda j=j: pe.wait_ge(self.parts_in[j], 16)) for j in range(1, 5)} | {KB - 3: prepare})
        else:
            chunk(0, {KB - 3: prepare})
        with pe.Fori(first, NC) as c:
            chunk(c, at_blocks(pe.snap(c - 1), at))
        steps[0](NC - 1)
        if not self.ahead:
            for s in steps[1:]:
                s(NC - 1)
            return
        pe.wait_ge(taken, NC)
        assert HEAD // 3 == 7
        later = {6: lambda: pe.wait_ge(self.ahead_in[1], 16), 13: lambda: pe.wait_ge(self.ahead_in[2], 16)}
        for n, s in enumerate(steps[1:]):
            later[14 + 3 * n] = lambda s=s: s(NC - 1)
        pe.wait_ge(self.ahead_in[0], 16)
        sum_blocks(nc, pe, d, self.bank(NC), 0, later, self.rest, range(HEAD))


def rows_of(ap, c):
    return ap[bass.ds(c * CH, CH), :].rearrange("(s p) f -> p s f", p=SN)


def phase_conv1(nc, d, w, repeats):
    with ExitStack() as ctx:
        m = Mem(nc, ctx, "c1")
        sT, inv, xT, hT = (m.sb(n, [P, CH]) for n in ("sT", "inv", "xT", "hT"))
        wl, wr = m.sb("wl", [D, D]), m.sb("wr", [D, D])
        vec = m.sb("vec", [D, 8])
        scale, shift, eps = m.sb("scale", [D, 1]), m.sb("shift", [D, 1]), m.sb("eps", [D, 1])
        rest = m.sb("rest", [SN, SUB, D])
        stage = m.sb("stage", [SN, SUB, 3, D], BF16)
        sums = Sums(nc, d, m, ahead=True)
        h_ps = m.ps("h_ps", [P, 512])
        t_ps = m.ps("t_ps", [SN, SUB, D])
        (w_in, cst, sd, v, summed, taken, i_in, x_in, h_done, h_ready, turned, hi, r, mid, lo, h_out, p_out, rep, rep_past) = (
            m.sem(n) for n in ("w_in", "cst", "sd", "v", "summed", "taken", "i_in", "x_in", "h_done", "h_ready",
                               "turned", "hi", "r", "mid", "lo", "h_out", "p_out", "rep", "rep_past"))
        names = ("b1", "bn_gamma", "bn_beta", "bn_mean", "bn_var")
        block = ctx.enter_context(nc.Block())

        @block.sync
        def _(sp):
            sp.dma_start(wl[:], w["L0_gnn_W1_l"]).then_inc(w_in, 16)
            sp.dma_start(wr[:], w["L0_gnn_W1_r"]).then_inc(w_in, 16)
            for n, name in enumerate(names):
                sp.dma_start(vec[:, n:n + 1], w["L0_gnn_" + name].rearrange("(p a) -> p a", a=1)).then_inc(w_in, 16)

            def load(c, wait):
                if wait:
                    sp.wait_ge(taken, c + 1)
                sp.dma_start(inv[:], d["inv"][:, bass.ds(c * CH, CH)]).then_inc(i_in, 16)
                if wait:
                    sp.wait_ge(h_done, c)
                sp.dma_start(xT[:], d["xT"][:, bass.ds(c * CH, CH)]).then_inc(x_in, 16)

            def store(c):
                sp.wait_ge(h_ready, c + 1)
                sp.dma_start(d["hT"][:, bass.ds(c * CH, CH)], hT[:]).then_inc(h_out, 16)
                sp.wait_ge(lo, c + 1)
                sp.dma_start(rows_of(d["ptab"], c), stage[:].rearrange("p s a f -> p s (a f)")).then_inc(p_out, 16)

            load(0, False)
            with sp.Fori(0, NC - 1) as c:
                load(sp.snap(c + 1), True)
                store(c)
            sums.load_ahead(sp, summed, p_out)
            store(NC - 1)
            sp.wait_ge(h_out, 16 * NC)
            sums.load_last(sp, p_out)

        @block.gpsimd
        def _(pool):
            nc.gpsimd.memset(eps[:], 1e-5).then_inc(cst, 1)
            sums.rest.load(pool)

        @block.scalar
        def _(act):
            act.wait_ge(w_in, 16 * 7)
            act.wait_ge(cst, 1)
            nc.scalar.activation(vec[:, 5:6], vec[:, 4:5], ACT.Sqrt, bias=eps[:, 0:1]).then_inc(sd, 1)
            act.wait_ge(v, 4)
            with act.Fori(0, NC) as c:
                act.wait_ge(h_done, c + 1)
                act.wait_ge(h_out, 16 * c)
                act.wait_ge(turned, c)
                nc.scalar.activation(hT[:], h_ps[:, 0:CH], ACT.Relu, bias=shift[:, 0:1], scale=scale[:, 0:1]).then_inc(h_ready, 1)
                split_act(nc, act, t_ps[:], rest, stage, c, turned, r, p_out, hi, mid)

        @block.vector
        def _(dve):
            dve.wait_ge(sd, 1)
            nc.vector.reciprocal(vec[:, 6:7], vec[:, 5:6]).then_inc(v, 1)
            dve.wait_ge(v, 1)
            nc.vector.tensor_tensor(scale[:], vec[:, 1:2], vec[:, 6:7], ALU.mult).then_inc(v, 1)
            nc.vector.tensor_tensor(vec[:, 7:8], vec[:, 0:1], vec[:, 3:4], ALU.subtract)
            dve.wait_ge(v, 2)
            dve.drain()
            nc.vector.scalar_tensor_tensor(out=shift[:], in0=vec[:, 7:8], scalar=scale[:, 0:1], in1=vec[:, 2:3],
                                           op0=ALU.mult, op1=ALU.add).then_inc(v, 2)
            for k in range(2):
                repeats.block(dve, rep, rep_past, k + 1, k)

            def chunk(c, more):
                dve.wait_ge(summed, c + 1)
                dve.wait_ge(i_in, 16 * (c + 1))
                dve.wait_ge(h_done, c)
                nc.vector.tensor_tensor(sT[:], sums.bank(c), inv[:],
                                        ALU.mult).then_inc(taken, 1)
                repeats.block(dve, rep, rep_past, c * 2 + 3, c * 2 + 2)
                split_dve(nc, dve, t_ps[:], rest, stage, c, hi, mid, r, lo)
                if more:
                    repeats.block(dve, rep, rep_past, c * 2 + 4, c * 2 + 3)

            with dve.Fori(0, NC - 1) as c:
                chunk(c, True)
            chunk(NC - 1, False)

        @block.tensor
        def _(pe):
            def hidden(c):
                pe.wait_ge(taken, c + 2)
                pe.wait_ge(x_in, 16 * (c + 1))
                pe.wait_ge(h_ready, c)
                nc.tensor.matmul(h_ps[:, 0:CH], wl[:], sT[:], start=True, stop=False)
                nc.tensor.matmul(h_ps[:, 0:CH], wr[:], xT[:], start=False, stop=True).then_inc(h_done, 1)

            def turn(c):
                pe.wait_ge(h_ready, c + 1)
                pe.wait_ge(r, c)
                for s in range(SUB):
                    ins = nc.tensor.transpose(t_ps[:, s, :], hT[:, s * SN:(s + 1) * SN], d["ident"][:])
                ins.then_inc(turned, 1)

            sums.run(pe, summed, taken, False, (hidden, turn), (4, 10), lambda: pe.wait_ge(w_in, 16 * 7))


def split_act(nc, act, src, rest, stage, c, ready, r, stored, hi, mid):
    act.wait_ge(ready, c + 1)
    act.wait_ge(stored, 16 * c)
    nc.scalar.copy(stage[:, :, 0, :], src).then_inc(hi, 1)
    act.wait_ge(r, c + 1)
    nc.scalar.copy(stage[:, :, 1, :], rest[:]).then_inc(mid, 1)


def split_dve(nc, dve, src, rest, stage, c, hi, mid, r, lo):
    dve.wait_ge(hi, c + 1)
    dve.wait_ge(lo, c)
    nc.vector.tensor_tensor(rest[:], src, stage[:, :, 0, :], ALU.subtract).then_inc(r, 1)
    dve.wait_ge(mid, c + 1)
    nc.vector.tensor_tensor(stage[:, :, 2, :], rest[:], stage[:, :, 1, :], ALU.subtract).then_inc(lo, 1)


def waited(eng, sem):
    eng.sem_inc(sem, 1)


def norm_dve(nc, dve, y, stats, mv, sdev, rstd, out, c, y_ready, mv_ready, sd_ready, rs_ready, bn, out_ready):
    dve.wait_ge(y_ready, c + 1)
    for s in range(SUB):
        ins = nc.vector.bn_stats(stats[:, s, :], y[:, s, :])
    ins.then_inc(bn, 1)
    dve.wait_ge(bn, 2 * c + 1)
    waited(dve, bn)
    for s in range(SUB):
        ins = nc.vector.bn_aggr(mv[:, s, :], stats[:, s, :])
    ins.then_inc(mv_ready, 1)
    dve.wait_ge(sd_ready, c + 1)
    nc.vector.reciprocal(rstd[:], sdev[:]).then_inc(rs_ready, 1)
    dve.wait_ge(rs_ready, c + 1)
    for s in range(SUB):
        ins = nc.vector.tensor_scalar(out[:, s, :], y[:, s, :], mv[:, s, 0:1], rstd[:, s:s + 1], ALU.subtract, ALU.mult)
    ins.then_inc(out_ready, 1)


def phase_conv2(nc, d, w, repeats):
    with ExitStack() as ctx:
        m = Mem(nc, ctx, "c2")
        sT, inv, hT, xT, xtn = (m.sb(n, [P, CH]) for n in ("sT", "inv", "hT", "xT", "xtn"))
        wl, wr, wg, wgT = (m.sb(n, [D, D]) for n in ("wl", "wr", "wg", "wgT"))
        att = m.sb("att", [D, 2 * HEADS])
        wa = m.sb("wa", [D, 2 * HEADS])
        b2 = m.sb("b2", [1, D])
        ones = m.sb("ones", [1, SN])
        eps = m.sb("eps", [P, 1])
        stats, mv = m.sb("stats", [SN, SUB, 6]), m.sb("mv", [SN, SUB, 2])
        sdev, rstd = m.sb("sdev", [SN, SUB]), m.sb("rstd", [SN, SUB])
        xn = m.sb("xn", [SN, SUB, D])
        gb = m.sb("gb", [SN, SUB, D])
        sc = m.sb("sc", [SN, SUB, 2 * HEADS])
        ajb = m.sb("ajb", [HEADS, 3, CH], BF16)
        ajr = m.sb("ajr", [HEADS, CH])
        sums = Sums(nc, d, m, begun=True, flip=1)
        y_ps = m.ps("y_ps", [SN, SUB, D])
        x_ps = m.ps("x_ps", [P, 512])
        g_ps = m.ps("g_ps", [P, SUB, D])
        sc_ps = m.ps("sc_ps", [P, SUB, 128])
        aj_ps = m.ps("aj_ps", [HEADS, 512])
        names = ("w_in", "cst", "wt", "wtc", "wa_r", "wa_c", "summed", "taken", "i_in", "h_in", "x_in", "y_done", "bn", "mvr",
                 "sdr", "rsr", "xnr", "turned", "xtr", "proj", "gr", "scr", "aj_hi", "aj_r", "aj_mid", "aj_lo",
                 "xt_out", "xn_out", "g_out", "sc_out", "aj_out", "past", "rep", "rep_past")
        q = {n: m.sem(n) for n in names}
        block = ctx.enter_context(nc.Block())

        @block.sync
        def _(sp):
            sums.load(sp)
            for t, name in ((wl, "L0_gnn_W2_l"), (wr, "L0_gnn_W2_r"), (wg, "L1_gnn_W")):
                sp.dma_start(t[:], w[name]).then_inc(q["w_in"], 16)
            sp.dma_start(b2[:], w["L0_gnn_b2"].rearrange("(a f) -> a f", a=1)).then_inc(q["w_in"], 16)
            sp.wait_ge(q["cst"], 1)
            for h in range(HEADS):
                rows = slice(h * HC, (h + 1) * HC)
                for half in range(2):
                    sp.dma_start(att[rows, half * HEADS + h:half * HEADS + h + 1],
                                 w["L1_gnn_att"][h:h + 1, (1 - half) * HC:(2 - half) * HC].rearrange("a c -> c a")).then_inc(q["w_in"], 16)

            def load(c, wait):
                cols = bass.ds(c * CH, CH)
                if wait:
                    sp.wait_ge(q["taken"], c + 1)
                sp.dma_start(inv[:], d["inv"][:, cols]).then_inc(q["i_in"], 16)
                if wait:
                    sp.wait_ge(q["y_done"], c)
                sp.dma_start(hT[:], d["hT"][:, cols]).then_inc(q["h_in"], 16)
                sp.dma_start(xT[:], d["xT"][:, cols]).then_inc(q["x_in"], 16)

            def store(c):
                cols = bass.ds(c * CH, CH)
                sp.wait_ge(q["xnr"], c + 1)
                sp.dma_start(rows_of(d["xn"], c), xn[:]).then_inc(q["xn_out"], 16)
                sp.wait_ge(q["xtr"], c + 1)
                waited(sp, q["past"])
                sp.dma_start(d["xT"][:, cols], xtn[:]).then_inc(q["xt_out"], 16)
                sp.wait_ge(q["gr"], c + 1)
                sp.dma_start(rows_of(d["heads"], c), gb[:]).then_inc(q["g_out"], 16)
                sp.wait_ge(q["scr"], c + 1)
                sp.dma_start(rows_of(d["score"], c), sc[:]).then_inc(q["sc_out"], 16)
                sp.wait_ge(q["aj_lo"], c + 1)
                waited(sp, q["past"])
                sp.dma_start(d["aj"][:, :, cols].rearrange("a h n -> h a n"), ajb[:]).then_inc(q["aj_out"], 16)

            load(0, False)
            with sp.Fori(0, NC - 1) as c:
                load(sp.snap(c + 1), True)
                store(c)
            store(NC - 1)
            for n in ("xt_out", "xn_out", "g_out", "sc_out", "aj_out"):
                sp.wait_ge(q[n], 16 * NC)

        @block.gpsimd
        def _(pool):
            nc.gpsimd.memset(att[:], 0.0).then_inc(q["cst"], 1)
            nc.gpsimd.memset(ones[:], 1.0).then_inc(q["cst"], 1)
            nc.gpsimd.memset(eps[:], 1e-5).then_inc(q["cst"], 1)
            sums.rest.load(pool)

        @block.scalar
        def _(act):
            act.wait_ge(q["wt"], 1)
            nc.scalar.copy(wgT[:], g_ps[:, 0, :]).then_inc(q["wtc"], 1)
            act.wait_ge(q["wa_r"], 1)
            nc.scalar.copy(wa[:], sc_ps[:, 0, 0:2 * HEADS]).then_inc(q["wa_c"], 1)
            act.wait_ge(q["cst"], 3)
            with act.Fori(0, NC) as c:
                act.wait_ge(q["mvr"], c + 1)
                nc.scalar.activation(sdev[:], mv[:, :, 1], ACT.Sqrt, bias=eps[0:SN, 0:1]).then_inc(q["sdr"], 1)
                act.wait_ge(q["turned"], c + 1)
                act.wait_ge(q["xt_out"], 16 * c)
                act.wait_ge(q["proj"], c)
                nc.scalar.copy(xtn[:], x_ps[:, 0:CH]).then_inc(q["xtr"], 1)
                act.wait_ge(q["proj"], c + 1)
                act.wait_ge(q["g_out"], 16 * c)
                nc.scalar.copy(gb[:], g_ps[0:SN, :, :]).then_inc(q["gr"], 1)
                act.wait_ge(q["sc_out"], 16 * c)
                nc.scalar.copy(sc[:], sc_ps[0:SN, :, 0:2 * HEADS]).then_inc(q["scr"], 1)
                act.wait_ge(q["aj_out"], 16 * c)
                nc.scalar.copy(ajb[:, 0, :], aj_ps[:, 0:CH]).then_inc(q["aj_hi"], 1)
                act.wait_ge(q["aj_r"], c + 1)
                nc.scalar.copy(ajb[:, 1, :], ajr[:]).then_inc(q["aj_mid"], 1)

        @block.vector
        def _(dve):
            first = 2 + 2 * NC
            for k in range(2):
                repeats.block(dve, q["rep"], q["rep_past"], first + k, k)
            with dve.Fori(0, NC) as c:
                dve.wait_ge(q["summed"], c + 1)
                dve.wait_ge(q["i_in"], 16 * (c + 1))
                dve.wait_ge(q["y_done"], c)
                nc.vector.tensor_tensor(sT[:], sums.bank(c), inv[:],
                                        ALU.mult).then_inc(q["taken"], 1)
                dve.wait_ge(q["xn_out"], 16 * c)
                dve.wait_ge(q["turned"], c)
                norm_dve(nc, dve, y_ps, stats, mv, sdev, rstd, xn, c, q["y_done"], q["mvr"], q["sdr"], q["rsr"], q["bn"], q["xnr"])
                repeats.block(dve, q["rep"], q["rep_past"], c + (first + 2), c + 2)
                dve.wait_ge(q["aj_hi"], c + 1)
                nc.vector.tensor_tensor(ajr[:], aj_ps[:, 0:CH], ajb[:, 0, :], ALU.subtract).then_inc(q["aj_r"], 1)
                dve.wait_ge(q["aj_mid"], c + 1)
                nc.vector.tensor_tensor(ajb[:, 2, :], ajr[:], ajb[:, 1, :], ALU.subtract).then_inc(q["aj_lo"], 1)
            repeats.finish(dve, q["rep"], KB - first)

        @block.tensor
        def _(pe):
            def prepare():
                pe.wait_ge(q["w_in"], 16 * 12)
                nc.tensor.transpose(g_ps[:, 0, :], wg[:], d["ident"][:]).then_inc(q["wt"], 1)
                pe.wait_ge(q["wtc"], 1)
                nc.tensor.matmul(sc_ps[:, 0, 0:2 * HEADS], wgT[:], att[:], start=True, stop=True).then_inc(q["wa_r"], 1)
                pe.wait_ge(q["wa_c"], 1)
                pe.wait_ge(q["cst"], 3)

            def products(c):
                pe.wait_ge(q["taken"], c + 2)
                pe.wait_ge(q["h_in"], 16 * (c + 1))
                pe.wait_ge(q["x_in"], 16 * (c + 1))
                pe.wait_ge(q["xnr"], c)
                for s in range(SUB):
                    n = slice(s * SN, (s + 1) * SN)
                    nc.tensor.matmul(y_ps[:, s, :], xT[:, n], d["ident"][:], start=True, stop=False)
                    nc.tensor.matmul(y_ps[:, s, :], sT[:, n], wl[:], start=False, stop=False)
                    nc.tensor.matmul(y_ps[:, s, :], hT[:, n], wr[:], start=False, stop=False)
                    ins = nc.tensor.matmul(y_ps[:, s, :], ones[:], b2[:], start=False, stop=True)
                ins.then_inc(q["y_done"], 1)

            def turn(c):
                pe.wait_ge(q["xnr"], c + 1)
                pe.wait_ge(q["xtr"], c)
                for s in range(SUB):
                    ins = nc.tensor.transpose(x_ps[:, s * SN:(s + 1) * SN], xn[:, s, :], d["ident"][0:SN, 0:SN])
                ins.then_inc(q["turned"], 1)

            def project(c):
                pe.wait_ge(q["xtr"], c + 1)
                pe.wait_ge(q["aj_r"], c)
                for s in range(SUB):
                    nc.tensor.matmul(g_ps[0:SN, s, :], xtn[:, s * SN:(s + 1) * SN], wg[:], start=True, stop=True)
                for s in range(SUB):
                    nc.tensor.matmul(sc_ps[0:SN, s, 0:2 * HEADS], xtn[:, s * SN:(s + 1) * SN], wa[:], start=True, stop=True)
                nc.tensor.matmul(aj_ps[:, 0:CH], wa[:, 0:HEADS], xtn[:], start=True, stop=True).then_inc(q["proj"], 1)

            sums.run(pe, q["summed"], q["taken"], True,
                    (products, turn, project), (3, 11, 19), prepare)


def phase_many(nc, d):
    with ExitStack() as ctx:
        m = Mem(nc, ctx, "ma")
        eighth, first, most = (m.sb(n, [P, 1]) for n in ("eighth", "first", "most"))
        v = m.sem("steps")
        vector, tensor, sync = to_flag(nc, m, d, "many", most, 1)
        block = ctx.enter_context(nc.Block())

        @block.vector
        def _(dve):
            nc.vector.tensor_reduce(eighth[:], d["more"][:, :, TOPK - 1], AX.X, ALU.max).then_inc(v, 1)
            nc.vector.tensor_reduce(first[:], d["more"][:, :, 0], AX.X, ALU.max).then_inc(v, 1)
            dve.wait_ge(v, 2)
            vector(dve, nc.vector.scalar_tensor_tensor(out=most[:], in0=first[:], scalar=-2047.0, in1=eighth[:],
                                                       op0=ALU.add, op1=ALU.max))

        @block.tensor
        def _(pe):
            tensor(pe)

        @block.sync
        def _(sp):
            sync(sp)


NOEDGE = -1e30
OWN = NPAD
SC = NPAD + 1
LAST = KB - 1


def phase_attention(nc, d):
    K = HEADS * TOPK
    HALF = CH // 2
    with ExitStack() as ctx:
        m = Mem(nc, ctx, "at")
        spare = d["parts"][:].rearrange("p k a f -> p (k a f)").bitcast(F32)
        none = m.sb("none", [P, NPAD], BF16)
        S = [m.sb("S0", [P, SC]), spare[:, 0:SC]]
        G = spare[:, 3200:3200 + K * HC].rearrange("p (k c) -> p k c", c=HC)
        ajp = m.sb("ajp", [3 * HEADS, NPAD], BF16)
        pick = m.sb("pick", [3 * HEADS, HEADS, P], BF16)
        identb = m.sb("identb", [P, P], BF16)
        score = m.sb("score", [P, KB, 2 * HEADS])
        own = m.sb("own", [P, KB])
        headno = m.sb("headno", [P, K])
        within = m.sb("within", [P, K])
        eps, one = m.sb("eps", [P, 1]), m.sb("one", [P, 1])
        column = m.sb("column", [P, HALF], I16)
        first = m.sb("first", [P, 2 * NC])
        shifted, found = (spare[:, 4736 + j * K:4736 + (j + 1) * K] for j in range(2))
        junk = m.ps("junk", [P, 512])
        left = m.sb("left", [P, K])
        top = m.sb("top", [P, K])
        idx = m.sb("idx", [P, K], U32)
        idxf, isown, topc, count, upto, room, take, e, lr, rel, ex, wt, alpha = (
            m.sb(n, [P, K]) for n in ("idxf", "isown", "topc", "count", "upto", "room", "take", "e", "lr", "rel", "ex", "wt", "alpha"))
        node = m.sb("node", [P, K])
        rowno = m.sb("rowno", [P, K], U32)
        same = m.sb("same", [P, K, TOPK])
        den, rden = m.sb("den", [P, HEADS]), m.sb("rden", [P, HEADS])
        o, neg, ex2, y = (spare[:, 4224 + j * D:4224 + (j + 1) * D] for j in range(4))
        xb, xn, rest, xt = (m.sb(n, [P, D]) for n in ("xb", "xn", "rest", "xt"))
        stats, mv, sdev, rstd = m.sb("stats", [P, 6]), m.sb("mv", [P, 2]), m.sb("sdev", [P, 1]), m.sb("rstd", [P, 1])
        stage = m.sb("stage", [P, 3, D], BF16)
        s_ps = [m.ps(f"s_ps{i}", [P, 512]) for i in range(4)]
        t_ps = m.ps("t_ps", [P, 512])
        names = ("cst", "past", "past_sp", "past_pool", "in_", "nmr", "smm", "sev", "mx", "mi", "v", "own_in", "t", "relr", "exr", "rowr0", "rowr1", "gath0", "gath1", "aw0", "aw1", "or_", "negr", "ex2r",
                 "x_in", "yr", "bn", "mvr", "sdr", "rsr", "xnr", "tr", "xtr", "hi", "r", "mid", "lo", "xt_out", "p_out")
        q = {n: m.sem(n) for n in names}
        block = ctx.enter_context(nc.Block())

        def grid(t):
            return t[:].rearrange("p (h k) -> p h k", k=TOPK)

        @block.gpsimd
        def _(pool):
            kw = dict(allow_small_or_imprecise_dtypes=True)
            c = q["cst"]
            nc.gpsimd.iota(own[:], [[P, KB]], base=0, channel_multiplier=1, **kw).then_inc(c, 1)
            nc.gpsimd.iota(headno[:], [[1, HEADS], [0, TOPK]], base=0, channel_multiplier=0, **kw).then_inc(c, 1)
            nc.gpsimd.memset(within[:], 1.0).then_inc(c, 1)
            nc.gpsimd.memset(identb[:], 0.0).then_inc(c, 1)
            nc.gpsimd.memset(pick[:], 1.0).then_inc(c, 1)
            nc.gpsimd.memset(eps[:], 1e-5).then_inc(c, 1)
            nc.gpsimd.memset(one[:], 1.0).then_inc(c, 1)
            nc.gpsimd.iota(left[:], [[0, HEADS], [-1, TOPK]], base=TOPK, channel_multiplier=0, **kw).then_inc(c, 1)
            nc.gpsimd.iota(column[:], [[1, HALF]], base=0, channel_multiplier=0).then_inc(c, 1)
            nc.gpsimd.iota(first[:], [[HALF, 2 * NC]], base=0, channel_multiplier=0, **kw).then_inc(c, 1)
            pool.wait_ge(c, 10)
            nc.gpsimd.memset(grid(within)[:, :, 0:1], 0.0).then_inc(c, 1)
            nc.gpsimd.affine_select(out=identb[:], in_=identb[:], compare_op=ALU.not_equal, fill=NOEDGE, base=0,
                                    pattern=[[-1, P]], channel_multiplier=1).then_inc(c, 1)
            nc.gpsimd.affine_select(out=pick[:], in_=pick[:], compare_op=ALU.is_ge, fill=0.0, base=0,
                                    pattern=[[-3, HEADS], [0, P]], channel_multiplier=1).then_inc(c, 1)
            pool.wait_ge(c, 13)
            nc.gpsimd.affine_select(out=pick[:], in_=pick[:], compare_op=ALU.is_ge, fill=0.0, base=2,
                                    pattern=[[3, HEADS], [0, P]], channel_multiplier=-1).then_inc(c, 1)
            heads = d["heads"].rearrange("n (h c) -> (n h) c", c=HC)
            pool.wait_ge(c, 14)
            with pool.Fori(0, KB) as i:
                for half in range(2):
                    pool.wait_ge(q[f"rowr{half}"], i + 1)
                    pool.wait_ge(q[f"aw{half}"], i)
                    waited(pool, q["past_pool"])
                    for k in range(half * K // 2, (half + 1) * K // 2):
                        nc.gpsimd.indirect_dma_start(G[:, k, :], None, heads, bass.IndirectOffsetOnAxis(
                            ap=rowno[:, k:k + 1], axis=0)).then_inc(q[f"gath{half}"], 16)

        @block.sync
        def _(sp):
            for h in range(HEADS):
                sp.dma_start(ajp[3 * h:3 * h + 3, :], d["aj"][:, h, :]).then_inc(q["in_"], 16)
            sp.dma_start(score[:], d["score"].rearrange("(i p) f -> p i f", p=P)).then_inc(q["in_"], 16)
            sp.dma_start(xb[:], d["xn"][0:P, :]).then_inc(q["x_in"], 16)

            def store(i):
                rows = bass.ds(i * P, P)
                sp.wait_ge(q["lo"], i + 1)
                sp.dma_start(d["ptab"][rows, :], stage[:].rearrange("p a f -> p (a f)")).then_inc(q["p_out"], 16)
                sp.wait_ge(q["xtr"], i + 1)
                waited(sp, q["past_sp"])
                sp.dma_start(d["xT"][:, rows], xt[:]).then_inc(q["xt_out"], 16)

            with sp.Fori(0, KB - 1) as i:
                sp.wait_ge(q["yr"], i + 1)
                sp.dma_start(xb[:], d["xn"][bass.ds((i + 1) * P, P), :]).then_inc(q["x_in"], 16)
                store(i)
            store(KB - 1)
            sp.wait_ge(q["xt_out"], 16 * KB)
            sp.wait_ge(q["p_out"], 16 * KB)

        @block.tensor
        def _(pe):
            pe.sem_inc(q["sev"], 4)
            pe.wait_ge(q["cst"], 14)
            pe.wait_ge(q["in_"], 16 * (HEADS + 1))

            def turn(i):
                pe.wait_ge(q["xnr"], i + 1)
                pe.wait_ge(q["xtr"], i)
                nc.tensor.transpose(t_ps[:, 0:P], xn[:], d["ident"][:]).then_inc(q["tr"], 1)

            def scores(i, then=None):
                pe.wait_ge(q["nmr"], i + 1)
                for h in range(HEADS):
                    for c in range(NC):
                        n = h * NC + c
                        cols = slice(c * CH, (c + 1) * CH)
                        pe.wait_ge(q["sev"], HEADS * NC * i + n + 1)
                        nc.tensor.matmul(s_ps[n % 4][:, 0:CH], identb[:], none[:, cols], start=True, stop=False)
                        nc.tensor.matmul(s_ps[n % 4][:, 0:CH], pick[:, h, :], ajp[:, cols], start=False, stop=True).then_inc(q["smm"], 1)
                    if h == 2 and then is not None:
                        turn(then)

            scores(0)
            scores(1)
            scores(2)
            with pe.Fori(3, KB) as i:
                scores(i, pe.snap(i - 3))
            for i in range(KB - 3, KB):
                turn(i)

        @block.scalar
        def _(act):
            act.wait_ge(q["in_"], 16 * (HEADS + 1))
            act.wait_ge(q["cst"], 14)

            def evacuate(i, h):
                for c in range(NC):
                    n = h * NC + c
                    act.wait_ge(q["smm"], HEADS * NC * i + n + 1)
                    if c == 0:
                        act.wait_ge(q["mi"], HEADS * i + h + 1)
                    nc.scalar.copy(S[h % 2][:, c * CH:(c + 1) * CH], s_ps[n % 4][:, 0:CH]).then_inc(q["sev"], 1)
                nc.scalar.copy(S[h % 2][:, OWN:SC], score[:, bass.ds(i, 1), h:h + 1].rearrange("p a b -> p (a b)")).then_inc(q["own_in"], 1)

            def no_edges(i, wait=True):
                if wait:
                    act.wait_ge(q["smm"], HEADS * NC * i)
                nc.scalar.activation(none[:], d["AT"][:, bass.ds(i, 1), :].rearrange("p a n -> p (a n)"), ACT.Relu,
                                     bias=one[:, 0:1], scale=-1.0).then_inc(q["nmr"], 1)

            def softmax(i):
                act.wait_ge(q["relr"], i + 1)
                nc.scalar.activation(ex[:], rel[:], ACT.Exp).then_inc(q["exr"], 1)

            def elu(i):
                act.wait_ge(q["negr"], i + 1)
                nc.scalar.activation(ex2, neg, ACT.Exp).then_inc(q["ex2r"], 1)

            def deviation(i):
                act.wait_ge(q["mvr"], i + 1)
                nc.scalar.activation(sdev[:], mv[:, 1:2], ACT.Sqrt, bias=eps[:, 0:1]).then_inc(q["sdr"], 1)

            def split_hi(i):
                act.wait_ge(q["xnr"], i + 1)
                act.wait_ge(q["p_out"], 16 * i)
                nc.scalar.copy(stage[:, 0, :], xn[:]).then_inc(q["hi"], 1)

            def split_mid(i):
                act.wait_ge(q["r"], i + 1)
                nc.scalar.copy(stage[:, 1, :], rest[:]).then_inc(q["mid"], 1)

            def turned(i):
                act.wait_ge(q["tr"], i + 1)
                act.wait_ge(q["xt_out"], 16 * i)
                nc.scalar.copy(xt[:], t_ps[:, 0:P]).then_inc(q["xtr"], 1)

            def tile(i, before, old, older, following):
                evacuate(i, 1)
                evacuate(i, 2)
                if old is not None:
                    deviation(old)
                evacuate(i, 3)
                if following is not None:
                    no_edges(following)
                if old is not None:
                    split_hi(old)
                if older is not None:
                    turned(older)
                if old is not None:
                    split_mid(old)
                if following is not None:
                    evacuate(following, 0)
                if before is not None:
                    elu(before)
                softmax(i)

            no_edges(0, False)
            evacuate(0, 0)
            tile(0, None, None, None, 1)
            tile(1, 0, None, None, 2)
            tile(2, 1, 0, None, 3)
            with act.Fori(3, LAST) as i:
                tile(i, act.snap(i - 1), act.snap(i - 2), act.snap(i - 3), act.snap(i + 1))
            tile(LAST, LAST - 1, LAST - 2, LAST - 3, None)
            for i in (LAST - 1, LAST):
                if i == LAST:
                    elu(i)
                deviation(i)
                split_hi(i)
                turned(i - 1)
                split_mid(i)
            turned(LAST)

        @block.vector
        def _(dve):
            dve.sem_inc(q["mi"], 2)
            dve.wait_ge(q["cst"], 14)
            nc.vector.tensor_scalar(own[:], own[:], float(N - 1), float(-OWN), ALU.min, ALU.add).then_inc(q["v"], 1)
            dve.wait_ge(q["in_"], 16 * (HEADS + 1))
            many = flagged(nc, dve, d, "many")
            STEPS = 17

            def greatest(i, h):
                dve.wait_ge(q["sev"], HEADS * NC * i + NC * (h + 1) + 4)
                dve.wait_ge(q["own_in"], HEADS * i + h + 1)
                waited(dve, q["past"])
                nc.vector.max(top[:, h * TOPK:(h + 1) * TOPK], S[h % 2][:] if h % 2 == 0 else S[1]).then_inc(q["mx"], 1)

            def places(i, h):
                dve.wait_ge(q["mx"], HEADS * i + h + 1)
                waited(dve, q["past"])
                nc.vector.max_index(idx[:, h * TOPK:(h + 1) * TOPK], top[:, h * TOPK:(h + 1) * TOPK],
                                    S[h % 2][:] if h % 2 == 0 else S[1]).then_inc(q["mi"], 1)

            def done(i, k, ins):
                ins.then_inc(q["t"], 1)

            def after(i, k):
                dve.wait_ge(q["t"], STEPS * i + k)

            def row_numbers(i, half):
                V = nc.vector
                part = slice(half * K // 2, (half + 1) * K // 2)
                if half == 0:
                    dve.wait_ge(q["mi"], HEADS * i + HEADS + 2)
                    done(i, 1, V.tensor_copy(idxf[:], idx[:]))
                    done(i, 2, V.tensor_scalar(isown[:], idx[:], float(OWN), None, ALU.is_equal))
                    done(i, 3, V.tensor_copy(topc[:], top[:]))
                    after(i, 2)
                    done(i, 4, V.scalar_tensor_tensor(out=node[:], in0=isown[:], scalar=own[:, bass.ds(i, 1)], in1=idxf[:],
                                                      op0=ALU.mult, op1=ALU.add))
                    after(i, 4)
                dve.wait_ge(q[f"gath{half}"], 8 * K * i)
                V.scalar_tensor_tensor(out=rowno[:, part], in0=node[:, part], scalar=float(HEADS), in1=headno[:, part],
                                       op0=ALU.mult, op1=ALU.add).then_inc(q[f"rowr{half}"], 1)

            def recount(i):
                V = nc.vector
                with dve.Fori(0, 2 * NC) as c:
                    edges = d["AT"][:, bass.ds(i, 1), bass.ds(c * HALF, HALF)].rearrange("p a n -> p (a n)")
                    V.tensor_scalar(shifted, idxf[:], first[:, bass.ds(c, 1)], None, ALU.subtract)
                    dve.drain()
                    with dve.Fori(0, K) as k:
                        V.scalar_tensor_tensor(out=junk[:, 0:HALF], in0=column[:], scalar=shifted[:, bass.ds(k, 1)], in1=edges,
                                               op0=ALU.is_equal, op1=ALU.mult)
                        dve.drain()
                        V.tensor_reduce(found[:, bass.ds(k, 1)], junk[:, 0:HALF], AX.X, ALU.add)
                        dve.drain()
                    with dve.If(c == 0):
                        V.tensor_scalar(count[:], found, -1.0, None, ALU.add)
                    with dve.Else():
                        V.tensor_tensor(count[:], count[:], found, ALU.add)
                    dve.drain()
                V.tensor_scalar(count[:], count[:], 0.0, None, ALU.max)
                dve.drain()

            def weights(i):
                V = nc.vector
                again = d["again"][:, bass.ds(i, 1), :].to_broadcast([P, K, TOPK])
                more = d["more"][:, bass.ds(i, 1), :].to_broadcast([P, K, TOPK])
                ai = score[:, bass.ds(i, 1), HEADS:2 * HEADS].rearrange("p a h -> p h a").to_broadcast([P, HEADS, TOPK])
                done(i, 5, V.tensor_tensor(same[:], idxf[:].unsqueeze(2).to_broadcast([P, K, TOPK]), again, ALU.is_equal))
                done(i, 6, V.tensor_tensor(grid(e), grid(topc), ai, ALU.add))
                after(i, 5)
                done(i, 7, V.tensor_tensor(same[:], same[:], more, ALU.mult))
                after(i, 6)
                done(i, 8, V.scalar_tensor_tensor(out=lr[:], in0=e[:], scalar=0.2, in1=e[:], op0=ALU.mult, op1=ALU.max))
                after(i, 7)
                done(i, 9, V.tensor_reduce(count[:], same[:], AX.X, ALU.add))
                after(i, 8)
                V.tensor_tensor(grid(rel), grid(lr), grid(lr)[:, :, 0:1].to_broadcast([P, HEADS, TOPK]),
                                ALU.subtract).then_inc(q["relr"], 1)
                after(i, 9)
                waited(dve, q["past"])
                with dve.If(many == 1):
                    recount(i)
                done(i, 10, V.tensor_tensor_scan(upto[:], within[:], count[:], 0.0, ALU.mult, ALU.add))
                done(i, 11, V.tensor_tensor(room[:], left[:], count[:], ALU.add))
                after(i, 10)
                after(i, 11)
                done(i, 12, V.scalar_tensor_tensor(out=room[:], in0=upto[:], scalar=-1.0, in1=room[:], op0=ALU.mult, op1=ALU.add))
                after(i, 12)
                done(i, 13, V.scalar_tensor_tensor(out=take[:], in0=count[:], scalar=1.0, in1=room[:], op0=ALU.add, op1=ALU.min))

            def shares(i, k):
                V = nc.vector
                if k == 0:
                    after(i, 13)
                    dve.wait_ge(q["exr"], i + 1)
                    done(i, 14, V.scalar_tensor_tensor(out=wt[:], in0=take[:], scalar=0.0, in1=ex[:], op0=ALU.max, op1=ALU.mult))

                elif k == 1:
                    after(i, 14)
                    done(i, 15, V.tensor_reduce(den[:], grid(wt), AX.X, ALU.add))
                elif k == 2:
                    after(i, 15)
                    done(i, 16, V.reciprocal(rden[:], den[:]))
                else:
                    after(i, 16)
                    done(i, 17, V.tensor_tensor(grid(alpha), grid(wt), rden[:].unsqueeze(2).to_broadcast([P, HEADS, TOPK]), ALU.mult))

            def combine(i, half):
                part = slice(half * K // 2, (half + 1) * K // 2)
                if half == 0:
                    after(i, 17)
                dve.wait_ge(q[f"gath{half}"], 8 * K * (i + 1))
                nc.vector.tensor_tensor(G[:, part, :], G[:, part, :], alpha[:, part].unsqueeze(2).to_broadcast([P, K // 2, HC]),
                                        ALU.mult).then_inc(q["or_"], 1)
                dve.wait_ge(q["or_"], 2 * i + half + 1)
                nc.vector.tensor_reduce(o[:, half * D // 2:(half + 1) * D // 2].rearrange("p (h c) -> p h c", c=HC),
                                        G[:, part, :].rearrange("p (h k) c -> p h c k", k=TOPK), AX.X, ALU.add).then_inc(q[f"aw{half}"], 1)
                if half == 1:
                    dve.wait_ge(q["aw1"], i + 1)
                    nc.vector.tensor_scalar(neg, o, 0.0, None, ALU.min).then_inc(q["negr"], 1)

            def residual(i, k):
                if k == 0:
                    dve.wait_ge(q["ex2r"], i + 1)
                    dve.wait_ge(q["x_in"], 16 * (i + 1))
                    nc.vector.scalar_tensor_tensor(out=y, in0=o, scalar=0.0, in1=ex2, op0=ALU.max, op1=ALU.add).then_inc(q["bn"], 1)
                elif k == 1:
                    dve.wait_ge(q["bn"], 3 * i + 1)
                    nc.vector.scalar_tensor_tensor(out=y, in0=y, scalar=-1.0, in1=xb[:], op0=ALU.add, op1=ALU.add).then_inc(q["yr"], 1)
                elif k == 2:
                    dve.wait_ge(q["yr"], i + 1)
                    nc.vector.bn_stats(stats[:], y).then_inc(q["bn"], 2)
                else:
                    dve.wait_ge(q["bn"], 3 * i + 3)
                    waited(dve, q["past"])
                    nc.vector.bn_aggr(mv[:], stats[:]).then_inc(q["mvr"], 1)

            def normalize(i, k):
                if k == 0:
                    dve.wait_ge(q["sdr"], i + 1)
                    nc.vector.reciprocal(rstd[:], sdev[:]).then_inc(q["rsr"], 1)
                else:
                    dve.wait_ge(q["rsr"], i + 1)
                    dve.wait_ge(q["tr"], i)
                    dve.wait_ge(q["hi"], i)
                    nc.vector.tensor_scalar(xn[:], y, mv[:, 0:1], rstd[:, 0:1], ALU.subtract, ALU.mult).then_inc(q["xnr"], 1)

            def split_r(i):
                dve.wait_ge(q["hi"], i + 1)
                nc.vector.tensor_tensor(rest[:], xn[:], stage[:, 0, :], ALU.subtract).then_inc(q["r"], 1)

            def split_lo(i):
                dve.wait_ge(q["mid"], i + 1)
                nc.vector.tensor_tensor(stage[:, 2, :], rest[:], stage[:, 1, :], ALU.subtract).then_inc(q["lo"], 1)

            def tile(i, before, old):
                greatest(i, 0)
                if before is not None:
                    shares(before, 0)
                if old is not None:
                    residual(old, 0)
                places(i, 0)
                if before is not None:
                    shares(before, 1)
                if old is not None:
                    residual(old, 1)
                greatest(i, 1)
                if before is not None:
                    shares(before, 2)
                if old is not None:
                    residual(old, 2)
                places(i, 1)
                if before is not None:
                    shares(before, 3)
                if old is not None:
                    residual(old, 3)
                greatest(i, 2)
                if before is not None:
                    combine(before, 0)
                if old is not None:
                    normalize(old, 0)
                places(i, 2)
                if old is not None:
                    normalize(old, 1)
                greatest(i, 3)
                if old is not None:
                    split_r(old)
                places(i, 3)
                if old is not None:
                    split_lo(old)
                row_numbers(i, 0)
                if before is not None:
                    combine(before, 1)
                row_numbers(i, 1)
                weights(i)

            tile(0, None, None)
            tile(1, 0, None)
            with dve.Fori(2, KB) as i:
                tile(i, dve.snap(i - 1), dve.snap(i - 2))
            for i in (LAST - 1, LAST):
                if i == LAST:
                    for k in range(4):
                        shares(i, k)
                    combine(i, 0)
                    combine(i, 1)
                for k in range(4):
                    residual(i, k)
                for k in range(2):
                    normalize(i, k)
                split_r(i)
                split_lo(i)


def phase_gru(nc, d, w, t, last):
    with ExitStack() as ctx:
        m = Mem(nc, ctx, f"g{t}")
        sT, inv, ind, hT, hm, meT, r, u = (m.sb(n, [P, CH]) for n in ("sT", "inv", "ind", "hT", "hm", "meT", "r", "u"))
        z_rest = m.sb("z_rest", [P, SUB * D])
        z = z_rest[:, 0:CH]
        rest = z_rest[0:SN, :].rearrange("p (s f) -> p s f", f=D)
        stage = m.sb("stage", [SN, SUB, 3, D], BF16)
        wm, wi, wh = m.sb("wm", [D, 2, 3 * D]), m.sb("wi", [D, 2, 3 * D]), m.sb("wh", [D, 3 * D])
        hnew = wi[:].rearrange("p k n -> p (k n)")[:, 0:CH]
        wc = m.sb("wc", [D, 3, 3 * D])
        bm = m.sb("bm", [D, 2])
        bc = m.sb("bc", [D, 3])
        bi, bh, brz = m.sb("bi", [D, 3]), m.sb("bh", [D, 3]), m.sb("brz", [D, 2])
        if last:
            xn = wm[0:SN, :, :].rearrange("p k n -> p (k n)")[:, 0:SUB * D].rearrange("p (s f) -> p s f", f=D)
            xT = m.sb("xT", [P, CH])
            stats, mv = m.sb("stats", [SN, SUB, 6]), m.sb("mv", [SN, SUB, 2])
            sdev, rstd = m.sb("sdev", [SN, SUB]), m.sb("rstd", [SN, SUB])
            eps = m.sb("eps", [P, 1])
        sums = Sums(nc, d, m, begun=last, ahead=True, flip=int(last))
        gate_ps = [m.ps(f"gate_ps{j}", [P, 512]) for j in range(4)]
        t_ps = m.ps("t_ps", [SN, SUB, D])
        names = ("w_in", "cst", "b", "wc_ps", "wc_r", "summed", "taken", "i_in", "n_in", "h_in", "e_in", "x_in", "hmr", "gates",
                 "rp", "zp", "rr", "zr", "u1", "u2", "nin", "nr", "v1", "v2", "hr", "td", "hi", "r_", "mid", "lo", "h_out", "p_out",
                 "bn", "mvr", "sdr", "rsr", "xnr", "xn_out", "y_done")
        q = {n: m.sem(n) for n in names}
        h_from = d["hT"] if t else d["xT"]
        block = ctx.enter_context(nc.Block())

        @block.sync
        def _(sp):
            sums.load(sp)
            sp.dma_start(wm[:], w[f"L2_gnn_W_msg_{t}"].rearrange("(k p) n -> p k n", p=D)).then_inc(q["w_in"], 16)
            sp.dma_start(wi[:], w[f"L2_gnn_Wih_{t}"].rearrange("(k p) n -> p k n", p=D)).then_inc(q["w_in"], 16)
            sp.dma_start(wh[:], w[f"L2_gnn_Whh_{t}"]).then_inc(q["w_in"], 16)
            for to, name in ((bm, "b_msg"), (bi, "bih"), (bh, "bhh")):
                sp.dma_start(to[:], w[f"L2_gnn_{name}_{t}"].rearrange("(k p) -> p k", p=D), allow_slow_non_contiguous=True).then_inc(q["w_in"], 16)

            def load(c, wait):
                cols = bass.ds(c * CH, CH)
                if wait:
                    sp.wait_ge(q["taken"], c + 1)
                sp.dma_start(inv[:], d["inv"][:, cols]).then_inc(q["i_in"], 16)
                if wait:
                    sp.wait_ge(q["gates"], c)
                sp.dma_start(meT[:], d["meT"][:, cols]).then_inc(q["e_in"], 16)
                if wait:
                    sp.wait_ge(q["hr"], c)
                sp.dma_start(ind[:], d["ind"][:, cols]).then_inc(q["n_in"], 16)
                sp.dma_start(hT[:], h_from[:, cols]).then_inc(q["h_in"], 16)
                if last:
                    if wait:
                        sp.wait_ge(q["y_done"], c)
                    sp.dma_start(xT[:], d["xT"][:, cols]).then_inc(q["x_in"], 16)

            def store(c):
                if last:
                    sp.wait_ge(q["xnr"], c + 1)
                    sp.dma_start(rows_of(d["xn"], c), xn).then_inc(q["xn_out"], 16)
                else:
                    sp.wait_ge(q["hr"], c + 1)
                    sp.dma_start(d["hT"][:, bass.ds(c * CH, CH)], hnew).then_inc(q["h_out"], 16)
                sp.wait_ge(q["lo"], c + 1)
                sp.dma_start(rows_of(d["ptab"], c), stage[:].rearrange("p s a f -> p s (a f)")).then_inc(q["p_out"], 16)

            load(0, False)
            with sp.Fori(0, NC - 1) as c:
                load(sp.snap(c + 1), True)
                store(c)
            sums.load_ahead(sp, q["summed"], q["p_out"])
            store(NC - 1)
            sp.wait_ge(q["xn_out"] if last else q["h_out"], 16 * NC)
            sums.load_last(sp, q["p_out"])

        @block.gpsimd
        def _(pool):
            if last:
                nc.gpsimd.memset(eps[:], 1e-5).then_inc(q["cst"], 1)
            sums.rest.load(pool)

        @block.scalar
        def _(act):
            act.wait_ge(q["wc_ps"], 1)
            for k in range(3):
                nc.scalar.copy(wc[:, k, :], gate_ps[k][:, 0:3 * D])
            nc.scalar.copy(bc[:], gate_ps[3][:, 0:3]).then_inc(q["wc_r"], 1)
            act.wait_ge(q["b"], 1)
            if last:
                act.wait_ge(q["cst"], 1)
            with act.Fori(0, NC) as c:
                act.wait_ge(q["rp"], c + 1)
                nc.scalar.activation(r[:], r[:], ACT.Sigmoid, bias=brz[:, 0:1]).then_inc(q["rr"], 1)
                act.wait_ge(q["zp"], c + 1)
                nc.scalar.activation(z, z, ACT.Sigmoid, bias=brz[:, 1:2]).then_inc(q["zr"], 1)
                act.wait_ge(q["nin"], c + 1)
                nc.scalar.activation(u[:], u[:], ACT.Tanh, bias=bi[:, 2:3]).then_inc(q["nr"], 1)
                if last:
                    act.wait_ge(q["mvr"], c + 1)
                    nc.scalar.activation(sdev[:], mv[:, :, 1], ACT.Sqrt, bias=eps[0:SN, 0:1]).then_inc(q["sdr"], 1)
                split_act(nc, act, xn if last else t_ps[:], rest, stage, c, q["xnr"] if last else q["td"], q["r_"], q["p_out"],
                          q["hi"], q["mid"])

        @block.vector
        def _(dve):
            dve.wait_ge(q["w_in"], 16 * 6)
            nc.vector.tensor_tensor(brz[:], bi[:, 0:2], bh[:, 0:2], ALU.add).then_inc(q["b"], 1)
            dve.wait_ge(q["wc_r"], 1)
            with dve.Fori(0, NC) as c:
                dve.wait_ge(q["h_in"], 16 * (c + 1))
                dve.wait_ge(q["n_in"], 16 * (c + 1))
                dve.wait_ge(q["gates"], c)
                nc.vector.tensor_tensor(hm[:], hT[:], ind[:], ALU.mult).then_inc(q["hmr"], 1)
                dve.wait_ge(q["summed"], c + 1)
                dve.wait_ge(q["i_in"], 16 * (c + 1))
                nc.vector.tensor_tensor(sT[:], sums.bank(c), inv[:],
                                        ALU.mult).then_inc(q["taken"], 1)
                dve.wait_ge(q["gates"], c + 1)
                nc.vector.scalar_tensor_tensor(out=r[:], in0=ind[:], scalar=bc[:, 0:1], in1=gate_ps[0][:, 0:CH],
                                               op0=ALU.mult, op1=ALU.add).then_inc(q["rp"], 1)
                nc.vector.scalar_tensor_tensor(out=z, in0=ind[:], scalar=bc[:, 1:2], in1=gate_ps[1][:, 0:CH],
                                               op0=ALU.mult, op1=ALU.add).then_inc(q["zp"], 1)
                dve.wait_ge(q["rr"], c + 1)
                nc.vector.scalar_tensor_tensor(out=u[:], in0=gate_ps[3][:, 0:CH], scalar=bh[:, 2:3], in1=r[:],
                                               op0=ALU.add, op1=ALU.mult).then_inc(q["u1"], 1)
                dve.wait_ge(q["u1"], c + 1)
                nc.vector.tensor_tensor(u[:], u[:], gate_ps[2][:, 0:CH], ALU.add).then_inc(q["u2"], 1)
                dve.wait_ge(q["u2"], c + 1)
                nc.vector.scalar_tensor_tensor(out=u[:], in0=ind[:], scalar=bc[:, 2:3], in1=u[:],
                                               op0=ALU.mult, op1=ALU.add).then_inc(q["nin"], 1)
                dve.wait_ge(q["nr"], c + 1)
                nc.vector.tensor_tensor(r[:], hT[:], u[:], ALU.subtract).then_inc(q["v1"], 1)
                dve.wait_ge(q["v1"], c + 1)
                dve.wait_ge(q["zr"], c + 1)
                nc.vector.tensor_tensor(z, r[:], z, ALU.mult).then_inc(q["v2"], 1)
                dve.wait_ge(q["v2"], c + 1)
                dve.wait_ge(q["y_done"] if last else q["td"], c)
                if not last:
                    dve.wait_ge(q["h_out"], 16 * c)
                nc.vector.tensor_tensor(hnew, z, u[:], ALU.add).then_inc(q["hr"], 1)
                if last:
                    dve.wait_ge(q["xn_out"], 16 * c)
                    norm_dve(nc, dve, t_ps, stats, mv, sdev, rstd, xn, c, q["y_done"], q["mvr"], q["sdr"], q["rsr"], q["bn"], q["xnr"])
                split_dve(nc, dve, xn if last else t_ps[:], rest, stage, c, q["hi"], q["mid"], q["r_"], q["lo"])

        @block.tensor
        def _(pe):
            def prepare():
                pe.wait_ge(q["w_in"], 16 * 6)
                for k in range(3):
                    for j in range(2):
                        nc.tensor.matmul(gate_ps[k][:, 0:3 * D], wm[:, j, k * D:(k + 1) * D], wi[:, j, :], start=j == 0, stop=j == 1)
                for g in range(3):
                    for j in range(2):
                        ins = nc.tensor.matmul(gate_ps[3][:, g:g + 1], wi[:, j, g * D:(g + 1) * D], bm[:, j:j + 1], start=j == 0, stop=j == 1)
                ins.then_inc(q["wc_ps"], 1)

            def gates(c):
                pe.wait_ge(q["hmr"], c + 1)
                pe.wait_ge(q["e_in"], 16 * (c + 1))
                pe.wait_ge(q["nin"], c)
                pe.wait_ge(q["taken"], c + 2)
                pe.wait_ge(q["wc_r"], 1)
                for g in range(3):
                    n = slice(g * D, (g + 1) * D)
                    out = gate_ps[g][:, 0:CH]
                    nc.tensor.matmul(out, wc[:, 2, n], meT[:], start=True, stop=False)
                    nc.tensor.matmul(out, wc[:, 0, n], hm[:], start=False, stop=False)
                    nc.tensor.matmul(out, wc[:, 1, n], sT[:], start=False, stop=g == 2)
                    hidden = gate_ps[g if g < 2 else 3][:, 0:CH]
                    ins = nc.tensor.matmul(hidden, wh[:, n], hT[:], start=g == 2, stop=True)
                ins.then_inc(q["gates"], 1)

            def turn(c):
                pe.wait_ge(q["hr"], c + 1)
                pe.wait_ge(q["xnr"] if last else q["r_"], c)
                if last:
                    pe.wait_ge(q["x_in"], 16 * (c + 1))
                for s in range(SUB):
                    n = slice(s * SN, (s + 1) * SN)
                    if last:
                        nc.tensor.matmul(t_ps[:, s, :], xT[:, n], d["ident"][:], start=True, stop=False)
                        ins = nc.tensor.matmul(t_ps[:, s, :], hnew[:, n], d["ident"][:], start=False, stop=True)
                    else:
                        ins = nc.tensor.transpose(t_ps[:, s, :], hnew[:, n], d["ident"][:])
                ins.then_inc(q["y_done"] if last else q["td"], 1)

            sums.run(pe, q["summed"], q["taken"], True,
                    (gates, turn), (3, 17), prepare)


def phase_hop1(nc, d):
    with ExitStack() as ctx:
        m = Mem(nc, ctx, "h1")
        sT = m.sb("sT", [P, CH])
        rest = m.sb("rest", [SN, SUB, D])
        stage = m.sb("stage", [SN, SUB, 3, D], BF16)
        sums = Sums(nc, d, m, begun=True, ahead=True)
        t_ps = m.ps("t_ps", [SN, SUB, D])
        summed, taken, td, hi, r, mid, lo, p_out = (
            m.sem(n) for n in ("summed", "taken", "td", "hi", "r", "mid", "lo", "p_out"))
        block = ctx.enter_context(nc.Block())

        @block.sync
        def _(sp):
            sums.load(sp)

            def store(c):
                sp.wait_ge(lo, c + 1)
                sp.dma_start(rows_of(d["ptab"], c), stage[:].rearrange("p s a f -> p s (a f)")).then_inc(p_out, 16)

            with sp.Fori(0, NC - 1) as c:
                store(c)
            sums.load_ahead(sp, summed, p_out)
            store(NC - 1)
            sums.load_last(sp, p_out)

        @block.gpsimd
        def _(pool):
            sums.rest.load(pool)

        @block.scalar
        def _(act):
            with act.Fori(0, NC) as c:
                split_act(nc, act, t_ps[:], rest, stage, c, td, r, p_out, hi, mid)

        @block.vector
        def _(dve):
            with dve.Fori(0, NC) as c:
                dve.wait_ge(summed, c + 1)
                dve.wait_ge(td, c)
                nc.vector.tensor_copy(sT[:], sums.bank(c)).then_inc(taken, 1)
                split_dve(nc, dve, t_ps[:], rest, stage, c, hi, mid, r, lo)

        @block.tensor
        def _(pe):
            def turn(c):
                pe.wait_ge(taken, c + 2)
                pe.wait_ge(r, c)
                for s in range(SUB):
                    ins = nc.tensor.transpose(t_ps[:, s, :], sT[:, s * SN:(s + 1) * SN], d["ident"][:])
                ins.then_inc(td, 1)

            sums.run(pe, summed, taken, True, (turn,), (4,))


def phase_hop2(nc, d, w, out):
    with ExitStack() as ctx:
        m = Mem(nc, ctx, "h2")
        sT = m.sb("sT", [P, CH])
        wf, bf, ones = m.sb("wf", [D, D]), m.sb("bf", [1, D]), m.sb("ones", [1, SN])
        xb, y, xo = (m.sb(n, [SN, SUB, D]) for n in ("xb", "y", "xo"))
        stats, mv = m.sb("stats", [SN, SUB, 6]), m.sb("mv", [SN, SUB, 2])
        sdev, rstd = m.sb("sdev", [SN, SUB]), m.sb("rstd", [SN, SUB])
        eps = m.sb("eps", [P, 1])
        sums = Sums(nc, d, m, begun=True, flip=1)
        y_ps = m.ps("y_ps", [SN, SUB, D])
        names = ("w_in", "cst", "summed", "taken", "x_in", "y_done", "yr", "bn", "mvr", "sdr", "rsr", "xor_", "o_out")
        q = {n: m.sem(n) for n in names}
        block = ctx.enter_context(nc.Block())

        @block.sync
        def _(sp):
            sums.load(sp)
            sp.dma_start(wf[:], w["L3_gnn_W"]).then_inc(q["w_in"], 16)
            sp.dma_start(bf[:], w["L3_gnn_b"].rearrange("(a f) -> a f", a=1)).then_inc(q["w_in"], 16)

            sp.dma_start(xb[:], rows_of(d["xn"], 0)).then_inc(q["x_in"], 16)
            with sp.Fori(0, NC - 1) as c:
                sp.wait_ge(q["yr"], c + 1)
                sp.dma_start(xb[:], rows_of(d["xn"], c + 1)).then_inc(q["x_in"], 16)
                sp.wait_ge(q["xor_"], c + 1)
                sp.dma_start(rows_of(out, c), xo[:]).then_inc(q["o_out"], 16)
            sp.wait_ge(q["xor_"], NC)
            first = (NC - 1) * CH
            whole = (N - first) // SN
            sp.dma_start(out[first:first + whole * SN, :].rearrange("(s p) f -> p s f", p=SN),
                         xo[:, 0:whole, :]).then_inc(q["o_out"], 16)
            sp.dma_start(out[first + whole * SN:N, :], xo[0:N - first - whole * SN, whole, :]).then_inc(q["o_out"], 16)
            sp.wait_ge(q["o_out"], 16 * (NC + 1))

        @block.gpsimd
        def _(pool):
            nc.gpsimd.memset(eps[:], 1e-5).then_inc(q["cst"], 1)
            nc.gpsimd.memset(ones[:], 1.0).then_inc(q["cst"], 1)
            sums.rest.load(pool)

        @block.scalar
        def _(act):
            act.wait_ge(q["cst"], 2)
            with act.Fori(0, NC) as c:
                act.wait_ge(q["mvr"], c + 1)
                nc.scalar.activation(sdev[:], mv[:, :, 1], ACT.Sqrt, bias=eps[0:SN, 0:1]).then_inc(q["sdr"], 1)

        @block.vector
        def _(dve):
            with dve.Fori(0, NC) as c:
                dve.wait_ge(q["summed"], c + 1)
                dve.wait_ge(q["y_done"], c)
                nc.vector.tensor_copy(sT[:], sums.bank(c)).then_inc(q["taken"], 1)
                dve.wait_ge(q["y_done"], c + 1)
                dve.wait_ge(q["x_in"], 16 * (c + 1))
                nc.vector.tensor_tensor(y[:], y_ps[:], xb[:], ALU.add).then_inc(q["yr"], 1)
                dve.wait_ge(q["o_out"], 16 * c)
                norm_dve(nc, dve, y, stats, mv, sdev, rstd, xo, c, q["yr"], q["mvr"], q["sdr"], q["rsr"], q["bn"], q["xor_"])

        @block.tensor
        def _(pe):
            def products(c):
                pe.wait_ge(q["taken"], c + 2)
                pe.wait_ge(q["yr"], c)
                for s in range(SUB):
                    nc.tensor.matmul(y_ps[:, s, :], sT[:, s * SN:(s + 1) * SN], wf[:], start=True, stop=False)
                    ins = nc.tensor.matmul(y_ps[:, s, :], ones[:], bf[:], start=False, stop=True)
                ins.then_inc(q["y_done"], 1)

            def prepare():
                pe.wait_ge(q["w_in"], 32)
                pe.wait_ge(q["cst"], 2)

            sums.run(pe, q["summed"], q["taken"], True, (products,), (4,), prepare)


def phase_ident(nc, d):
    with ExitStack() as ctx:
        zeroed = Mem(nc, ctx, "id").sem("zeroed")
        block = ctx.enter_context(nc.Block())

        @block.gpsimd
        def _(pool):
            nc.gpsimd.memset(d["ident"][:], 0.0).then_inc(zeroed, 1)
            pool.wait_ge(zeroed, 1)
            nc.gpsimd.affine_select(out=d["ident"][:], in_=d["ident"][:], compare_op=ALU.not_equal, fill=1.0,
                                    base=0, pattern=[[-1, P]], channel_multiplier=1)


def make(nc, x, src, dst, edge_attr, w, out):
    with ExitStack() as ctx:
        m = Mem(nc, ctx, "g")
        d = {}

        def dram(name, shape, dt=F32):
            d[name] = nc.dram_tensor(name, shape, dt).ap()

        dram("flag", [1, 1], I32)
        dram("many", [1, 1], I32)
        dram("AR", [P, KB, NPAD], BF16)
        dram("wins", [1, NWIN], I32)
        dram("ptab", [ROWS, 3 * D], BF16)
        dram("xT", [D, ROWS])
        dram("hT", [D, ROWS])
        dram("xn", [ROWS, D])
        dram("inv", [P, ROWS])
        dram("ind", [P, ROWS])
        dram("se", [NPAD, D])
        dram("meT", [D, ROWS])
        dram("heads", [ROWS, D])
        dram("score", [ROWS, 2 * HEADS])
        dram("aj", [3, HEADS, NPAD], BF16)
        d["AT"] = m.sb("AT", [P, KB, NPAD], BF16)
        d["ident"] = m.sb("ident", [P, P])
        d["agg"] = m.ps("agg", [P, 2, 512])
        phase_ident(nc, d)
        with ExitStack() as edges:
            mem = Mem(nc, edges, "gi")
            d["dsts"] = mem.sb("dsts", [P, NG, GT])
            for name in ("windows", "lows", "codes"):
                d[name] = [mem.sb(f"{name}{j}", [P, NG]) for j in range(GT)]
            phase_index(nc, d, src, dst)
            d["bound"] = mem.sb("bound", [P, NWIN])
            phase_build(nc, d, edge_attr)
            phase_flag(nc, d)
            phase_rest(nc, d)
        d["parts"] = m.sb("parts", [P, KB, 3, D], BF16)
        with ExitStack() as rows:
            mem = Mem(nc, rows, "gr")
            d["again"] = mem.sb("again", [P, KB, TOPK])
            d["more"] = mem.sb("more", [P, KB, TOPK])
            with ExitStack() as search:
                repeats = Repeats(nc, d, Mem(nc, search, "rp"))
                phase_start(nc, d, x, repeats)
                phase_conv1(nc, d, w, repeats)
                phase_conv2(nc, d, w, repeats)
            phase_many(nc, d)
            phase_attention(nc, d)
        phase_gru(nc, d, w, 0, False)
        phase_gru(nc, d, w, 1, True)
        phase_hop1(nc, d)
        phase_hop2(nc, d, w, out)


def kernel(**inputs):
    import numpy as _np
    import concourse.bacc as _bacc
    from concourse import mybir as _mybir
    from concourse.bass_utils import run_bass_kernel_spmd as _run

    nc = _bacc.Bacc("TRN2", target_bir_lowering=False, num_devices=1)
    arrays, aps = {}, {}
    for name, a in inputs.items():
        a = _np.asarray(a)
        if "Wih" in name or "Whh" in name:
            a = a.T
        a = _np.ascontiguousarray(a)
        arrays[f"in_{name}"] = a
        aps[name] = nc.dram_tensor(f"in_{name}", a.shape, _mybir.dt.from_np(a.dtype), kind="ExternalInput").ap()
    out = nc.dram_tensor("out_0", (N, D), _mybir.dt.float32, kind="ExternalOutput").ap()
    x, src, dst, ea = (aps.pop(k) for k in ("x", "src", "dst", "edge_attr_128"))
    make(nc, x, src, dst, ea, aps, out)
    r = _run(nc, [arrays], core_ids=[0])
    return r.results[0]["out_0"]
```
